# Optimizing a Trainium2 kernel written in Bass

```python
import numpy as np
import jax
import jax.numpy as jnp

def _softmax(x, axis=-1):
    return jax.nn.softmax(x, axis=axis)

def _gelu(x):
    return jax.nn.gelu(x, approximate=True)

def _silu(x):
    return jax.nn.silu(x)

def _sigmoid(x):
    return jax.nn.sigmoid(x)

def _layernorm(x, axis=-1, eps=1e-05):
    m = jnp.mean(x, axis=axis, keepdims=True)
    v = jnp.var(x, axis=axis, keepdims=True)
    return (x - m) / jnp.sqrt(v + eps)

def _scatter_add(tgt, idx, src, axis=0):
    return tgt.at[idx].add(src)

def _segment_sum(src, seg, n):
    return jax.ops.segment_sum(src, seg, n)
kernel_name = 'mk_adaln_d1_jaxref_r8_51ca44'

def setup_inputs(seed: int=0):
    np.random.seed(seed)
    _w = jnp.asarray

    def _L0_attn_setup():
        import jax, jax.numpy as jnp
        import numpy as np
        BATCH, SEQ, D_MODEL, N_HEADS, D_HEAD = (2, 256, 256, 16, 128)
        ATTN_SCALE = np.sqrt(D_HEAD).astype(np.float32)
        IGNORE = jnp.float32(-100000.0)
        key = jax.random.key(seed)
        ks = jax.random.split(key, 5)
        init = 1.0 / np.sqrt(D_MODEL)
        return {'x': jax.random.normal(ks[0], (BATCH, SEQ, D_MODEL), jnp.float32), 'W_Q': jax.random.normal(ks[1], (N_HEADS, D_MODEL, D_HEAD), jnp.float32) * init, 'W_K': jax.random.normal(ks[2], (N_HEADS, D_MODEL, D_HEAD), jnp.float32) * init, 'W_V': jax.random.normal(ks[3], (N_HEADS, D_MODEL, D_HEAD), jnp.float32) * init, 'W_O': jax.random.normal(ks[4], (N_HEADS, D_HEAD, D_MODEL), jnp.float32) * init, 'b_Q': jnp.zeros((N_HEADS, D_HEAD), jnp.float32), 'b_K': jnp.zeros((N_HEADS, D_HEAD), jnp.float32), 'b_V': jnp.zeros((N_HEADS, D_HEAD), jnp.float32), 'b_O': jnp.zeros((D_MODEL,), jnp.float32)}
    _L0_attn_in = _L0_attn_setup()

    def _L0_ffn_setup():
        import jax, jax.numpy as jnp
        import numpy as np
        IN_F, OUT_F = (256, 256)
        N_EXPERTS, RANK, TOP_K = (8, 128, 2)
        key = jax.random.key(seed)
        k_x, k_r, k_a, k_b = jax.random.split(key, 4)
        hidden_states = jax.random.normal(k_x, (4, 512, IN_F), dtype=jnp.float32)
        router_w = jax.random.normal(k_r, (IN_F, N_EXPERTS), dtype=jnp.float32) * IN_F ** (-0.5)
        Wa = jax.random.normal(k_a, (N_EXPERTS, IN_F, RANK), dtype=jnp.float32) * IN_F ** (-0.5)
        Wb = jax.random.normal(k_b, (N_EXPERTS, RANK, OUT_F), dtype=jnp.float32) * RANK ** (-0.5)
        return {'hidden_states': hidden_states, 'router_w': router_w, 'Wa': Wa, 'Wb': Wb}
    _L0_ffn_in = _L0_ffn_setup()
    _L0_c = _w((lambda *s: np.random.randn(*s).astype(np.float32) * 0.05)(2, 256))
    _L0_wmod = _w((lambda *s: np.random.randn(*s).astype(np.float32) * 0.05)(256, 6 * 256) * 256 ** (-0.5))
    _d = {'L0_attn_x': _L0_attn_in['x'], 'L0_attn_W_Q': _L0_attn_in['W_Q'], 'L0_attn_W_K': _L0_attn_in['W_K'], 'L0_attn_W_V': _L0_attn_in['W_V'], 'L0_attn_W_O': _L0_attn_in['W_O'], 'L0_attn_b_Q': _L0_attn_in['b_Q'], 'L0_attn_b_K': _L0_attn_in['b_K'], 'L0_attn_b_V': _L0_attn_in['b_V'], 'L0_attn_b_O': _L0_attn_in['b_O'], 'L0_ffn_router_w': _L0_ffn_in['router_w'], 'L0_ffn_Wa': _L0_ffn_in['Wa'], 'L0_ffn_Wb': _L0_ffn_in['Wb'], 'L0_c': _L0_c, 'L0_wmod': _L0_wmod}
    _x0 = _d['L0_attn_x']
    _d['L0_attn_x'] = jax.random.normal(jax.random.fold_in(jax.random.key(seed), 1), (2, 1024, 256), dtype=_x0.dtype)
    del _x0
    return _d

def reference(L0_attn_x, L0_attn_W_Q, L0_attn_W_K, L0_attn_W_V, L0_attn_W_O, L0_attn_b_Q, L0_attn_b_K, L0_attn_b_V, L0_attn_b_O, L0_ffn_router_w, L0_ffn_Wa, L0_ffn_Wb, L0_c, L0_wmod):

    def _L0_attn_ref(x, W_Q, W_K, W_V, W_O, b_Q, b_K, b_V, b_O):
        import jax, jax.numpy as jnp
        import numpy as np
        BATCH, SEQ, D_MODEL, N_HEADS, D_HEAD = (2, 256, 256, 16, 128)
        ATTN_SCALE = np.sqrt(D_HEAD).astype(np.float32)
        IGNORE = jnp.float32(-100000.0)
        q = jnp.einsum('bpd,hde->bphe', x, W_Q) + b_Q
        k = jnp.einsum('bpd,hde->bphe', x, W_K) + b_K
        v = jnp.einsum('bpd,hde->bphe', x, W_V) + b_V
        scores = jnp.einsum('bqhe,bkhe->bhqk', q, k) / ATTN_SCALE
        S = x.shape[1]
        causal = jnp.tril(jnp.ones((S, S), bool))
        scores = jnp.where(causal, scores, IGNORE)
        attn = jax.nn.softmax(scores, axis=-1)
        z = jnp.einsum('bkhe,bhqk->bqhe', v, attn)
        out = jnp.einsum('bqhe,hed->bqd', z, W_O) + b_O
        return out

    def _L0_ffn_ref(hidden_states, router_w, Wa, Wb):
        import jax, jax.numpy as jnp
        import numpy as np
        IN_F, OUT_F = (256, 256)
        N_EXPERTS, RANK, TOP_K = (8, 128, 2)
        B, S, D = hidden_states.shape
        x = hidden_states.reshape(-1, D)
        norm = jnp.maximum(jnp.linalg.norm(x, axis=-1, keepdims=True), 1e-12)
        router_logits = x / norm @ router_w
        routing_weights = jax.nn.softmax(router_logits.astype(jnp.float32), axis=-1)
        rw, selected_experts = jax.lax.top_k(routing_weights, TOP_K)
        rw = rw / jnp.sum(rw, axis=-1, keepdims=True)
        rw = rw.astype(hidden_states.dtype)
        combine = jnp.sum(jax.nn.one_hot(selected_experts, N_EXPERTS, dtype=rw.dtype) * rw[..., None], axis=1)
        out = jnp.zeros((x.shape[0], OUT_F), dtype=hidden_states.dtype)
        for e in range(N_EXPERTS):
            out = out + combine[:, e, None] * (x @ Wa[e] @ Wb[e])
        return out.reshape(B, S, OUT_F)
    x = L0_attn_x
    mod = (_silu(L0_c) @ L0_wmod).reshape(L0_c.shape[0], 6, 1, -1)
    sa, ca, ga, sb, cb, gb = (mod[:, 0], mod[:, 1], mod[:, 2], mod[:, 3], mod[:, 4], mod[:, 5])
    ga = (2 * (ga >= 0) - 1) * jnp.maximum(jnp.abs(ga), 0.25)
    gb = (2 * (gb >= 0) - 1) * jnp.maximum(jnp.abs(gb), 0.25)
    h = _layernorm(x, axis=-1) * (1 + ca) + sa
    x = x + ga * _L0_attn_ref(h, L0_attn_W_Q, L0_attn_W_K, L0_attn_W_V, L0_attn_W_O, L0_attn_b_Q, L0_attn_b_K, L0_attn_b_V, L0_attn_b_O)
    h = _layernorm(x, axis=-1) * (1 + cb) + sb
    x = x + gb * _L0_ffn_ref(h, L0_ffn_router_w, L0_ffn_Wa, L0_ffn_Wb)
    return x

_drawn_inputs = setup_inputs


def setup_inputs(seed=0):
    import zlib

    import numpy as np

    out = dict(_drawn_inputs(seed))
    spreads = {'L0_attn_b_Q': (0.0, 0.33),
     'L0_attn_b_K': (0.0, 0.8),
     'L0_attn_b_V': (0.0, 0.1),
     'L0_attn_b_O': (0.0, 0.1)}
    factors = {}
    for name, (base, spread) in spreads.items():
        noise = np.random.default_rng([zlib.crc32(name.encode()), seed]).standard_normal(out[name].shape)
        drawn = base * np.exp(spread * noise) if base else spread * noise
        out[name] = jnp.asarray(drawn.astype(out[name].dtype))
    for name, factor in factors.items():
        out[name] = (out[name] * factor).astype(out[name].dtype)
    return out
```

```python
from contextlib import ExitStack

import concourse.bass as bass
from concourse import mybir

P = 128
BATCH, SEQ, DM, NH, DH = 2, 1024, 256, 16, 128
TOK = BATCH * SEQ
KC = DM // P
TILES = TOK // P
QT = SEQ // P
HALF = SEQ // 2
HT = HALF // P
PAIRS = NH // 2
UNITS = 2 * BATCH
NE, RANK = 8, 128
CHUNK = 512
CHUNKS = TOK // CHUNK
CT = CHUNK // P
EPS = 1e-5
SCALE = float(DH) ** -0.5
MASKED = -1e30
NMOD = 6 * DM

F32 = mybir.dt.float32
F32R = mybir.dt.float32r
ALU = mybir.AluOpType
ACT = mybir.ActivationFunctionType
AX = mybir.AxisListType

GROUPS = [[(0, min(q + 1, HT))] + ([(HT, q + 1 - HT)] if q >= HT else []) for q in range(QT)]
FIRST_GROUP = [sum(len(g) for g in GROUPS[:q]) for q in range(QT + 1)]
NG = FIRST_GROUP[QT]

FILL_EVEN = {1: ("wo", 0), 2: ("wo", 1), 3: ("proj", 0), 4: ("proj", 1), 5: ("wo", 2), 6: ("proj", 2), 7: ("proj", 3)}
FILL_EVEN_2 = {7: ("wo", 3)}
FILL_ODD = {0: ("v", 0), 1: ("v", 1), 2: ("v", 2), 3: ("proj", 0), 4: ("proj", 1), 5: ("v", 3), 6: ("proj", 2), 7: ("proj", 3)}


def fillers(u, q):
    if u % 2:
        return [FILL_ODD[q]]
    return [f[q] for f in (FILL_EVEN, FILL_EVEN_2) if q in f]


def wait(eng, sem, value):
    if isinstance(value, int) and value <= 0:
        return
    eng.wait_ge(sem, value)


def wait_apart(eng, spare, *waits):
    holds, registers = spare
    if not all(isinstance(v, int) for _, v in waits):
        for register, (_, v) in zip(registers, waits):
            eng.reg_mov(register, v)
        waits = [(sem, register) for register, (sem, _) in zip(registers, waits)]
        eng.wait_ge(holds, 1)
    for sem, v in waits:
        wait(eng, sem, v)


def adaln_block(nc, x, wqkv, wo, bias, b_o, router_w, wa, wb, cond, wmod, out):
    ctx = ExitStack()
    with ctx:
        def sb(name, shape, dt=F32, scope=ctx):
            return scope.enter_context(nc.sbuf_tensor(name, shape, dt))

        def pb(name, shape):
            return ctx.enter_context(nc.psum_tensor(name, shape, F32))

        def sem(name):
            return ctx.enter_context(nc.semaphore(name))

        ident = sb("ident", [P, P])
        mod = sb("mod", [P, 2, KC, BATCH])
        biases = sb("biases", [P, 3, NH])
        h_hi = sb("h_hi", [P, KC, TOK], F32R)
        h_lo = sb("h_lo", [P, KC, TOK], F32R)
        acc = sb("acc", [P, TILES, DM])

        s_tiles = [pb(f"s_tile{i}", [P, SEQ]) for i in range(2)]
        t_bank = [pb(f"t_bank{i}", [P, HALF]) for i in range(2)]
        z_bank = pb("z_bank", [P, HALF])
        fill_bank = pb("fill_bank", [P, HALF])

        prepare(nc, sb, sem, locals())
        attend(nc, sb, sem, locals())
        experts(nc, sb, sem, locals())


def rsqrt_newton(dve, link, y, v, t):
    link(dve.tensor_tensor(t, y, y, ALU.mult))
    link(dve.tensor_tensor(t, t, v, ALU.mult))
    link(dve.tensor_scalar(t, t, -0.5, 1.5, ALU.mult, ALU.add))
    link(dve.tensor_tensor(y, y, t, ALU.mult))


def prepare(nc, sb, sem, g):
    ident, mod, biases, h_hi, h_lo, acc = (g[n] for n in ("ident", "mod", "biases", "h_hi", "h_lo", "acc"))
    banks = [g["s_tiles"][i][:, HALF * k:HALF * (k + 1)] for i in range(2) for k in range(2)]
    mod_bank = g["z_bank"]
    with ExitStack() as scope:
        condT = sb("condT", [P, KC, BATCH], scope=scope)
        cexp = sb("cexp", [P, KC, BATCH], scope=scope)
        csilu = sb("csilu", [P, KC, BATCH], scope=scope)
        wm = sb("wm", [P, KC, 2 * DM], scope=scope)
        stats = sb("stats", [P, TILES, 6], scope=scope)
        mv = sb("mv", [P, TILES, 2], scope=scope)
        var = sb("var", [P, TILES], scope=scope)
        rstd = sb("rstd", [P, TILES], scope=scope)
        scratch = sb("scratch", [P, TILES], scope=scope)
        power = sb("power", [P, TILES], scope=scope)
        xn = sb("xn", [P, TILES, DM], scope=scope)
        full = sb("full", [P, 2, CHUNK], scope=scope)
        x_in, cond_in, wm_in, bias_in = (sem(n) for n in ("x_in", "cond_in", "wm_in", "bias_in"))
        x_in1 = sem("x_in1")
        id_zero, id_ready, pow_ready = sem("id_zero"), sem("id_ready"), sem("pow_ready")
        c_exp, mod_psum, mod_ready = sem("c_exp"), sem("mod_psum"), sem("mod_ready")
        var_ready, guess_ready, xn_ready = sem("var_ready"), sem("guess_ready"), sem("xn_ready")
        xT_ready, hhi_ready, full_ready, hlo_ready = (sem(n) for n in ("xT_ready", "hhi_ready", "full_ready", "hlo_ready"))
        chain = sem("prep_chain")
        NB = BATCH * 2 * KC

        def where(n):
            b, r = divmod(n, 2 * KC)
            half, c = divmod(r, KC)
            return b, half, c

        with nc.Block() as block:
            @block.sync
            def _(sp):
                sp.dma_start(condT[:, :, :], g["cond"]).then_inc(cond_in, 16)
                xv = g["x"].rearrange("b (t p) d -> p (b t) d", p=P)
                sp.dma_start(acc[:, 0:QT, :], xv[:, 0:QT, :]).then_inc(x_in, 16)
                sp.dma_start(wm[:, :, :], g["wmod"].rearrange("(c p) n -> p c n", p=P)[:, :, 0:2 * DM]).then_inc(wm_in, 16)
                sp.dma_start(acc[:, QT:, :], xv[:, QT:, :]).then_inc(x_in1, 16)
                sp.dma_start(biases[:, :, :], g["bias"]).then_inc(bias_in, 16)
                sp.wait_ge(bias_in, 16)

            @block.gpsimd
            def _(pool):
                pool.memset(power[:, :], -0.5).then_inc(pow_ready, 1)
                pool.memset(ident[:, :], 0.0).then_inc(id_zero, 1)
                pool.wait_ge(id_zero, 1)
                pool.affine_select(out=ident[:, :], in_=ident[:, :], compare_op=ALU.not_equal, fill=1.0,
                                   base=0, pattern=[[-1, P]], channel_multiplier=1).then_inc(id_ready, 1)
                pool.wait_ge(pow_ready, 1)
                for b in range(BATCH):
                    t = slice(b * QT, (b + 1) * QT)
                    pool.wait_ge(var_ready, b + 1)
                    pool.tensor_tensor(rstd[:, t], var[:, t], power[:, t], ALU.pow).then_inc(guess_ready, 1)
                pool.wait_ge(xn_ready, TILES)
                pool.memset(acc[:, :, :], 0.0)

            @block.scalar
            def _(act):
                act.wait_ge(cond_in, 16)
                nc.scalar.activation(cexp[:, :, :], condT[:, :, :], ACT.Exp, scale=-1.0).then_inc(c_exp, 1)
                act.wait_ge(mod_ready, 1)
                for n in range(NB):
                    b, half, c = where(n)
                    cols = slice(b * SEQ + half * HALF, b * SEQ + (half + 1) * HALF)
                    act.wait_ge(xT_ready, n + 1)
                    nc.scalar.activation(h_hi[:, c, cols], banks[n % 4], ACT.Identity, scale=mod[:, 0, c, b:b + 1],
                                         bias=mod[:, 1, c, b:b + 1]).then_inc(hhi_ready, 1)

            @block.tensor
            def _(pe):
                pe.wait_ge(chain, 3)
                pe.wait_ge(wm_in, 16)
                for k in range(2):
                    for m in range(KC):
                        for c in range(KC):
                            col = k * DM + m * P
                            last = nc.tensor.matmul(mod_bank[:, (k * KC + m) * BATCH:(k * KC + m + 1) * BATCH],
                                                    wm[:, c, col:col + P], csilu[:, c, :], start=(c == 0), stop=(c == KC - 1))
                last.then_inc(mod_psum, 1)
                pe.wait_ge(id_ready, 1)
                for n in range(NB):
                    b, half, c = where(n)
                    pe.wait_ge(xn_ready, b * QT + (half + 1) * HT)
                    if n >= 4:
                        pe.wait_ge(full_ready, n - 3)
                    for i in range(HT):
                        t = b * QT + half * HT + i
                        last = nc.tensor.transpose(banks[n % 4][:, i * P:(i + 1) * P], xn[:, t, c * P:(c + 1) * P], ident[:, :])
                    last.then_inc(xT_ready, 1)

            @block.vector
            def _(dve):
                count = [0]

                def link(ins):
                    count[0] += 1
                    ins.then_inc(chain, 1)
                    dve.wait_ge(chain, count[0])

                v = nc.vector
                dve.wait_ge(c_exp, 1)
                link(v.tensor_scalar_add(cexp[:, :, :], cexp[:, :, :], 1.0))
                link(v.reciprocal(cexp[:, :, :], cexp[:, :, :]))
                link(v.tensor_tensor(csilu[:, :, :], condT[:, :, :], cexp[:, :, :], ALU.mult))
                for b in range(BATCH):
                    dve.wait_ge(x_in1 if b else x_in, 16)
                    for t in range(b * QT, (b + 1) * QT):
                        last = v.bn_stats(stats[:, t, :], acc[:, t, :])
                    link(last)
                    for t in range(b * QT, (b + 1) * QT):
                        last = v.bn_aggr(mv[:, t, :], stats[:, t, :])
                    link(last)
                    ts = slice(b * QT, (b + 1) * QT)
                    v.tensor_scalar_add(var[:, ts], mv[:, ts, 1], EPS).then_inc(var_ready, 1)
                    if b == 0:
                        dve.wait_ge(mod_psum, 1)
                        mp = mod_bank[:, 0:2 * KC * BATCH].rearrange("p (k c b) -> p k c b", k=2, c=KC)
                        link(v.tensor_scalar_add(mod[:, 0, :, :], mp[:, 1, :, :], 1.0))
                        v.tensor_copy(mod[:, 1, :, :], mp[:, 0, :, :]).then_inc(mod_ready, 1)
                    dve.wait_ge(guess_ready, b + 1)
                    rsqrt_newton(v, link, rstd[:, ts], var[:, ts], scratch[:, ts])
                    for t in range(b * QT, (b + 1) * QT):
                        v.tensor_scalar(xn[:, t, :], acc[:, t, :], mv[:, t, 0:1], rstd[:, t:t + 1],
                                        ALU.subtract, ALU.mult).then_inc(xn_ready, 1)
                    if b == 0:
                        dve.wait_ge(mod_ready, 1)
                    for n in range(b * 2 * KC, (b + 1) * 2 * KC):
                        _, half, c = where(n)
                        cols = slice(b * SEQ + half * HALF, b * SEQ + (half + 1) * HALF)
                        dve.wait_ge(hhi_ready, n + 1)
                        if n >= 2:
                            dve.wait_ge(hlo_ready, n - 1)
                        v.tensor_scalar(full[:, n % 2, :], banks[n % 4], mod[:, 0, c, b:b + 1], mod[:, 1, c, b:b + 1],
                                        ALU.mult, ALU.add).then_inc(full_ready, 1)
                        dve.wait_ge(full_ready, n + 1)
                        v.tensor_tensor(h_lo[:, c, cols], full[:, n % 2, :], h_hi[:, c, cols].bitcast(F32),
                                        ALU.subtract).then_inc(hlo_ready, 1)


def attend(nc, sb, sem, g):
    ident, biases, h_hi, h_lo, acc = (g[n] for n in ("ident", "biases", "h_hi", "h_lo", "acc"))
    s_tiles, t_bank, z_bank, fill_bank = (g[n] for n in ("s_tiles", "t_bank", "z_bank", "fill_bank"))
    AHEAD, SLOTS = 2, 4
    with ExitStack() as scope:
        def sbl(name, shape, dt=F32):
            return sb(name, shape, dt, scope)

        def split(name, shape):
            return [sbl(f"{name}_hi", shape, F32R), sbl(f"{name}_lo", shape, F32R)]

        w_qkv = split("w_qkv", [P, 3, KC, 2 * DH])
        w_o = split("w_o", [P, 2, DM])
        raw_qkv = sbl("raw_qkv", [P, 3, KC * 2 * DH])
        raw_o = sbl("raw_o", [P, 2 * DM])
        q_half = [split(f"q{i}", [P, HALF]) for i in range(2)]
        k_first = [split(f"k0_{i}", [P, HALF]) for i in range(2)]
        k_second = split("k1", [P, HALF])
        vals = [split(f"v{b}", [P, QT, 2 * DH]) for b in range(BATCH)]
        pT = [split("pT0", [P, HT, HALF]), split("pT1", [P, QT, HALF])]
        z = [split(f"z{i}", [P, SEQ]) for i in range(2)]
        probs = [sbl(f"probs{i}", [P, (HT + 1 + i) * P]) for i in range(SLOTS)]
        mask = sbl("mask", [P, P])
        m_diag, m_rest, neg_max, row_sum, inv_sum = (sbl(n, [P, SLOTS]) for n in ("m_diag", "m_rest", "neg_max", "row_sum", "inv_sum"))

        names = ("raw_qkv_in", "raw_o_in", "mask_zero", "mask_ready", "w_hi", "w_split",
                 "scores", "partial_max", "max_ready", "exp_done", "inv_ready", "normed",
                 "transposed", "pT_hi", "pT_lo", "z_psum", "z_hi", "z_lo",
                 "proj_psum", "proj_hi", "proj_lo", "v_psum", "v_hi", "v_lo", "wo_psum", "wo_added")
        S = {n: sem(n) for n in names}

        def tiles_to(i, u, q):
            return UNITS * QT * i + QT * u + q + 1

        def groups_to(i, u, q):
            return UNITS * NG * i + NG * u + FIRST_GROUP[q + 1]

        def z_to(i, u, c):
            return 2 * UNITS * i + 2 * u + c + 1

        def proj_to(i, u, k):
            return 4 * UNITS * i + 4 * u + k + 1

        def v_to(i, b, k):
            return 4 * BATCH * i + 4 * b + k + 1

        def wo_to(i, b, k):
            return 4 * BATCH * i + 4 * b + k + 1

        def wsplit_to(i, k):
            return 3 + 4 * i + k + 1

        def after(i, u, q, n):
            t = QT * u + q + n
            return i + t // (UNITS * QT), t // QT % UNITS, t % QT

        def next_unit(i, u):
            return (i, u + 1) if u + 1 < UNITS else (i + 1, 0)

        def fill_index(i, u, what, k):
            if what == "proj":
                n = next_unit(i, u)
                return n, proj_to(*n, k)
            if what == "v":
                n = (i, 1) if u == 1 else (i + 1, 0)
                return n, v_to(*n, k)
            n = (i, 0) if u == 2 else (i - 1, 1)
            return n, wo_to(*n, k)

        FREED = {"proj": S["proj_lo"], "v": S["v_lo"], "wo": S["wo_added"]}

        def bank_free(eng, i, u, q, pos, first):
            done = [w for p in range(q) for w in fillers(u, p)] + fillers(u, q)[:pos]
            bi, bu = i, u
            if first and u == 0:
                done = [w for w in done if w[0] != "wo"]
                if not done:
                    wait(eng, FREED["v"], v_to(0, 0, 3))
                    return
            if not done:
                bi, bu = (i, u - 1) if u else (i - 1, UNITS - 1)
                done = fillers(bu, QT - 1)
                if first and bu == 0:
                    done = [w for w in done if w[0] != "wo"]
            what, k = done[-1]
            wait(eng, FREED[what], fill_index(bi, bu, what, k)[1])

        def schedule(i, first, last):
            for u in range(UNITS):
                for q in range(QT):
                    fill = []
                    for pos, (what, k) in enumerate(fillers(u, q)):
                        if what == "wo" and first and u == 0:
                            continue
                        if what in ("proj", "v") and last and u == UNITS - 1:
                            continue
                        fill.append((pos, what, k))
                    ahead = not (last and u == UNITS - 1 and q >= QT - AHEAD)
                    yield u, q, fill, ahead, not (first and u == 0)

        def bias_of(kind, i, head):
            return biases[:, kind, bass.ds(2 * i + head, 1)]

        def proj_target(u, k):
            return [(0, 0, q_half[0]), (1, 0, k_first[u % 2]), (1, 1, k_second), (0, 1, q_half[1])][k]

        with nc.Block() as block:
            @block.sync
            def _(sp):
                def load(i, what, when):
                    if when is not None:
                        sp.wait_ge(S["w_split"], when)
                    if what == "qkv":
                        sp.dma_start(raw_qkv[:, :, :], g["wqkv"][bass.ds(i, 1), :, :, :].rearrange("o p k n -> p (o k) n")).then_inc(S["raw_qkv_in"], 16)
                    else:
                        sp.dma_start(raw_o[:, :], g["wo"][bass.ds(i, 1), :, :].rearrange("o p n -> p (o n)")).then_inc(S["raw_o_in"], 16)

                load(0, "qkv", None)
                load(0, "o", None)
                load(1, "qkv", 3)
                with sp.Fori(1, PAIRS - 1) as i:
                    load(i, "o", wsplit_to(i - 1, 0))
                    load(i + 1, "qkv", wsplit_to(i - 1, 3))
                load(PAIRS - 1, "o", wsplit_to(PAIRS - 2, 0))

            @block.gpsimd
            def _(pool):
                pool_spare = (S["mask_ready"], [pool.alloc_register(f"pool_until_{n}") for n in range(2)])
                def normalise(i, u, q):
                    s = q % SLOTS
                    w = (q + 1) * P
                    wait(pool, S["inv_ready"], tiles_to(i, u, q))
                    pool.tensor_tensor(probs[s][:, 0:w], probs[s][:, 0:w], inv_sum[:, s:s + 1].broadcast_to([P, w]),
                                       ALU.mult).then_inc(S["normed"], 1)

                def split_weights(raw, pair, n):
                    hi, lo = pair
                    pool.tensor_copy(hi, raw).then_inc(S["w_hi"], 1)
                    wait(pool, S["w_hi"], n)
                    pool.tensor_tensor(lo, raw, hi.bitcast(F32), ALU.subtract).then_inc(S["w_split"], 1)

                def w_of(kind):
                    return [w[:, kind, :, :].rearrange("p c n -> p (c n)") for w in w_qkv]

                def w_o_all():
                    return [w[:, :, :].rearrange("p h n -> p (h n)") for w in w_o]

                def pair(i, first, last):
                    for u, q, _, ahead, _ in schedule(i, first, last):
                        if (u, q) == (1, 0):
                            wait_apart(pool, pool_spare, (S["raw_o_in"], 16 * (i + 1)), (S["wo_psum"], wo_to(i - 1, 1, 3)))
                            split_weights(raw_o[:, :], w_o_all(), wsplit_to(i, 0))
                        if (u, q) == (2, 0) and not last:
                            wait_apart(pool, pool_spare, (S["raw_qkv_in"], 16 * (i + 2)), (S["v_psum"], v_to(i, 1, 3)))
                            split_weights(raw_qkv[:, 2, :], w_of(2), wsplit_to(i, 1))
                        if (u, q) == (3, 0) and not last:
                            for kind in range(2):
                                wait_apart(pool, pool_spare, (S["proj_psum"], proj_to(i, 3, 3)))
                                split_weights(raw_qkv[:, kind, :], w_of(kind), wsplit_to(i, 2 + kind))
                        if ahead:
                            normalise(*after(i, u, q, AHEAD))

                pool.memset(mask[:, :], 0.0).then_inc(S["mask_zero"], 1)
                pool.wait_ge(S["mask_zero"], 1)
                pool.affine_select(out=mask[:, :], in_=mask[:, :], compare_op=ALU.is_ge, fill=MASKED,
                                   base=0, pattern=[[-1, P]], channel_multiplier=1).then_inc(S["mask_ready"], 1)
                pool.wait_ge(S["raw_qkv_in"], 16)
                for kind in range(3):
                    split_weights(raw_qkv[:, kind, :], w_of(kind), kind + 1)
                for q in range(AHEAD):
                    normalise(0, 0, q)
                pair(0, True, False)
                with pool.Fori(1, PAIRS - 1) as i:
                    pair(i, False, False)
                pair(PAIRS - 1, False, True)

            @block.tensor
            def _(pe):
                mm = nc.tensor.matmul

                def product(dst, a, b, start, stop):
                    mm(dst, a[0], b[0], start=start, stop=False)
                    mm(dst, a[0], b[1], start=False, stop=False)
                    return mm(dst, a[1], b[0], start=False, stop=stop)

                def cut(pair, *idx):
                    return [x[idx] for x in pair]

                def score(i, u, q):
                    wait(pe, S["exp_done"], tiles_to(i, u, q) - 2)
                    if q == 0:
                        wait(pe, S["proj_lo"], proj_to(i, u, 1))
                    if q == HT:
                        wait(pe, S["proj_lo"], proj_to(i, u, 3))
                    dst = s_tiles[q % 2]
                    c = slice(q % HT * P, (q % HT + 1) * P)
                    rows = cut(q_half[q // HT], slice(None), c)
                    w = min((q + 1) * P, HALF)
                    last = product(dst[:, 0:w], rows, cut(k_first[u % 2], slice(None), slice(0, w)), True, True)
                    if q >= HT:
                        w = (q + 1 - HT) * P
                        last = product(dst[:, HALF:HALF + w], rows, cut(k_second, slice(None), slice(0, w)), True, True)
                    last.then_inc(S["scores"], 1)

                def project(i, u, k):
                    kind, half, _ = proj_target(u, k)
                    b, head = divmod(u, 2)
                    wait(pe, S["w_split"], wsplit_to(i - 1, 3))
                    cols = slice(b * SEQ + half * HALF, b * SEQ + (half + 1) * HALF)
                    for c in range(KC):
                        last = product(fill_bank[:, :], cut(w_qkv, slice(None), kind, c, slice(head * DH, (head + 1) * DH)),
                                       [h_hi[:, c, cols], h_lo[:, c, cols]], c == 0, c == KC - 1)
                    last.then_inc(S["proj_psum"], 1)

                def values(i, b, k):
                    wait(pe, S["w_split"], 3 if isinstance(i, int) and i == 0 else wsplit_to(i - 1, 1))
                    for n in range(2):
                        t = b * QT + 2 * k + n
                        for c in range(KC):
                            last = product(fill_bank[:, n * DM:(n + 1) * DM],
                                           [h_hi[:, c, t * P:(t + 1) * P], h_lo[:, c, t * P:(t + 1) * P]],
                                           cut(w_qkv, slice(None), 2, c, slice(None)), c == 0, c == KC - 1)
                    last.then_inc(S["v_psum"], 1)

                def out_project(i, b, k):
                    wait(pe, S["w_split"], wsplit_to(i, 0))
                    wait(pe, S["z_lo"], z_to(i, 2 * b + 1, k // 2))
                    for n in range(2):
                        t = slice((2 * k + n) * P, (2 * k + n + 1) * P)
                        for h in range(2):
                            last = product(fill_bank[:, n * DM:(n + 1) * DM], cut(z[h], slice(None), t),
                                           cut(w_o, slice(None), h, slice(None)), h == 0, h == 1)
                    last.then_inc(S["wo_psum"], 1)

                def transpose(i, u, q):
                    wait(pe, S["normed"], tiles_to(i, u, q))
                    for n, (k0, count) in enumerate(GROUPS[q]):
                        m = FIRST_GROUP[q] + n
                        bank = t_bank[m % 2]
                        wait(pe, S["pT_lo"], UNITS * NG * i + NG * u + m - 1)
                        for j in range(count):
                            last = nc.tensor.transpose(bank[:, j * P:(j + 1) * P], probs[q % SLOTS][:, (k0 + j) * P:(k0 + j + 1) * P], ident[:, :])
                        last.then_inc(S["transposed"], 1)

                def attend_values(i, u, c):
                    b, head = divmod(u, 2)
                    wait(pe, S["pT_lo"], groups_to(i, u, HT * c + HT - 1))
                    wait(pe, S["z_lo"], z_to(i, u, c) - 1)
                    if c == 0:
                        wait(pe, S["v_lo"], v_to(i, b, 3))
                    blocks = HT * (c + 1)
                    for k in range(blocks):
                        q0 = max(0, k - HT * c) * P
                        last = product(z_bank[:, q0:HALF], cut(vals[b], slice(None), k, slice(head * DH, (head + 1) * DH)),
                                       cut(pT[c], slice(None), k, slice(q0, HALF)), k == 0, k == blocks - 1)
                    last.then_inc(S["z_psum"], 1)

                def fill(i, u, q, pos, what, k, first):
                    bank_free(pe, i, u, q, pos, first)
                    n, _ = fill_index(i, u, what, k)
                    {"proj": project, "v": values, "wo": out_project}[what](*n, k)

                def pair(i, first, last):
                    for u, q, fill_list, ahead, has_before in schedule(i, first, last):
                        if ahead:
                            score(*after(i, u, q, AHEAD))
                        for f in fill_list:
                            fill(i, u, q, *f, first)
                        if q == HT:
                            attend_values(i, u, 0)
                        transpose(i, u, q)
                        if q == 0 and has_before:
                            attend_values(*(after(i, u, q, -1)[:2]), 1)

                for k in range(4):
                    if k:
                        pe.wait_ge(S["proj_lo"], k)
                    kind, half, _ = proj_target(0, k)
                    pe.wait_ge(S["w_split"], 2)
                    for c in range(KC):
                        cols = slice(half * HALF, (half + 1) * HALF)
                        last = product(fill_bank[:, :], cut(w_qkv, slice(None), kind, c, slice(0, DH)),
                                       [h_hi[:, c, cols], h_lo[:, c, cols]], c == 0, c == KC - 1)
                    last.then_inc(S["proj_psum"], 1)
                for q in range(AHEAD):
                    score(0, 0, q)
                for k in range(4):
                    if k:
                        pe.wait_ge(S["v_lo"], k)
                    else:
                        pe.wait_ge(S["proj_lo"], 4)
                    values(0, 0, k)
                pair(0, True, False)
                with pe.Fori(1, PAIRS - 1) as i:
                    pair(i, False, False)
                pair(PAIRS - 1, False, True)
                attend_values(PAIRS - 1, UNITS - 1, 1)
                for k in range(4):
                    if k:
                        pe.wait_ge(S["wo_added"], wo_to(PAIRS - 1, 1, k - 1))
                    else:
                        pe.wait_ge(S["wo_added"], wo_to(PAIRS - 1, 0, 3))
                    out_project(PAIRS - 1, 1, k)

            @block.scalar
            def _(act):
                act_spare = (S["mask_ready"], [act.alloc_register(f"act_until_{n}") for n in range(2)])
                def exponential(i, u, q):
                    s = q % SLOTS
                    w = (q + 1) * P
                    wait(act, S["max_ready"], tiles_to(i, u, q))
                    bi, bu, bq = after(i, u, q, -SLOTS)
                    wait(act, S["transposed"], groups_to(bi, bu, bq))
                    nc.scalar.activation(probs[s][:, 0:w], s_tiles[q % 2][:, 0:w], ACT.Exp, bias=neg_max[:, s:s + 1],
                                         scale=SCALE, accum_out=row_sum[:, s:s + 1]).then_inc(S["exp_done"], 1)

                def hi_projection(i, u, k):
                    kind, _, dst = proj_target(u, k)
                    wait_apart(act, act_spare, (S["proj_psum"], proj_to(i, u, k)),
                               (S["scores"], [tiles_to(i, u - 1, HT - 1), tiles_to(i, u - 2, QT - 1),
                                              tiles_to(i, u - 1, QT - 1), tiles_to(i, u - 1, QT - 1)][k]))
                    nc.scalar.activation(dst[0][:, :], fill_bank[:, :], ACT.Identity,
                                         bias=bias_of(kind, i, u % 2)).then_inc(S["proj_hi"], 1)

                def hi_values(i, b, k):
                    wait(act, S["v_psum"], v_to(i, b, k))
                    wait(act, S["z_psum"], z_to(i - 1, 2 * b + 1, 1))
                    nc.scalar.activation(vals[b][0][:, 2 * k:2 * k + 2, :].rearrange("p t n -> p (t n)"), fill_bank[:, :],
                                         ACT.Copy).then_inc(S["v_hi"], 1)

                def hi_transposed(i, u, q):
                    c, ql = divmod(q, HT)
                    if ql == 0:
                        bi, bu = (i, u - 1) if u else (i - 1, UNITS - 1)
                        wait(act, S["z_psum"], z_to(bi, bu, c))
                    for n, (k0, count) in enumerate(GROUPS[q]):
                        m = FIRST_GROUP[q] + n
                        wait(act, S["transposed"], UNITS * NG * i + NG * u + m + 1)
                        nc.scalar.activation(pT[c][0][:, k0:k0 + count, ql * P:(ql + 1) * P],
                                             t_bank[m % 2][:, 0:count * P].rearrange("p (k n) -> p k n", n=P), ACT.Copy).then_inc(S["pT_hi"], 1)

                def hi_z(i, u, c):
                    b, head = divmod(u, 2)
                    wait_apart(act, act_spare, (S["z_psum"], z_to(i, u, c)), (S["wo_psum"], wo_to(i, b - 1, 2 * c + 1)))
                    nc.scalar.activation(z[head][0][:, c * HALF:(c + 1) * HALF], z_bank[:, :], ACT.Identity,
                                         bias=bias_of(2, i, head)).then_inc(S["z_hi"], 1)

                def pair(i, first, last):
                    for u, q, fill_list, ahead, has_before in schedule(i, first, last):
                        if ahead:
                            exponential(*after(i, u, q, AHEAD))
                        for _, what, k in fill_list:
                            n, _ = fill_index(i, u, what, k)
                            if what == "proj":
                                hi_projection(*n, k)
                            elif what == "v":
                                hi_values(*n, k)
                        if q == HT:
                            hi_z(i, u, 0)
                        hi_transposed(i, u, q)
                        if q == 0 and has_before:
                            hi_z(*(after(i, u, q, -1)[:2]), 1)

                for k in range(4):
                    hi_projection(0, 0, k)
                for q in range(AHEAD):
                    exponential(0, 0, q)
                for k in range(4):
                    hi_values(0, 0, k)
                pair(0, True, False)
                with act.Fori(1, PAIRS - 1) as i:
                    pair(i, False, False)
                pair(PAIRS - 1, False, True)
                hi_z(PAIRS - 1, UNITS - 1, 1)

            @block.vector
            def _(dve):
                dve_spare = (S["mask_ready"], [dve.alloc_register(f"dve_until_{n}") for n in range(2)])
                v = nc.vector

                def maximum(i, u, q):
                    s = q % SLOTS
                    t = s_tiles[q % 2]
                    n = tiles_to(i, u, q)
                    wait_apart(dve, dve_spare, (S["scores"], n))
                    diag = t[:, q * P:(q + 1) * P]
                    v.tensor_tensor_reduce(out=diag, in0=diag, in1=mask[:, :], scale=1.0, scalar=-3e38, op0=ALU.add,
                                           op1=ALU.max, accum_out=m_diag[:, s:s + 1]).then_inc(S["partial_max"], 1)
                    v.tensor_reduce(out=m_rest[:, s:s + 1], in_=t[:, 0:max(q, 1) * P], axis=AX.X, op=ALU.max).then_inc(S["partial_max"], 1) if q else None
                    wait(dve, S["partial_max"], (2 * QT - 1) * UNITS * i + (2 * QT - 1) * u + 2 * q + 1)
                    other = m_rest if q else m_diag
                    v.tensor_scalar(neg_max[:, s:s + 1], m_diag[:, s:s + 1], other[:, s:s + 1], -SCALE,
                                    ALU.max, ALU.mult).then_inc(S["max_ready"], 1)

                def invert(i, u, q):
                    s = q % SLOTS
                    wait(dve, S["exp_done"], tiles_to(i, u, q))
                    v.reciprocal(inv_sum[:, s:s + 1], row_sum[:, s:s + 1]).then_inc(S["inv_ready"], 1)

                def lo_projection(i, u, k):
                    kind, _, dst = proj_target(u, k)
                    wait(dve, S["proj_hi"], proj_to(i, u, k))
                    v.scalar_tensor_tensor(out=dst[1][:, :], in0=fill_bank[:, :], scalar=bias_of(kind, i, u % 2),
                                           in1=dst[0][:, :].bitcast(F32), op0=ALU.add, op1=ALU.subtract).then_inc(S["proj_lo"], 1)

                def lo_values(i, b, k):
                    hi, lo = [x[:, 2 * k:2 * k + 2, :].rearrange("p t n -> p (t n)") for x in vals[b]]
                    wait(dve, S["v_hi"], v_to(i, b, k))
                    v.tensor_tensor(lo, fill_bank[:, :], hi.bitcast(F32), ALU.subtract).then_inc(S["v_lo"], 1)

                def add_projected(i, b, k):
                    t = b * QT + 2 * k
                    dst = acc[:, t:t + 2, :].rearrange("p t n -> p (t n)")
                    wait(dve, S["wo_psum"], wo_to(i, b, k))
                    v.tensor_tensor(dst, fill_bank[:, :], dst, ALU.add).then_inc(S["wo_added"], 1)

                def lo_transposed(i, u, q):
                    c, ql = divmod(q, HT)
                    for n, (k0, count) in enumerate(GROUPS[q]):
                        m = FIRST_GROUP[q] + n
                        hi, lo = [x[:, k0:k0 + count, ql * P:(ql + 1) * P] for x in pT[c]]
                        wait(dve, S["pT_hi"], UNITS * NG * i + NG * u + m + 1)
                        v.tensor_tensor(lo, t_bank[m % 2][:, 0:count * P].rearrange("p (k n) -> p k n", n=P), hi.bitcast(F32),
                                        ALU.subtract).then_inc(S["pT_lo"], 1)

                def lo_z(i, u, c):
                    head = u % 2
                    hi, lo = [x[:, c * HALF:(c + 1) * HALF] for x in z[head]]
                    wait(dve, S["z_hi"], z_to(i, u, c))
                    v.scalar_tensor_tensor(out=lo, in0=z_bank[:, :], scalar=bias_of(2, i, head), in1=hi.bitcast(F32),
                                           op0=ALU.add, op1=ALU.subtract).then_inc(S["z_lo"], 1)

                def pair(i, first, last):
                    for u, q, fill_list, ahead, has_before in schedule(i, first, last):
                        if ahead:
                            maximum(*after(i, u, q, AHEAD))
                        for _, what, k in fill_list:
                            n, _ = fill_index(i, u, what, k)
                            {"proj": lo_projection, "v": lo_values, "wo": add_projected}[what](*n, k)
                        if q == HT:
                            lo_z(i, u, 0)
                        lo_transposed(i, u, q)
                        if ahead:
                            invert(*after(i, u, q, AHEAD))
                        if q == 0 and has_before:
                            lo_z(*(after(i, u, q, -1)[:2]), 1)

                dve.wait_ge(S["mask_ready"], 1)
                for k in range(4):
                    lo_projection(0, 0, k)
                for q in range(AHEAD):
                    maximum(0, 0, q)
                    invert(0, 0, q)
                for k in range(4):
                    lo_values(0, 0, k)
                pair(0, True, False)
                with dve.Fori(1, PAIRS - 1) as i:
                    pair(i, False, False)
                pair(PAIRS - 1, False, True)
                lo_z(PAIRS - 1, UNITS - 1, 1)
                for k in range(4):
                    add_projected(PAIRS - 1, 1, k)


def experts(nc, sb, sem, g):
    ident, acc, h_hi, h_lo = (g[n] for n in ("ident", "acc", "h_hi", "h_lo"))
    s_tiles, t_bank, z_bank, fill_bank = (g[n] for n in ("s_tiles", "t_bank", "z_bank", "fill_bank"))
    GD = CT * DM
    with ExitStack() as scope:
        def sbl(name, shape, dt=F32):
            return sb(name, shape, dt, scope)

        def split(name, shape):
            return [sbl(f"{name}_hi", shape, F32R), sbl(f"{name}_lo", shape, F32R)]

        x_sb = sbl("x_sb", [P, TILES, DM])
        condT = sbl("condT2", [P, KC, BATCH])
        cexp = sbl("cexp2", [P, KC, BATCH])
        csilu = sbl("csilu2", [P, KC, BATCH, P])
        wm = sbl("wm2", [P, KC, 4 * DM])
        mods = sbl("mods", [P, 4, BATCH, DM])
        bo = sbl("bo", [P, DM])
        clamp = sbl("clamp", [P, BATCH * DM])
        sign = sbl("sign", [P, BATCH * DM])
        rank = sbl("rank", [P, CT, NE])
        raw_w = sbl("raw_w", [P, KC * NE * RANK])
        raw_r = sbl("raw_r", [P, KC, NE])
        w_a = split("w_a", [P, KC * NE * RANK])
        w_b = split("w_b", [P, NE * DM])
        w_r = split("w_r", [P, KC, P])
        stats = sbl("stats2", [P, CT, 6])
        mv = sbl("mv2", [P, CT, 2])
        var = sbl("var2", [P, CT, 2])
        root = sbl("root", [P, CT, 2])
        scratch = sbl("scratch2", [P, CT, 2])
        power = sbl("power2", [P, CT])
        hn = sbl("hn", [P, CT, DM])
        square = sbl("square", [P, DM])
        logitT = sbl("logitT", [P, CHUNK])
        lg, eq, s1, lg2, s2, ex = (sbl(n, [P, CT, NE]) for n in ("lg", "eq", "s1", "lg2", "s2", "ex"))
        m1, m2, pos, den = (sbl(n, [P, CT]) for n in ("m1", "m2", "pos", "den"))
        comb = sbl("comb", [P, TILES, NE])
        upT = [split(f"up{i}", [P, CHUNK]) for i in range(2)]
        res = sbl("res", [P, CT, DM])

        names = ("xr_in", "c2_in", "wm2_in", "bo_in", "router_in", "wa_in", "wb_in", "pow2", "chain2", "c2_exp", "mods_psum",
                 "consts", "wa_hi", "e_split", "router_split", "x_gated", "res_ready", "var2_ready", "guess2", "xn2_ready", "h2_mul", "h2_ready",
                 "squared", "norm2_ready", "h2_T", "h2_hi", "h2_lo", "logit_psum", "logit_sb", "logit_T", "ex_in", "ex_ready",
                 "comb_ready", "up_psum", "up_hi", "up_lo", "down_psum", "mixed", "gated", "stored", "pool_chain")
        S = {n: sem(n) for n in names}

        with nc.Block() as block:
            @block.sync
            def _(sp):
                sp.dma_start(condT[:, :, :], g["cond"]).then_inc(S["c2_in"], 16)
                sp.dma_start(wm[:, :, :], g["wmod"].rearrange("(c p) n -> p c n", p=P)[:, :, 2 * DM:]).then_inc(S["wm2_in"], 16)
                sp.dma_start(bo[:, :], g["b_o"].broadcast_to([P, DM])).then_inc(S["bo_in"], 16)
                sp.dma_start(x_sb[:, :, :], g["x"].rearrange("b (t p) d -> p (b t) d", p=P)).then_inc(S["xr_in"], 16)
                sp.dma_start(raw_r[:, :, :], g["router_w"].rearrange("(c p) n -> p c n", p=P)).then_inc(S["router_in"], 16)
                sp.dma_start(raw_w[:, :], g["wa"]).then_inc(S["wa_in"], 16)
                sp.wait_ge(S["e_split"], 1)
                sp.dma_start(raw_w[:, :], g["wb"]).then_inc(S["wb_in"], 16)
                ov = g["out"].rearrange("b (t p) d -> p (b t) d", p=P)
                with sp.Fori(0, CHUNKS) as n:
                    sp.wait_ge(S["gated"], n + 1)
                    sp.dma_start(ov[:, bass.ds(CT * n, CT), :], x_sb[:, bass.ds(CT * n, CT), :]).then_inc(S["stored"], 16)
                sp.wait_ge(S["stored"], 16 * CHUNKS)

            @block.gpsimd
            def _(pool):
                pool_spare = (S["router_in"], [pool.alloc_register("pool_then")])
                count = [0]

                def link(ins):
                    count[0] += 1
                    ins.then_inc(S["pool_chain"], 1)
                    pool.wait_ge(S["pool_chain"], count[0])

                for j in range(CT):
                    pool.memset(power[:, j:j + 1], -0.5)
                for w in w_r:
                    pool.memset(w[:, :, :].bitcast(F32), 0.0)
                for e in range(NE):
                    last = pool.memset(rank[:, :, e:e + 1], float(NE - e))
                link(last)
                pool.wait_ge(S["router_in"], 16)
                link(pool.tensor_copy(w_r[0][:, :, 0:NE], raw_r[:, :, :]))
                pool.tensor_tensor(w_r[1][:, :, 0:NE], raw_r[:, :, :], w_r[0][:, :, 0:NE].bitcast(F32), ALU.subtract).then_inc(S["router_split"], 1)

                with pool.Fori(0, CHUNKS // 2) as b:
                    for half in range(2):
                        n = 2 * b + half
                        wait_apart(pool, pool_spare, (S["x_gated"], n + 1))
                        t = bass.ds(CT * n, CT)
                        pool.tensor_tensor(x_sb[:, t, :], x_sb[:, t, :], acc[:, t, :], ALU.add).then_inc(S["res_ready"], 1)
                        pool.wait_ge(S["var2_ready"], 2 * n + 1)
                        pool.tensor_tensor(root[:, :, 0], var[:, :, 0], power[:, :], ALU.pow).then_inc(S["guess2"], 1)
                        wait_apart(pool, pool_spare, (S["xn2_ready"], n + 1))
                        pool.tensor_tensor(hn[:, :, :], hn[:, :, :], mods[:, 2, bass.ds(b, 1), :].broadcast_to([P, CT, DM]), ALU.mult).then_inc(S["h2_mul"], 1)
                        wait_apart(pool, pool_spare, (S["h2_mul"], n + 1))
                        pool.tensor_tensor(hn[:, :, :], hn[:, :, :], mods[:, 1, bass.ds(b, 1), :].broadcast_to([P, CT, DM]), ALU.add).then_inc(S["h2_ready"], 1)
                        pool.wait_ge(S["var2_ready"], 2 * n + 2)
                        pool.tensor_tensor(root[:, :, 1], var[:, :, 1], power[:, :], ALU.pow).then_inc(S["guess2"], 1)

            @block.scalar
            def _(act):
                act_spare = (S["wa_in"], [act.alloc_register("act_then")])
                act.wait_ge(S["c2_in"], 16)
                nc.scalar.activation(cexp[:, :, :], condT[:, :, :], ACT.Exp, scale=-1.0).then_inc(S["c2_exp"], 1)
                act.wait_ge(S["wa_in"], 16)
                nc.scalar.activation(w_a[0][:, :], raw_w[:, :], ACT.Copy).then_inc(S["wa_hi"], 1)
                act.wait_ge(S["wb_in"], 16)
                nc.scalar.activation(w_b[0][:, :], raw_w[:, :], ACT.Copy).then_inc(S["wa_hi"], 1)
                with act.Fori(0, CHUNKS) as n:
                    act.wait_ge(S["h2_ready"], n + 1)
                    for t in range(CT):
                        if t:
                            act.wait_ge(S["squared"], CT * n + t)
                        else:
                            act.wait_ge(S["guess2"], 2 * n + 1)
                        nc.scalar.activation(square[:, :], hn[:, t, :], ACT.Square, accum_out=var[:, t, 1:2]).then_inc(S["squared"], 1)
                    act.wait_ge(S["squared"], CT * n + CT)
                    for c in range(KC):
                        wait_apart(act, act_spare, (S["h2_T"], KC * n + c + 1))
                        nc.scalar.activation(h_hi[:, c, bass.ds(CHUNK * n, CHUNK)], t_bank[c][:, :], ACT.Copy).then_inc(S["h2_hi"], 1)
                    act.wait_ge(S["logit_psum"], n + 1)
                    nc.scalar.activation(logitT[:, :], fill_bank[:, :], ACT.Copy).then_inc(S["logit_sb"], 1)
                    act.wait_ge(S["ex_in"], n + 1)
                    nc.scalar.activation(ex[:, :, :], ex[:, :, :], ACT.Exp).then_inc(S["ex_ready"], 1)
                with act.Fori(0, CHUNKS) as n:
                    for e in range(NE):
                        act.wait_ge(S["up_psum"], NE * n + e + 1)
                        nc.scalar.activation(upT[e % 2][0][:, :], [z_bank, fill_bank][e % 2][:, :], ACT.Copy).then_inc(S["up_hi"], 1)

            @block.tensor
            def _(pe):
                mm = nc.tensor.matmul

                def product(dst, a, b, start, stop):
                    mm(dst, a[0], b[0], start=start, stop=False)
                    mm(dst, a[0], b[1], start=False, stop=False)
                    return mm(dst, a[1], b[0], start=False, stop=stop)

                pe.wait_ge(S["chain2"], 3)
                pe.wait_ge(S["wm2_in"], 16)
                for k in range(4):
                    for b in range(BATCH):
                        for c in range(KC):
                            last = mm(s_tiles[k // 2][:, (k % 2) * HALF + b * DM:(k % 2) * HALF + (b + 1) * DM], csilu[:, c, b, :],
                                      wm[:, c, k * DM:(k + 1) * DM], start=(c == 0), stop=(c == KC - 1))
                last.then_inc(S["mods_psum"], 1)
                pe.wait_ge(S["router_split"], 1)
                with pe.Fori(0, CHUNKS) as n:
                    pe.wait_ge(S["h2_ready"], n + 1)
                    for c in range(KC):
                        for t in range(CT):
                            last = nc.tensor.transpose(t_bank[c][:, t * P:(t + 1) * P], hn[:, t, c * P:(c + 1) * P], ident[:, :])
                        last.then_inc(S["h2_T"], 1)
                    pe.wait_ge(S["h2_lo"], KC * n + KC)
                    cols = bass.ds(CHUNK * n, CHUNK)
                    for c in range(KC):
                        last = product(fill_bank[:, :], [w[:, c, :] for w in w_r], [h_hi[:, c, cols], h_lo[:, c, cols]], c == 0, c == KC - 1)
                    last.then_inc(S["logit_psum"], 1)
                    pe.wait_ge(S["logit_sb"], n + 1)
                    for t in range(CT):
                        last = nc.tensor.transpose(z_bank[:, t * P:(t + 1) * P], logitT[:, t * P:(t + 1) * P], ident[:, :])
                    last.then_inc(S["logit_T"], 1)
                    pe.wait_ge(S["comb_ready"], n + 1)

                pe.wait_ge(S["e_split"], 2)
                with pe.Fori(0, CHUNKS) as n:
                    cols = bass.ds(CHUNK * n, CHUNK)

                    def up(e, first):
                        if not first:
                            pe.wait_ge(S["up_lo"], NE * n + e - 1)
                        for c in range(KC):
                            w = [x[:, (c * NE + e) * RANK:(c * NE + e + 1) * RANK] for x in w_a]
                            last = product([z_bank, fill_bank][e % 2][:, :], w, [h_hi[:, c, cols], h_lo[:, c, cols]], c == 0, c == KC - 1)
                        last.then_inc(S["up_psum"], 1)

                    def down(e):
                        pe.wait_ge(S["up_lo"], NE * n + e + 1)
                        if e >= 2:
                            pe.wait_ge(S["mixed"], CT * (NE * n + e - 1))
                        for t in range(CT):
                            last = product(s_tiles[e % 2][:, t * DM:(t + 1) * DM], [x[:, t * P:(t + 1) * P] for x in upT[e % 2]],
                                           [x[:, e * DM:(e + 1) * DM] for x in w_b], True, True)
                            if t % 2:
                                last.then_inc(S["down_psum"], 1)

                    up(0, True)
                    for e in range(NE):
                        if e + 1 < NE:
                            up(e + 1, e == 0)
                        down(e)
                    pe.wait_ge(S["mixed"], CT * NE * n + CT * NE)

            @block.vector
            def _(dve):
                dve_spare = (S["bo_in"], [dve.alloc_register("dve_then")])
                v = nc.vector
                count = [0]

                def link(ins):
                    count[0] += 1
                    ins.then_inc(S["chain2"], 1)
                    dve.wait_ge(S["chain2"], count[0])

                dve.wait_ge(S["c2_exp"], 1)
                link(v.tensor_scalar_add(cexp[:, :, :], cexp[:, :, :], 1.0))
                link(v.reciprocal(cexp[:, :, :], cexp[:, :, :]))
                link(v.tensor_tensor(csilu[:, :, :, :], condT[:, :, :].unsqueeze(3).broadcast_to([P, KC, BATCH, P]),
                                     cexp[:, :, :].unsqueeze(3).broadcast_to([P, KC, BATCH, P]), ALU.mult))
                dve.wait_ge(S["mods_psum"], 1)
                for k, bank in ((0, s_tiles[0][:, 0:HALF]), (3, s_tiles[1][:, HALF:])):
                    link(v.tensor_scalar(clamp[:, :], bank, -1.0, None, ALU.mult))
                    link(v.tensor_tensor(clamp[:, :], clamp[:, :], bank, ALU.max))
                    link(v.tensor_scalar(clamp[:, :], clamp[:, :], 0.25, None, ALU.max))
                    link(v.tensor_scalar(sign[:, :], bank, 0.0, None, ALU.is_ge))
                    link(v.tensor_scalar(sign[:, :], sign[:, :], 2.0, -1.0, ALU.mult, ALU.add))
                    link(v.tensor_tensor(mods[:, k, :, :].rearrange("p b n -> p (b n)"), clamp[:, :], sign[:, :], ALU.mult))
                link(v.tensor_copy(mods[:, 1, :, :].rearrange("p b n -> p (b n)"), s_tiles[0][:, HALF:]))
                link(v.tensor_scalar_add(mods[:, 2, :, :].rearrange("p b n -> p (b n)"), s_tiles[1][:, 0:HALF], 1.0))
                dve.wait_ge(S["wa_hi"], 1)
                v.tensor_tensor(w_a[1][:, :], raw_w[:, :], w_a[0][:, :].bitcast(F32), ALU.subtract).then_inc(S["e_split"], 1)
                dve.wait_ge(S["wa_hi"], 2)
                v.tensor_tensor(w_b[1][:, :], raw_w[:, :], w_b[0][:, :].bitcast(F32), ALU.subtract).then_inc(S["e_split"], 1)
                dve.wait_ge(S["bo_in"], 16)
                dve.wait_ge(S["xr_in"], 16)
                setup = count[0]
                LINKS = 27
                with dve.Fori(0, CHUNKS // 2) as b:
                    for half in range(2):
                        n = 2 * b + half
                        made = [0]

                        def step(ins):
                            made[0] += 1
                            ins.then_inc(S["chain2"], 1)
                            dve.wait_ge(S["chain2"], LINKS * n + setup + made[0])

                        t = bass.ds(CT * n, CT)
                        step(v.tensor_tensor(acc[:, t, :], acc[:, t, :], bo[:, :].unsqueeze(1).broadcast_to([P, CT, DM]), ALU.add))
                        v.tensor_tensor(acc[:, t, :], acc[:, t, :], mods[:, 0, bass.ds(b, 1), :].broadcast_to([P, CT, DM]),
                                        ALU.mult).then_inc(S["x_gated"], 1)
                        dve.wait_ge(S["res_ready"], n + 1)
                        for j in range(CT):
                            last = v.bn_stats(stats[:, j, :], x_sb[:, bass.ds(CT * n + j, 1), :].rearrange("p o d -> p (o d)"))
                        made[0] += 1
                        last.then_inc(S["chain2"], 1)
                        wait_apart(dve, dve_spare, (S["chain2"], LINKS * n + setup + made[0]))
                        for j in range(CT):
                            last = v.bn_aggr(mv[:, j, :], stats[:, j, :])
                        step(last)
                        v.tensor_scalar_add(var[:, :, 0], mv[:, :, 1], EPS).then_inc(S["var2_ready"], 1)
                        dve.wait_ge(S["guess2"], 2 * n + 1)
                        rsqrt_newton(v, step, root[:, :, 0], var[:, :, 0], scratch[:, :, 0])
                        for j in range(CT):
                            last = v.tensor_scalar(hn[:, j, :], x_sb[:, bass.ds(CT * n + j, 1), :].rearrange("p o d -> p (o d)"),
                                                   mv[:, j, 0:1], root[:, j, 0:1], ALU.subtract, ALU.mult)
                        last.then_inc(S["xn2_ready"], 1)
                        for c in range(KC):
                            dve.wait_ge(S["h2_hi"], KC * n + c + 1)
                            cols = bass.ds(CHUNK * n, CHUNK)
                            v.tensor_tensor(h_lo[:, c, cols], t_bank[c][:, :], h_hi[:, c, cols].bitcast(F32), ALU.subtract).then_inc(S["h2_lo"], 1)
                        dve.wait_ge(S["squared"], CT * n + CT)
                        v.tensor_scalar_max(var[:, :, 1], var[:, :, 1], 1e-24).then_inc(S["var2_ready"], 1)
                        dve.wait_ge(S["guess2"], 2 * n + 2)
                        rsqrt_newton(v, step, root[:, :, 1], var[:, :, 1], scratch[:, :, 1])
                        wide = [P, CT, NE]
                        dve.wait_ge(S["logit_T"], n + 1)
                        zl = z_bank[:, :].rearrange("p (t n) -> p t n", n=P)[:, :, 0:NE]
                        step(v.tensor_tensor(lg[:, :, :], zl, root[:, :, 1:2].broadcast_to(wide), ALU.mult))
                        step(v.tensor_reduce(out=m1[:, :], in_=lg[:, :, :], axis=AX.X, op=ALU.max))
                        v.tensor_tensor(ex[:, :, :], lg[:, :, :], m1[:, :].unsqueeze(2).broadcast_to(wide), ALU.subtract).then_inc(S["ex_in"], 1)

                        def pick(src, best, sel):
                            step(v.tensor_tensor(eq[:, :, :], src[:, :, :], best[:, :].unsqueeze(2).broadcast_to(wide), ALU.is_equal))
                            step(v.tensor_tensor(eq[:, :, :], eq[:, :, :], rank[:, :, :], ALU.mult))
                            step(v.tensor_reduce(out=pos[:, :], in_=eq[:, :, :], axis=AX.X, op=ALU.max))
                            step(v.tensor_tensor(sel[:, :, :], eq[:, :, :], pos[:, :].unsqueeze(2).broadcast_to(wide), ALU.is_equal))

                        pick(lg, m1, s1)
                        step(v.scalar_tensor_tensor(out=lg2[:, :, :], in0=s1[:, :, :], scalar=MASKED, in1=lg[:, :, :], op0=ALU.mult, op1=ALU.add))
                        step(v.tensor_reduce(out=m2[:, :], in_=lg2[:, :, :], axis=AX.X, op=ALU.max))
                        pick(lg2, m2, s2)
                        step(v.tensor_tensor(s1[:, :, :], s1[:, :, :], s2[:, :, :], ALU.add))
                        dve.wait_ge(S["ex_ready"], n + 1)
                        step(v.tensor_tensor(s2[:, :, :], s1[:, :, :], ex[:, :, :], ALU.mult))
                        step(v.tensor_reduce(out=den[:, :], in_=s2[:, :, :], axis=AX.X, op=ALU.add))
                        step(v.reciprocal(den[:, :], den[:, :]))
                        v.tensor_tensor(comb[:, t, :], s2[:, :, :], den[:, :].unsqueeze(2).broadcast_to(wide), ALU.mult).then_inc(S["comb_ready"], 1)
                        dve.wait_ge(S["comb_ready"], n + 1)
                        assert made[0] == LINKS, made
                with dve.Fori(0, CHUNKS) as n:
                    for e in range(NE):
                        hi, lo = upT[e % 2]
                        dve.wait_ge(S["up_hi"], NE * n + e + 1)
                        v.tensor_tensor(lo[:, :], [z_bank, fill_bank][e % 2][:, :], hi[:, :].bitcast(F32), ALU.subtract).then_inc(S["up_lo"], 1)
                        for t in range(CT):
                            k = CT * (NE * n + e) + t
                            if t % 2 == 0:
                                dve.wait_ge(S["down_psum"], CT // 2 * (NE * n + e) + t // 2 + 1)
                            y = s_tiles[e % 2][:, t * DM:(t + 1) * DM]
                            weight = comb[:, bass.ds(CT * n + t, 1), e:e + 1].rearrange("p o e -> p (o e)")
                            if e == 0:
                                v.tensor_scalar(res[:, t, :], y, weight, None, ALU.mult).then_inc(S["mixed"], 1)
                            else:
                                dve.wait_ge(S["mixed"], k + 1 - CT)
                                v.scalar_tensor_tensor(out=res[:, t, :], in0=y, scalar=weight, in1=res[:, t, :],
                                                       op0=ALU.mult, op1=ALU.add).then_inc(S["mixed"], 1)
                    b = n // 2
                    dve.wait_ge(S["mixed"], CT * NE * n + CT * NE)
                    t = bass.ds(CT * n, CT)
                    v.tensor_tensor(res[:, :, :], res[:, :, :], mods[:, 3, bass.ds(b, 1), :].broadcast_to([P, CT, DM]), ALU.mult).then_inc(S["pow2"], 1)
                    dve.wait_ge(S["pow2"], n + 1)
                    v.tensor_tensor(x_sb[:, t, :], x_sb[:, t, :], res[:, :, :], ALU.add).then_inc(S["gated"], 1)
                    dve.wait_ge(S["gated"], n + 1)


_OUT = ((BATCH, SEQ, DM), "float32")


def kernel(**inputs):
    import numpy as _np
    import concourse.bacc as _bacc
    from concourse import mybir as _mybir
    from concourse.bass_utils import run_bass_kernel_spmd as _run

    a = {k.replace("L0_", "").replace("attn_", "").replace("ffn_", ""): _np.asarray(v) for k, v in inputs.items()}

    def by_pair(w):
        w = w.reshape(PAIRS, 2, KC, P, DH).transpose(0, 3, 2, 1, 4)
        return w.reshape(PAIRS, P, KC * 2 * DH)

    arrays = {
        "x": a["x"],
        "wqkv": _np.stack([by_pair(a["W_Q"]), by_pair(a["W_K"]), by_pair(a["W_V"])], axis=2),
        "wo": a["W_O"].reshape(PAIRS, 2, DH, DM).transpose(0, 2, 1, 3).reshape(PAIRS, DH, 2 * DM),
        "bias": _np.stack([a["b_Q"].T, a["b_K"].T, a["b_V"].T], axis=1),
        "b_o": a["b_O"].reshape(1, DM),
        "router_w": a["router_w"],
        "wa": a["Wa"].reshape(NE, KC, P, RANK).transpose(2, 1, 0, 3).reshape(P, KC * NE * RANK),
        "wb": a["Wb"].transpose(1, 0, 2).reshape(RANK, NE * DM),
        "cond": a["c"].reshape(BATCH, KC, P).transpose(2, 1, 0),
        "wmod": a["wmod"],
    }
    nc = _bacc.Bacc("TRN2", target_bir_lowering=False, num_devices=1)
    maps, args = {}, []
    for name, v in arrays.items():
        v = _np.ascontiguousarray(v)
        maps[f"in_{name}"] = v
        args.append(nc.dram_tensor(f"in_{name}", v.shape, _mybir.dt.from_np(v.dtype), kind="ExternalInput").ap())
    shape, dtype = _OUT
    args.append(nc.dram_tensor("out_0", shape, _mybir.dt.from_np(_np.dtype(dtype)), kind="ExternalOutput").ap())
    adaln_block(nc, *args)
    r = _run(nc, [maps], core_ids=[0])
    return r.results[0]["out_0"]
```

```python
from contextlib import ExitStack

import concourse.bass as bass
from concourse import mybir

P = 128
BATCH, SEQ, DM, NH, DH = 2, 1024, 256, 16, 128
TOK = BATCH * SEQ
KC = DM // P
TILES = TOK // P
QT = SEQ // P
HALF = SEQ // 2
HT = HALF // P
PAIRS = NH // 2
UNITS = 2 * BATCH
NE, RANK = 8, 128
CHUNK = 512
CHUNKS = TOK // CHUNK
CT = CHUNK // P
EPS = 1e-5
SCALE = float(DH) ** -0.5
MASKED = -1e30
NMOD = 6 * DM

F32 = mybir.dt.float32
F32R = mybir.dt.float32r
ALU = mybir.AluOpType
ACT = mybir.ActivationFunctionType
AX = mybir.AxisListType

GROUPS = [[(0, min(q + 1, HT))] + ([(HT, q + 1 - HT)] if q >= HT else []) for q in range(QT)]
FIRST_GROUP = [sum(len(g) for g in GROUPS[:q]) for q in range(QT + 1)]
NG = FIRST_GROUP[QT]

PIECES_EVEN = [(0, "wo", 0), (1, "z", 1), (2, "wo", 1), (3, "proj", 0), (4, "proj", 1), (5, "z", 0),
               (6, "proj", 2), (6, "wo", 2), (7, "proj", 3), (7, "wo", 3)]
PIECES_ODD = [(0, "v", 0), (1, "z", 1), (2, "v", 1), (3, "proj", 0), (4, "proj", 1), (5, "z", 0),
              (6, "proj", 2), (6, "v", 2), (7, "proj", 3), (7, "v", 3)]
PIECES = [PIECES_EVEN, PIECES_ODD]


def has_piece(first, last, u, what, k):
    if first and u == 0 and (what == "wo" or (what, k) == ("z", 1)):
        return False
    return not (last and u == UNITS - 1 and what in ("proj", "v"))


def wait(eng, sem, value):
    if isinstance(value, int) and value <= 0:
        return
    eng.wait_ge(sem, value)


def wait_apart(eng, spare, *waits):
    holds, registers = spare
    if not all(isinstance(v, int) for _, v in waits):
        for register, (_, v) in zip(registers, waits):
            eng.reg_mov(register, v)
        waits = [(sem, register) for register, (sem, _) in zip(registers, waits)]
        eng.wait_ge(holds, 1)
    for sem, v in waits:
        wait(eng, sem, v)


def adaln_block(nc, x, wqkv, wo, bias, b_o, router_w, wa, wb, cond, wmod, out):
    ctx = ExitStack()
    with ctx:
        def sb(name, shape, dt=F32, scope=ctx):
            return scope.enter_context(nc.sbuf_tensor(name, shape, dt))

        def pb(name, shape):
            return ctx.enter_context(nc.psum_tensor(name, shape, F32))

        def sem(name):
            return ctx.enter_context(nc.semaphore(name))

        ident = sb("ident", [P, P])
        mod = sb("mod", [P, 2, KC, BATCH])
        biases = sb("biases", [P, 3, NH])
        h_hi = sb("h_hi", [P, KC, TOK], F32R)
        h_lo = sb("h_lo", [P, KC, TOK], F32R)
        acc = sb("acc", [P, TILES, DM])

        s_tiles = [pb(f"s_tile{i}", [P, SEQ]) for i in range(2)]
        t_bank = [pb(f"t_bank{i}", [P, HALF]) for i in range(2)]
        p_bank = [pb(f"p_bank{i}", [P, HALF]) for i in range(2)]

        prepare(nc, sb, sem, locals())
        attend(nc, sb, sem, locals())
        experts(nc, sb, sem, locals())


def rsqrt_newton(dve, link, y, v, t):
    link(dve.tensor_tensor(t, y, y, ALU.mult))
    link(dve.tensor_tensor(t, t, v, ALU.mult))
    link(dve.tensor_scalar(t, t, -0.5, 1.5, ALU.mult, ALU.add))
    link(dve.tensor_tensor(y, y, t, ALU.mult))


def prepare(nc, sb, sem, g):
    ident, mod, biases, h_hi, h_lo, acc = (g[n] for n in ("ident", "mod", "biases", "h_hi", "h_lo", "acc"))
    banks = [g["s_tiles"][i][:, HALF * k:HALF * (k + 1)] for i in range(2) for k in range(2)]
    mod_bank = g["p_bank"][0]
    with ExitStack() as scope:
        condT = sb("condT", [P, KC, BATCH], scope=scope)
        cexp = sb("cexp", [P, KC, BATCH], scope=scope)
        csilu = sb("csilu", [P, KC, BATCH], scope=scope)
        wm = sb("wm", [P, KC, 2 * DM], scope=scope)
        stats = sb("stats", [P, TILES, 6], scope=scope)
        mv = sb("mv", [P, TILES, 2], scope=scope)
        var = sb("var", [P, TILES], scope=scope)
        rstd = sb("rstd", [P, TILES], scope=scope)
        scratch = sb("scratch", [P, TILES], scope=scope)
        power = sb("power", [P, TILES], scope=scope)
        xn = sb("xn", [P, TILES, DM], scope=scope)
        full = sb("full", [P, 2, CHUNK], scope=scope)
        x_in, cond_in, wm_in, bias_in = (sem(n) for n in ("x_in", "cond_in", "wm_in", "bias_in"))
        x_in1 = sem("x_in1")
        id_zero, id_ready, pow_ready = sem("id_zero"), sem("id_ready"), sem("pow_ready")
        c_exp, mod_psum, mod_ready = sem("c_exp"), sem("mod_psum"), sem("mod_ready")
        var_ready, guess_ready, xn_ready = sem("var_ready"), sem("guess_ready"), sem("xn_ready")
        xT_ready, hhi_ready, full_ready, hlo_ready = (sem(n) for n in ("xT_ready", "hhi_ready", "full_ready", "hlo_ready"))
        chain = sem("prep_chain")
        NB = BATCH * 2 * KC

        def where(n):
            b, r = divmod(n, 2 * KC)
            half, c = divmod(r, KC)
            return b, half, c

        with nc.Block() as block:
            @block.sync
            def _(sp):
                sp.dma_start(condT[:, :, :], g["cond"]).then_inc(cond_in, 16)
                xv = g["x"].rearrange("b (t p) d -> p (b t) d", p=P)
                sp.dma_start(acc[:, 0:QT, :], xv[:, 0:QT, :]).then_inc(x_in, 16)
                sp.dma_start(wm[:, :, :], g["wmod"].rearrange("(c p) n -> p c n", p=P)[:, :, 0:2 * DM]).then_inc(wm_in, 16)
                sp.dma_start(acc[:, QT:, :], xv[:, QT:, :]).then_inc(x_in1, 16)
                sp.dma_start(biases[:, :, :], g["bias"]).then_inc(bias_in, 16)
                sp.wait_ge(bias_in, 16)

            @block.gpsimd
            def _(pool):
                pool.memset(power[:, :], -0.5).then_inc(pow_ready, 1)
                pool.memset(ident[:, :], 0.0).then_inc(id_zero, 1)
                pool.wait_ge(id_zero, 1)
                pool.affine_select(out=ident[:, :], in_=ident[:, :], compare_op=ALU.not_equal, fill=1.0,
                                   base=0, pattern=[[-1, P]], channel_multiplier=1).then_inc(id_ready, 1)
                pool.wait_ge(pow_ready, 1)
                for b in range(BATCH):
                    t = slice(b * QT, (b + 1) * QT)
                    pool.wait_ge(var_ready, b + 1)
                    pool.tensor_tensor(rstd[:, t], var[:, t], power[:, t], ALU.pow).then_inc(guess_ready, 1)
                pool.wait_ge(xn_ready, TILES)
                pool.memset(acc[:, :, :], 0.0)

            @block.scalar
            def _(act):
                act.wait_ge(cond_in, 16)
                nc.scalar.activation(cexp[:, :, :], condT[:, :, :], ACT.Exp, scale=-1.0).then_inc(c_exp, 1)
                act.wait_ge(mod_ready, 1)
                for n in range(NB):
                    b, half, c = where(n)
                    cols = slice(b * SEQ + half * HALF, b * SEQ + (half + 1) * HALF)
                    act.wait_ge(xT_ready, n + 1)
                    nc.scalar.activation(h_hi[:, c, cols], banks[n % 4], ACT.Identity, scale=mod[:, 0, c, b:b + 1],
                                         bias=mod[:, 1, c, b:b + 1]).then_inc(hhi_ready, 1)

            @block.tensor
            def _(pe):
                pe.wait_ge(chain, 3)
                pe.wait_ge(wm_in, 16)
                for k in range(2):
                    for m in range(KC):
                        for c in range(KC):
                            col = k * DM + m * P
                            last = nc.tensor.matmul(mod_bank[:, (k * KC + m) * BATCH:(k * KC + m + 1) * BATCH],
                                                    wm[:, c, col:col + P], csilu[:, c, :], start=(c == 0), stop=(c == KC - 1))
                last.then_inc(mod_psum, 1)
                pe.wait_ge(id_ready, 1)
                for n in range(NB):
                    b, half, c = where(n)
                    pe.wait_ge(xn_ready, b * QT + (half + 1) * HT)
                    if n >= 4:
                        pe.wait_ge(full_ready, n - 3)
                    for i in range(HT):
                        t = b * QT + half * HT + i
                        last = nc.tensor.transpose(banks[n % 4][:, i * P:(i + 1) * P], xn[:, t, c * P:(c + 1) * P], ident[:, :])
                    last.then_inc(xT_ready, 1)

            @block.vector
            def _(dve):
                count = [0]

                def link(ins):
                    count[0] += 1
                    ins.then_inc(chain, 1)
                    dve.wait_ge(chain, count[0])

                v = nc.vector
                dve.wait_ge(c_exp, 1)
                link(v.tensor_scalar_add(cexp[:, :, :], cexp[:, :, :], 1.0))
                link(v.reciprocal(cexp[:, :, :], cexp[:, :, :]))
                link(v.tensor_tensor(csilu[:, :, :], condT[:, :, :], cexp[:, :, :], ALU.mult))
                for b in range(BATCH):
                    dve.wait_ge(x_in1 if b else x_in, 16)
                    for t in range(b * QT, (b + 1) * QT):
                        last = v.bn_stats(stats[:, t, :], acc[:, t, :])
                    link(last)
                    for t in range(b * QT, (b + 1) * QT):
                        last = v.bn_aggr(mv[:, t, :], stats[:, t, :])
                    link(last)
                    ts = slice(b * QT, (b + 1) * QT)
                    v.tensor_scalar_add(var[:, ts], mv[:, ts, 1], EPS).then_inc(var_ready, 1)
                    if b == 0:
                        dve.wait_ge(mod_psum, 1)
                        mp = mod_bank[:, 0:2 * KC * BATCH].rearrange("p (k c b) -> p k c b", k=2, c=KC)
                        link(v.tensor_scalar_add(mod[:, 0, :, :], mp[:, 1, :, :], 1.0))
                        v.tensor_copy(mod[:, 1, :, :], mp[:, 0, :, :]).then_inc(mod_ready, 1)
                    dve.wait_ge(guess_ready, b + 1)
                    rsqrt_newton(v, link, rstd[:, ts], var[:, ts], scratch[:, ts])
                    for t in range(b * QT, (b + 1) * QT):
                        v.tensor_scalar(xn[:, t, :], acc[:, t, :], mv[:, t, 0:1], rstd[:, t:t + 1],
                                        ALU.subtract, ALU.mult).then_inc(xn_ready, 1)
                    if b == 0:
                        dve.wait_ge(mod_ready, 1)
                    for n in range(b * 2 * KC, (b + 1) * 2 * KC):
                        _, half, c = where(n)
                        cols = slice(b * SEQ + half * HALF, b * SEQ + (half + 1) * HALF)
                        dve.wait_ge(hhi_ready, n + 1)
                        if n >= 2:
                            dve.wait_ge(hlo_ready, n - 1)
                        v.tensor_scalar(full[:, n % 2, :], banks[n % 4], mod[:, 0, c, b:b + 1], mod[:, 1, c, b:b + 1],
                                        ALU.mult, ALU.add).then_inc(full_ready, 1)
                        dve.wait_ge(full_ready, n + 1)
                        v.tensor_tensor(h_lo[:, c, cols], full[:, n % 2, :], h_hi[:, c, cols].bitcast(F32),
                                        ALU.subtract).then_inc(hlo_ready, 1)


def attend(nc, sb, sem, g):
    ident, biases, h_hi, h_lo, acc = (g[n] for n in ("ident", "biases", "h_hi", "h_lo", "acc"))
    s_tiles, t_bank, p_bank = (g[n] for n in ("s_tiles", "t_bank", "p_bank"))
    AHEAD, SLOTS = 2, 4
    with ExitStack() as scope:
        def sbl(name, shape, dt=F32):
            return sb(name, shape, dt, scope)

        def split(name, shape):
            return [sbl(f"{name}_hi", shape, F32R), sbl(f"{name}_lo", shape, F32R)]

        w_qkv = split("w_qkv", [P, 3, KC, 2 * DH])
        w_o = split("w_o", [P, 2, DM])
        raw_qkv = sbl("raw_qkv", [P, 3, KC * 2 * DH])
        raw_o = sbl("raw_o", [P, 2 * DM])
        q_half = [split(f"q{i}", [P, HALF]) for i in range(2)]
        k_first = [split(f"k0_{i}", [P, HALF]) for i in range(2)]
        k_second = split("k1", [P, HALF])
        vals = [split(f"v{b}", [P, QT, 2 * DH]) for b in range(BATCH)]
        pT = [split("pT0", [P, HT, HALF]), split("pT1", [P, QT, HALF])]
        z = [split(f"z{i}", [P, SEQ]) for i in range(2)]
        probs = [sbl(f"probs{i}", [P, (HT + 1 + i) * P]) for i in range(SLOTS)]
        mask = sbl("mask", [P, P])
        m_diag, m_rest, neg_max, row_sum, inv_sum = (sbl(n, [P, SLOTS]) for n in ("m_diag", "m_rest", "neg_max", "row_sum", "inv_sum"))

        names = ("raw_qkv_in", "raw_o_in", "mask_zero", "mask_ready", "w_hi", "w_split",
                 "scores", "partial_max", "max_ready", "exp_done", "inv_ready", "normed",
                 "transposed", "pT_hi", "pT_lo", "z_psum", "z_hi", "z_lo",
                 "proj_psum", "proj_hi", "proj_lo", "v_psum", "v_hi", "v_lo", "wo_psum", "wo_added")
        S = {n: sem(n) for n in names}

        def tiles_to(i, u, q):
            return UNITS * QT * i + QT * u + q + 1

        def groups_to(i, u, q):
            return UNITS * NG * i + NG * u + FIRST_GROUP[q + 1]

        def z_to(i, u, c):
            return 2 * UNITS * i + 2 * u + c + 1

        def proj_to(i, u, k):
            return 4 * UNITS * i + 4 * u + k + 1

        def v_to(i, b, k):
            return 4 * BATCH * i + 4 * b + k + 1

        def wo_to(i, b, k):
            return 4 * BATCH * i + 4 * b + k + 1

        def wsplit_to(i, k):
            return 3 + 4 * i + k + 1

        def after(i, u, q, n):
            t = QT * u + q + n
            return i + t // (UNITS * QT), t // QT % UNITS, t % QT

        def before_unit(i, u):
            return (i, u - 1) if u else (i - 1, UNITS - 1)

        def next_unit(i, u):
            return (i, u + 1) if u + 1 < UNITS else (i + 1, 0)

        def target(i, u, what, k):
            if what == "z":
                return (i, u) if k == 0 else before_unit(i, u)
            if what == "proj":
                return next_unit(i, u)
            if what == "v":
                return (i, 1) if u == 1 else (i + 1, 0)
            return (i, 0) if u == 2 else (i - 1, 1)

        COUNT = {"z": z_to, "proj": proj_to, "v": v_to, "wo": wo_to}
        LEFT = {"z": S["z_lo"], "proj": S["proj_lo"], "v": S["v_lo"], "wo": S["wo_added"]}

        def bank_free(eng, i, u, n, first, last):
            def same(pieces):
                return [(what, k) for m, (_, what, k) in pieces if m % 2 == n % 2]

            here = [(m, x) for m, x in enumerate(PIECES[u % 2][:n]) if has_piece(first, last, u, *x[1:])]
            if same(here):
                bi, bu, (what, k) = i, u, same(here)[-1]
            elif first and u == 0:
                wait(eng, LEFT["v"], v_to(0, 0, 2 + n % 2))
                return
            else:
                bi, bu = before_unit(i, u)
                what, k = same([(m, x) for m, x in enumerate(PIECES[bu % 2]) if has_piece(first and bu == u - 1, False, bu, *x[1:])])[-1]
            wait(eng, LEFT[what], COUNT[what](*target(bi, bu, what, k), k))

        def schedule(first, last):
            for u in range(UNITS):
                for q in range(QT):
                    pieces = [(n, what, k) for n, (at, what, k) in enumerate(PIECES[u % 2])
                              if at == q and has_piece(first, last, u, what, k)]
                    left = QT * (UNITS - u) - q - 1 if last else QT
                    yield u, q, pieces, left >= AHEAD, left >= 1

        def bias_of(kind, i, head):
            return biases[:, kind, bass.ds(2 * i + head, 1)]

        def proj_target(u, k):
            return [(0, 0, q_half[0]), (1, 0, k_first[u % 2]), (1, 1, k_second), (0, 1, q_half[1])][k]

        with nc.Block() as block:
            @block.sync
            def _(sp):
                def load(i, what, when):
                    if when is not None:
                        sp.wait_ge(S["w_split"], when)
                    if what == "qkv":
                        sp.dma_start(raw_qkv[:, :, :], g["wqkv"][bass.ds(i, 1), :, :, :].rearrange("o p k n -> p (o k) n")).then_inc(S["raw_qkv_in"], 16)
                    else:
                        sp.dma_start(raw_o[:, :], g["wo"][bass.ds(i, 1), :, :].rearrange("o p n -> p (o n)")).then_inc(S["raw_o_in"], 16)

                load(0, "qkv", None)
                load(0, "o", None)
                load(1, "qkv", 3)
                with sp.Fori(1, PAIRS - 1) as i:
                    load(i, "o", wsplit_to(i - 1, 0))
                    load(i + 1, "qkv", wsplit_to(i - 1, 3))
                load(PAIRS - 1, "o", wsplit_to(PAIRS - 2, 0))

            @block.gpsimd
            def _(pool):
                pool_spare = (S["mask_ready"], [pool.alloc_register(f"pool_until_{n}") for n in range(2)])
                def normalise(i, u, q):
                    s = q % SLOTS
                    w = (q + 1) * P
                    wait(pool, S["inv_ready"], tiles_to(i, u, q))
                    pool.tensor_tensor(probs[s][:, 0:w], probs[s][:, 0:w], inv_sum[:, s:s + 1].broadcast_to([P, w]),
                                       ALU.mult).then_inc(S["normed"], 1)

                def split_weights(raw, pair, n):
                    hi, lo = pair
                    pool.tensor_copy(hi, raw).then_inc(S["w_hi"], 1)
                    wait(pool, S["w_hi"], n)
                    pool.tensor_tensor(lo, raw, hi.bitcast(F32), ALU.subtract).then_inc(S["w_split"], 1)

                def w_of(kind):
                    return [w[:, kind, :, :].rearrange("p c n -> p (c n)") for w in w_qkv]

                def w_o_all():
                    return [w[:, :, :].rearrange("p h n -> p (h n)") for w in w_o]

                def pair(i, first, last):
                    for u, q, _, _, more in schedule(first, last):
                        if (u, q) == (1, 0):
                            wait_apart(pool, pool_spare, (S["raw_o_in"], 16 * (i + 1)), (S["wo_psum"], wo_to(i - 1, 1, 3)))
                            split_weights(raw_o[:, :], w_o_all(), wsplit_to(i, 0))
                        if (u, q) == (2, 0) and not last:
                            wait_apart(pool, pool_spare, (S["raw_qkv_in"], 16 * (i + 2)), (S["v_psum"], v_to(i, 1, 3)))
                            split_weights(raw_qkv[:, 2, :], w_of(2), wsplit_to(i, 1))
                        if (u, q) == (3, 0) and not last:
                            for kind in range(2):
                                wait_apart(pool, pool_spare, (S["proj_psum"], proj_to(i, 3, 3)))
                                split_weights(raw_qkv[:, kind, :], w_of(kind), wsplit_to(i, 2 + kind))
                        if more:
                            normalise(*after(i, u, q, 1))

                pool.memset(mask[:, :], 0.0).then_inc(S["mask_zero"], 1)
                pool.wait_ge(S["mask_zero"], 1)
                pool.affine_select(out=mask[:, :], in_=mask[:, :], compare_op=ALU.is_ge, fill=MASKED,
                                   base=0, pattern=[[-1, P]], channel_multiplier=1).then_inc(S["mask_ready"], 1)
                pool.wait_ge(S["raw_qkv_in"], 16)
                for kind in range(3):
                    split_weights(raw_qkv[:, kind, :], w_of(kind), kind + 1)
                normalise(0, 0, 0)
                pair(0, True, False)
                with pool.Fori(1, PAIRS - 1) as i:
                    pair(i, False, False)
                pair(PAIRS - 1, False, True)

            @block.tensor
            def _(pe):
                mm = nc.tensor.matmul

                def product(dst, a, b, start, stop):
                    mm(dst, a[0], b[0], start=start, stop=False)
                    mm(dst, a[0], b[1], start=False, stop=False)
                    return mm(dst, a[1], b[0], start=False, stop=stop)

                def cut(pair, *idx):
                    return [x[idx] for x in pair]

                def score(i, u, q):
                    wait(pe, S["exp_done"], tiles_to(i, u, q) - 2)
                    if q == 0:
                        wait(pe, S["proj_lo"], proj_to(i, u, 1))
                    if q == HT:
                        wait(pe, S["proj_lo"], proj_to(i, u, 3))
                    dst = s_tiles[q % 2]
                    c = slice(q % HT * P, (q % HT + 1) * P)
                    rows = cut(q_half[q // HT], slice(None), c)
                    w = min((q + 1) * P, HALF)
                    last = product(dst[:, 0:w], rows, cut(k_first[u % 2], slice(None), slice(0, w)), True, True)
                    if q >= HT:
                        w = (q + 1 - HT) * P
                        last = product(dst[:, HALF:HALF + w], rows, cut(k_second, slice(None), slice(0, w)), True, True)
                    last.then_inc(S["scores"], 1)

                def project(bank, i, u, k):
                    kind, half, _ = proj_target(u, k)
                    b, head = divmod(u, 2)
                    wait(pe, S["w_split"], wsplit_to(i - 1, 3))
                    cols = slice(b * SEQ + half * HALF, b * SEQ + (half + 1) * HALF)
                    for c in range(KC):
                        last = product(bank[:, :], cut(w_qkv, slice(None), kind, c, slice(head * DH, (head + 1) * DH)),
                                       [h_hi[:, c, cols], h_lo[:, c, cols]], c == 0, c == KC - 1)
                    last.then_inc(S["proj_psum"], 1)

                def values(bank, i, b, k):
                    wait(pe, S["w_split"], 3 if isinstance(i, int) and i == 0 else wsplit_to(i - 1, 1))
                    for n in range(2):
                        t = b * QT + 2 * k + n
                        for c in range(KC):
                            last = product(bank[:, n * DM:(n + 1) * DM],
                                           [h_hi[:, c, t * P:(t + 1) * P], h_lo[:, c, t * P:(t + 1) * P]],
                                           cut(w_qkv, slice(None), 2, c, slice(None)), c == 0, c == KC - 1)
                    last.then_inc(S["v_psum"], 1)

                def out_project(bank, i, b, k):
                    wait(pe, S["w_split"], wsplit_to(i, 0))
                    wait(pe, S["z_lo"], z_to(i, 2 * b + 1, k // 2))
                    for n in range(2):
                        t = slice((2 * k + n) * P, (2 * k + n + 1) * P)
                        for h in range(2):
                            last = product(bank[:, n * DM:(n + 1) * DM], cut(z[h], slice(None), t),
                                           cut(w_o, slice(None), h, slice(None)), h == 0, h == 1)
                    last.then_inc(S["wo_psum"], 1)

                def transpose(i, u, q):
                    wait(pe, S["normed"], tiles_to(i, u, q))
                    for n, (k0, count) in enumerate(GROUPS[q]):
                        m = FIRST_GROUP[q] + n
                        bank = t_bank[m % 2]
                        wait(pe, S["pT_lo"], UNITS * NG * i + NG * u + m - 1)
                        for j in range(count):
                            last = nc.tensor.transpose(bank[:, j * P:(j + 1) * P], probs[q % SLOTS][:, (k0 + j) * P:(k0 + j + 1) * P], ident[:, :])
                        last.then_inc(S["transposed"], 1)

                def attend_values(bank, i, u, c):
                    b, head = divmod(u, 2)
                    wait(pe, S["pT_lo"], groups_to(i, u, HT * c + HT - 1))
                    if c == 0:
                        wait(pe, S["v_lo"], v_to(i, b, 3))
                    blocks = HT * (c + 1)
                    for k in range(blocks):
                        q0 = max(0, k - HT * c) * P
                        last = product(bank[:, q0:HALF], cut(vals[b], slice(None), k, slice(head * DH, (head + 1) * DH)),
                                       cut(pT[c], slice(None), k, slice(q0, HALF)), k == 0, k == blocks - 1)
                    last.then_inc(S["z_psum"], 1)

                MAKE = {"proj": project, "v": values, "wo": out_project, "z": attend_values}

                def pair(i, first, last):
                    for u, q, pieces, ahead, _ in schedule(first, last):
                        if ahead:
                            score(*after(i, u, q, AHEAD))
                        for n, what, k in pieces:
                            bank_free(pe, i, u, n, first, last)
                            MAKE[what](p_bank[n % 2], *target(i, u, what, k), k)
                        transpose(i, u, q)

                for k in range(4):
                    if k >= 2:
                        pe.wait_ge(S["proj_lo"], k - 1)
                    kind, half, _ = proj_target(0, k)
                    pe.wait_ge(S["w_split"], 2)
                    for c in range(KC):
                        cols = slice(half * HALF, (half + 1) * HALF)
                        last = product(p_bank[k % 2][:, :], cut(w_qkv, slice(None), kind, c, slice(0, DH)),
                                       [h_hi[:, c, cols], h_lo[:, c, cols]], c == 0, c == KC - 1)
                    last.then_inc(S["proj_psum"], 1)
                for q in range(AHEAD):
                    score(0, 0, q)
                for k in range(4):
                    if k >= 2:
                        pe.wait_ge(S["v_lo"], k - 1)
                    else:
                        pe.wait_ge(S["proj_lo"], 3 + k)
                    values(p_bank[k % 2], 0, 0, k)
                pair(0, True, False)
                with pe.Fori(1, PAIRS - 1) as i:
                    pair(i, False, False)
                pair(PAIRS - 1, False, True)
                pe.wait_ge(S["proj_lo"], proj_to(PAIRS - 1, UNITS - 1, 3))
                attend_values(p_bank[0], PAIRS - 1, UNITS - 1, 1)
                for k in range(4):
                    if k < 2:
                        pe.wait_ge(S["z_lo"], z_to(PAIRS - 1, UNITS - 1, k))
                    else:
                        pe.wait_ge(S["wo_added"], wo_to(PAIRS - 1, 1, k - 2))
                    out_project(p_bank[(k + 1) % 2], PAIRS - 1, 1, k)

            @block.scalar
            def _(act):
                act_spare = (S["mask_ready"], [act.alloc_register(f"act_until_{n}") for n in range(2)])
                def exponential(i, u, q):
                    s = q % SLOTS
                    w = (q + 1) * P
                    wait(act, S["max_ready"], tiles_to(i, u, q))
                    bi, bu, bq = after(i, u, q, -SLOTS)
                    wait(act, S["transposed"], groups_to(bi, bu, bq))
                    nc.scalar.activation(probs[s][:, 0:w], s_tiles[q % 2][:, 0:w], ACT.Exp, bias=neg_max[:, s:s + 1],
                                         scale=SCALE, accum_out=row_sum[:, s:s + 1]).then_inc(S["exp_done"], 1)

                def hi_projection(bank, i, u, k):
                    kind, _, dst = proj_target(u, k)
                    wait_apart(act, act_spare, (S["proj_psum"], proj_to(i, u, k)),
                               (S["scores"], [tiles_to(i, u - 1, HT - 1), tiles_to(i, u - 2, QT - 1),
                                              tiles_to(i, u - 1, QT - 1), tiles_to(i, u - 1, QT - 1)][k]))
                    nc.scalar.activation(dst[0][:, :], bank[:, :], ACT.Identity,
                                         bias=bias_of(kind, i, u % 2)).then_inc(S["proj_hi"], 1)

                def hi_values(bank, i, b, k):
                    wait(act, S["v_psum"], v_to(i, b, k))
                    wait(act, S["z_psum"], z_to(i - 1, 2 * b + 1, 1))
                    nc.scalar.activation(vals[b][0][:, 2 * k:2 * k + 2, :].rearrange("p t n -> p (t n)"), bank[:, :],
                                         ACT.Copy).then_inc(S["v_hi"], 1)

                def hi_transposed(i, u, q):
                    c, ql = divmod(q, HT)
                    if ql == 0:
                        bi, bu = (i, u - 1) if u else (i - 1, UNITS - 1)
                        wait(act, S["z_psum"], z_to(bi, bu, c))
                    for n, (k0, count) in enumerate(GROUPS[q]):
                        m = FIRST_GROUP[q] + n
                        wait(act, S["transposed"], UNITS * NG * i + NG * u + m + 1)
                        nc.scalar.activation(pT[c][0][:, k0:k0 + count, ql * P:(ql + 1) * P],
                                             t_bank[m % 2][:, 0:count * P].rearrange("p (k n) -> p k n", n=P), ACT.Copy).then_inc(S["pT_hi"], 1)

                def hi_z(bank, i, u, c):
                    b, head = divmod(u, 2)
                    wait_apart(act, act_spare, (S["z_psum"], z_to(i, u, c)), (S["wo_psum"], wo_to(i, b - 1, 2 * c + 1)))
                    nc.scalar.activation(z[head][0][:, c * HALF:(c + 1) * HALF], bank[:, :], ACT.Identity,
                                         bias=bias_of(2, i, head)).then_inc(S["z_hi"], 1)

                TAKE = {"proj": hi_projection, "v": hi_values, "z": hi_z}

                def pair(i, first, last):
                    for u, q, pieces, _, more in schedule(first, last):
                        if more:
                            exponential(*after(i, u, q, 1))
                        for n, what, k in pieces:
                            if what in TAKE:
                                TAKE[what](p_bank[n % 2], *target(i, u, what, k), k)
                        hi_transposed(i, u, q)

                for k in range(4):
                    hi_projection(p_bank[k % 2], 0, 0, k)
                exponential(0, 0, 0)
                for k in range(4):
                    hi_values(p_bank[k % 2], 0, 0, k)
                pair(0, True, False)
                with act.Fori(1, PAIRS - 1) as i:
                    pair(i, False, False)
                pair(PAIRS - 1, False, True)
                hi_z(p_bank[0], PAIRS - 1, UNITS - 1, 1)

            @block.vector
            def _(dve):
                dve_spare = (S["mask_ready"], [dve.alloc_register(f"dve_until_{n}") for n in range(2)])
                v = nc.vector

                def maximum(i, u, q):
                    s = q % SLOTS
                    t = s_tiles[q % 2]
                    n = tiles_to(i, u, q)
                    wait_apart(dve, dve_spare, (S["scores"], n))
                    diag = t[:, q * P:(q + 1) * P]
                    v.tensor_tensor_reduce(out=diag, in0=diag, in1=mask[:, :], scale=1.0, scalar=-3e38, op0=ALU.add,
                                           op1=ALU.max, accum_out=m_diag[:, s:s + 1]).then_inc(S["partial_max"], 1)
                    v.tensor_reduce(out=m_rest[:, s:s + 1], in_=t[:, 0:max(q, 1) * P], axis=AX.X, op=ALU.max).then_inc(S["partial_max"], 1) if q else None
                    wait(dve, S["partial_max"], (2 * QT - 1) * UNITS * i + (2 * QT - 1) * u + 2 * q + 1)
                    other = m_rest if q else m_diag
                    v.tensor_scalar(neg_max[:, s:s + 1], m_diag[:, s:s + 1], other[:, s:s + 1], -SCALE,
                                    ALU.max, ALU.mult).then_inc(S["max_ready"], 1)

                def invert(i, u, q):
                    s = q % SLOTS
                    wait(dve, S["exp_done"], tiles_to(i, u, q))
                    v.reciprocal(inv_sum[:, s:s + 1], row_sum[:, s:s + 1]).then_inc(S["inv_ready"], 1)

                def lo_projection(bank, i, u, k):
                    kind, _, dst = proj_target(u, k)
                    wait(dve, S["proj_hi"], proj_to(i, u, k))
                    v.scalar_tensor_tensor(out=dst[1][:, :], in0=bank[:, :], scalar=bias_of(kind, i, u % 2),
                                           in1=dst[0][:, :].bitcast(F32), op0=ALU.add, op1=ALU.subtract).then_inc(S["proj_lo"], 1)

                def lo_values(bank, i, b, k):
                    hi, lo = [x[:, 2 * k:2 * k + 2, :].rearrange("p t n -> p (t n)") for x in vals[b]]
                    wait(dve, S["v_hi"], v_to(i, b, k))
                    v.tensor_tensor(lo, bank[:, :], hi.bitcast(F32), ALU.subtract).then_inc(S["v_lo"], 1)

                def add_projected(bank, i, b, k):
                    t = b * QT + 2 * k
                    dst = acc[:, t:t + 2, :].rearrange("p t n -> p (t n)")
                    wait(dve, S["wo_psum"], wo_to(i, b, k))
                    v.tensor_tensor(dst, bank[:, :], dst, ALU.add).then_inc(S["wo_added"], 1)

                def lo_transposed(i, u, q):
                    c, ql = divmod(q, HT)
                    for n, (k0, count) in enumerate(GROUPS[q]):
                        m = FIRST_GROUP[q] + n
                        hi, lo = [x[:, k0:k0 + count, ql * P:(ql + 1) * P] for x in pT[c]]
                        wait(dve, S["pT_hi"], UNITS * NG * i + NG * u + m + 1)
                        v.tensor_tensor(lo, t_bank[m % 2][:, 0:count * P].rearrange("p (k n) -> p k n", n=P), hi.bitcast(F32),
                                        ALU.subtract).then_inc(S["pT_lo"], 1)

                def lo_z(bank, i, u, c):
                    head = u % 2
                    hi, lo = [x[:, c * HALF:(c + 1) * HALF] for x in z[head]]
                    wait(dve, S["z_hi"], z_to(i, u, c))
                    v.scalar_tensor_tensor(out=lo, in0=bank[:, :], scalar=bias_of(2, i, head), in1=hi.bitcast(F32),
                                           op0=ALU.add, op1=ALU.subtract).then_inc(S["z_lo"], 1)

                TAKE = {"proj": lo_projection, "v": lo_values, "wo": add_projected, "z": lo_z}

                def pair(i, first, last):
                    for u, q, pieces, ahead, more in schedule(first, last):
                        if ahead:
                            maximum(*after(i, u, q, AHEAD))
                        if more:
                            invert(*after(i, u, q, 1))
                        for n, what, k in pieces:
                            TAKE[what](p_bank[n % 2], *target(i, u, what, k), k)
                        lo_transposed(i, u, q)

                dve.wait_ge(S["mask_ready"], 1)
                for k in range(4):
                    lo_projection(p_bank[k % 2], 0, 0, k)
                for q in range(AHEAD):
                    maximum(0, 0, q)
                invert(0, 0, 0)
                for k in range(4):
                    lo_values(p_bank[k % 2], 0, 0, k)
                pair(0, True, False)
                with dve.Fori(1, PAIRS - 1) as i:
                    pair(i, False, False)
                pair(PAIRS - 1, False, True)
                lo_z(p_bank[0], PAIRS - 1, UNITS - 1, 1)
                for k in range(4):
                    add_projected(p_bank[(k + 1) % 2], PAIRS - 1, 1, k)


def experts(nc, sb, sem, g):
    ident, acc, h_hi, h_lo = (g[n] for n in ("ident", "acc", "h_hi", "h_lo"))
    s_tiles, t_bank, p_bank = (g[n] for n in ("s_tiles", "t_bank", "p_bank"))
    z_bank, fill_bank = p_bank
    GD = CT * DM
    with ExitStack() as scope:
        def sbl(name, shape, dt=F32):
            return sb(name, shape, dt, scope)

        def split(name, shape):
            return [sbl(f"{name}_hi", shape, F32R), sbl(f"{name}_lo", shape, F32R)]

        x_sb = sbl("x_sb", [P, TILES, DM])
        condT = sbl("condT2", [P, KC, BATCH])
        cexp = sbl("cexp2", [P, KC, BATCH])
        csilu = sbl("csilu2", [P, KC, BATCH, P])
        wm = sbl("wm2", [P, KC, 4 * DM])
        mods = sbl("mods", [P, 4, BATCH, DM])
        bo = sbl("bo", [P, DM])
        clamp = sbl("clamp", [P, BATCH * DM])
        sign = sbl("sign", [P, BATCH * DM])
        rank = sbl("rank", [P, CT, NE])
        raw_w = sbl("raw_w", [P, KC * NE * RANK])
        raw_r = sbl("raw_r", [P, KC, NE])
        w_a = split("w_a", [P, KC * NE * RANK])
        w_b = split("w_b", [P, NE * DM])
        w_r = split("w_r", [P, KC, P])
        stats = sbl("stats2", [P, CT, 6])
        mv = sbl("mv2", [P, CT, 2])
        var = sbl("var2", [P, CT, 2])
        root = sbl("root", [P, CT, 2])
        scratch = sbl("scratch2", [P, CT, 2])
        power = sbl("power2", [P, CT])
        hn = sbl("hn", [P, CT, DM])
        square = sbl("square", [P, DM])
        logitT = sbl("logitT", [P, CHUNK])
        lg, eq, s1, lg2, s2, ex = (sbl(n, [P, CT, NE]) for n in ("lg", "eq", "s1", "lg2", "s2", "ex"))
        m1, m2, pos, den = (sbl(n, [P, CT]) for n in ("m1", "m2", "pos", "den"))
        comb = sbl("comb", [P, TILES, NE])
        upT = [split(f"up{i}", [P, CHUNK]) for i in range(2)]
        res = sbl("res", [P, CT, DM])

        names = ("xr_in", "c2_in", "wm2_in", "bo_in", "router_in", "wa_in", "wb_in", "pow2", "chain2", "c2_exp", "mods_psum",
                 "consts", "wa_hi", "e_split", "router_split", "x_gated", "res_ready", "var2_ready", "guess2", "xn2_ready", "h2_mul", "h2_ready",
                 "squared", "norm2_ready", "h2_T", "h2_hi", "h2_lo", "logit_psum", "logit_sb", "logit_T", "ex_in", "ex_ready",
                 "comb_ready", "up_psum", "up_hi", "up_lo", "down_psum", "mixed", "gated", "stored", "pool_chain")
        S = {n: sem(n) for n in names}

        with nc.Block() as block:
            @block.sync
            def _(sp):
                sp.dma_start(condT[:, :, :], g["cond"]).then_inc(S["c2_in"], 16)
                sp.dma_start(wm[:, :, :], g["wmod"].rearrange("(c p) n -> p c n", p=P)[:, :, 2 * DM:]).then_inc(S["wm2_in"], 16)
                sp.dma_start(bo[:, :], g["b_o"].broadcast_to([P, DM])).then_inc(S["bo_in"], 16)
                sp.dma_start(x_sb[:, :, :], g["x"].rearrange("b (t p) d -> p (b t) d", p=P)).then_inc(S["xr_in"], 16)
                sp.dma_start(raw_r[:, :, :], g["router_w"].rearrange("(c p) n -> p c n", p=P)).then_inc(S["router_in"], 16)
                sp.dma_start(raw_w[:, :], g["wa"]).then_inc(S["wa_in"], 16)
                sp.wait_ge(S["e_split"], 1)
                sp.dma_start(raw_w[:, :], g["wb"]).then_inc(S["wb_in"], 16)
                ov = g["out"].rearrange("b (t p) d -> p (b t) d", p=P)
                with sp.Fori(0, CHUNKS) as n:
                    sp.wait_ge(S["gated"], n + 1)
                    sp.dma_start(ov[:, bass.ds(CT * n, CT), :], x_sb[:, bass.ds(CT * n, CT), :]).then_inc(S["stored"], 16)
                sp.wait_ge(S["stored"], 16 * CHUNKS)

            @block.gpsimd
            def _(pool):
                pool_spare = (S["router_in"], [pool.alloc_register("pool_then")])
                count = [0]

                def link(ins):
                    count[0] += 1
                    ins.then_inc(S["pool_chain"], 1)
                    pool.wait_ge(S["pool_chain"], count[0])

                for j in range(CT):
                    pool.memset(power[:, j:j + 1], -0.5)
                for w in w_r:
                    pool.memset(w[:, :, :].bitcast(F32), 0.0)
                for e in range(NE):
                    last = pool.memset(rank[:, :, e:e + 1], float(NE - e))
                link(last)
                pool.wait_ge(S["router_in"], 16)
                link(pool.tensor_copy(w_r[0][:, :, 0:NE], raw_r[:, :, :]))
                pool.tensor_tensor(w_r[1][:, :, 0:NE], raw_r[:, :, :], w_r[0][:, :, 0:NE].bitcast(F32), ALU.subtract).then_inc(S["router_split"], 1)

                with pool.Fori(0, CHUNKS // 2) as b:
                    for half in range(2):
                        n = 2 * b + half
                        wait_apart(pool, pool_spare, (S["x_gated"], n + 1))
                        t = bass.ds(CT * n, CT)
                        pool.tensor_tensor(x_sb[:, t, :], x_sb[:, t, :], acc[:, t, :], ALU.add).then_inc(S["res_ready"], 1)
                        pool.wait_ge(S["var2_ready"], 2 * n + 1)
                        pool.tensor_tensor(root[:, :, 0], var[:, :, 0], power[:, :], ALU.pow).then_inc(S["guess2"], 1)
                        wait_apart(pool, pool_spare, (S["xn2_ready"], n + 1))
                        pool.tensor_tensor(hn[:, :, :], hn[:, :, :], mods[:, 2, bass.ds(b, 1), :].broadcast_to([P, CT, DM]), ALU.mult).then_inc(S["h2_mul"], 1)
                        wait_apart(pool, pool_spare, (S["h2_mul"], n + 1))
                        pool.tensor_tensor(hn[:, :, :], hn[:, :, :], mods[:, 1, bass.ds(b, 1), :].broadcast_to([P, CT, DM]), ALU.add).then_inc(S["h2_ready"], 1)
                        pool.wait_ge(S["var2_ready"], 2 * n + 2)
                        pool.tensor_tensor(root[:, :, 1], var[:, :, 1], power[:, :], ALU.pow).then_inc(S["guess2"], 1)

            @block.scalar
            def _(act):
                act_spare = (S["wa_in"], [act.alloc_register("act_then")])
                act.wait_ge(S["c2_in"], 16)
                nc.scalar.activation(cexp[:, :, :], condT[:, :, :], ACT.Exp, scale=-1.0).then_inc(S["c2_exp"], 1)
                act.wait_ge(S["wa_in"], 16)
                nc.scalar.activation(w_a[0][:, :], raw_w[:, :], ACT.Copy).then_inc(S["wa_hi"], 1)
                act.wait_ge(S["wb_in"], 16)
                nc.scalar.activation(w_b[0][:, :], raw_w[:, :], ACT.Copy).then_inc(S["wa_hi"], 1)
                with act.Fori(0, CHUNKS) as n:
                    act.wait_ge(S["h2_ready"], n + 1)
                    for t in range(CT):
                        if t:
                            act.wait_ge(S["squared"], CT * n + t)
                        else:
                            act.wait_ge(S["guess2"], 2 * n + 1)
                        nc.scalar.activation(square[:, :], hn[:, t, :], ACT.Square, accum_out=var[:, t, 1:2]).then_inc(S["squared"], 1)
                    act.wait_ge(S["squared"], CT * n + CT)
                    for c in range(KC):
                        wait_apart(act, act_spare, (S["h2_T"], KC * n + c + 1))
                        nc.scalar.activation(h_hi[:, c, bass.ds(CHUNK * n, CHUNK)], t_bank[c][:, :], ACT.Copy).then_inc(S["h2_hi"], 1)
                    act.wait_ge(S["logit_psum"], n + 1)
                    nc.scalar.activation(logitT[:, :], fill_bank[:, :], ACT.Copy).then_inc(S["logit_sb"], 1)
                    act.wait_ge(S["ex_in"], n + 1)
                    nc.scalar.activation(ex[:, :, :], ex[:, :, :], ACT.Exp).then_inc(S["ex_ready"], 1)
                with act.Fori(0, CHUNKS) as n:
                    for e in range(NE):
                        act.wait_ge(S["up_psum"], NE * n + e + 1)
                        nc.scalar.activation(upT[e % 2][0][:, :], [z_bank, fill_bank][e % 2][:, :], ACT.Copy).then_inc(S["up_hi"], 1)

            @block.tensor
            def _(pe):
                mm = nc.tensor.matmul

                def product(dst, a, b, start, stop):
                    mm(dst, a[0], b[0], start=start, stop=False)
                    mm(dst, a[0], b[1], start=False, stop=False)
                    return mm(dst, a[1], b[0], start=False, stop=stop)

                pe.wait_ge(S["chain2"], 3)
                pe.wait_ge(S["wm2_in"], 16)
                for k in range(4):
                    for b in range(BATCH):
                        for c in range(KC):
                            last = mm(s_tiles[k // 2][:, (k % 2) * HALF + b * DM:(k % 2) * HALF + (b + 1) * DM], csilu[:, c, b, :],
                                      wm[:, c, k * DM:(k + 1) * DM], start=(c == 0), stop=(c == KC - 1))
                last.then_inc(S["mods_psum"], 1)
                pe.wait_ge(S["router_split"], 1)
                with pe.Fori(0, CHUNKS) as n:
                    pe.wait_ge(S["h2_ready"], n + 1)
                    for c in range(KC):
                        for t in range(CT):
                            last = nc.tensor.transpose(t_bank[c][:, t * P:(t + 1) * P], hn[:, t, c * P:(c + 1) * P], ident[:, :])
                        last.then_inc(S["h2_T"], 1)
                    pe.wait_ge(S["h2_lo"], KC * n + KC)
                    cols = bass.ds(CHUNK * n, CHUNK)
                    for c in range(KC):
                        last = product(fill_bank[:, :], [w[:, c, :] for w in w_r], [h_hi[:, c, cols], h_lo[:, c, cols]], c == 0, c == KC - 1)
                    last.then_inc(S["logit_psum"], 1)
                    pe.wait_ge(S["logit_sb"], n + 1)
                    for t in range(CT):
                        last = nc.tensor.transpose(z_bank[:, t * P:(t + 1) * P], logitT[:, t * P:(t + 1) * P], ident[:, :])
                    last.then_inc(S["logit_T"], 1)
                    pe.wait_ge(S["comb_ready"], n + 1)

                pe.wait_ge(S["e_split"], 2)
                with pe.Fori(0, CHUNKS) as n:
                    cols = bass.ds(CHUNK * n, CHUNK)

                    def up(e, first):
                        if not first:
                            pe.wait_ge(S["up_lo"], NE * n + e - 1)
                        for c in range(KC):
                            w = [x[:, (c * NE + e) * RANK:(c * NE + e + 1) * RANK] for x in w_a]
                            last = product([z_bank, fill_bank][e % 2][:, :], w, [h_hi[:, c, cols], h_lo[:, c, cols]], c == 0, c == KC - 1)
                        last.then_inc(S["up_psum"], 1)

                    def down(e):
                        pe.wait_ge(S["up_lo"], NE * n + e + 1)
                        if e >= 2:
                            pe.wait_ge(S["mixed"], CT * (NE * n + e - 1))
                        for t in range(CT):
                            last = product(s_tiles[e % 2][:, t * DM:(t + 1) * DM], [x[:, t * P:(t + 1) * P] for x in upT[e % 2]],
                                           [x[:, e * DM:(e + 1) * DM] for x in w_b], True, True)
                            if t % 2:
                                last.then_inc(S["down_psum"], 1)

                    up(0, True)
                    for e in range(NE):
                        if e + 1 < NE:
                            up(e + 1, e == 0)
                        down(e)
                    pe.wait_ge(S["mixed"], CT * NE * n + CT * NE)

            @block.vector
            def _(dve):
                dve_spare = (S["bo_in"], [dve.alloc_register("dve_then")])
                v = nc.vector
                count = [0]

                def link(ins):
                    count[0] += 1
                    ins.then_inc(S["chain2"], 1)
                    dve.wait_ge(S["chain2"], count[0])

                dve.wait_ge(S["c2_exp"], 1)
                link(v.tensor_scalar_add(cexp[:, :, :], cexp[:, :, :], 1.0))
                link(v.reciprocal(cexp[:, :, :], cexp[:, :, :]))
                link(v.tensor_tensor(csilu[:, :, :, :], condT[:, :, :].unsqueeze(3).broadcast_to([P, KC, BATCH, P]),
                                     cexp[:, :, :].unsqueeze(3).broadcast_to([P, KC, BATCH, P]), ALU.mult))
                dve.wait_ge(S["mods_psum"], 1)
                for k, bank in ((0, s_tiles[0][:, 0:HALF]), (3, s_tiles[1][:, HALF:])):
                    link(v.tensor_scalar(clamp[:, :], bank, -1.0, None, ALU.mult))
                    link(v.tensor_tensor(clamp[:, :], clamp[:, :], bank, ALU.max))
                    link(v.tensor_scalar(clamp[:, :], clamp[:, :], 0.25, None, ALU.max))
                    link(v.tensor_scalar(sign[:, :], bank, 0.0, None, ALU.is_ge))
                    link(v.tensor_scalar(sign[:, :], sign[:, :], 2.0, -1.0, ALU.mult, ALU.add))
                    link(v.tensor_tensor(mods[:, k, :, :].rearrange("p b n -> p (b n)"), clamp[:, :], sign[:, :], ALU.mult))
                link(v.tensor_copy(mods[:, 1, :, :].rearrange("p b n -> p (b n)"), s_tiles[0][:, HALF:]))
                link(v.tensor_scalar_add(mods[:, 2, :, :].rearrange("p b n -> p (b n)"), s_tiles[1][:, 0:HALF], 1.0))
                dve.wait_ge(S["wa_hi"], 1)
                v.tensor_tensor(w_a[1][:, :], raw_w[:, :], w_a[0][:, :].bitcast(F32), ALU.subtract).then_inc(S["e_split"], 1)
                dve.wait_ge(S["wa_hi"], 2)
                v.tensor_tensor(w_b[1][:, :], raw_w[:, :], w_b[0][:, :].bitcast(F32), ALU.subtract).then_inc(S["e_split"], 1)
                dve.wait_ge(S["bo_in"], 16)
                dve.wait_ge(S["xr_in"], 16)
                setup = count[0]
                LINKS = 27
                with dve.Fori(0, CHUNKS // 2) as b:
                    for half in range(2):
                        n = 2 * b + half
                        made = [0]

                        def step(ins):
                            made[0] += 1
                            ins.then_inc(S["chain2"], 1)
                            dve.wait_ge(S["chain2"], LINKS * n + setup + made[0])

                        t = bass.ds(CT * n, CT)
                        step(v.tensor_tensor(acc[:, t, :], acc[:, t, :], bo[:, :].unsqueeze(1).broadcast_to([P, CT, DM]), ALU.add))
                        v.tensor_tensor(acc[:, t, :], acc[:, t, :], mods[:, 0, bass.ds(b, 1), :].broadcast_to([P, CT, DM]),
                                        ALU.mult).then_inc(S["x_gated"], 1)
                        dve.wait_ge(S["res_ready"], n + 1)
                        for j in range(CT):
                            last = v.bn_stats(stats[:, j, :], x_sb[:, bass.ds(CT * n + j, 1), :].rearrange("p o d -> p (o d)"))
                        made[0] += 1
                        last.then_inc(S["chain2"], 1)
                        wait_apart(dve, dve_spare, (S["chain2"], LINKS * n + setup + made[0]))
                        for j in range(CT):
                            last = v.bn_aggr(mv[:, j, :], stats[:, j, :])
                        step(last)
                        v.tensor_scalar_add(var[:, :, 0], mv[:, :, 1], EPS).then_inc(S["var2_ready"], 1)
                        dve.wait_ge(S["guess2"], 2 * n + 1)
                        rsqrt_newton(v, step, root[:, :, 0], var[:, :, 0], scratch[:, :, 0])
                        for j in range(CT):
                            last = v.tensor_scalar(hn[:, j, :], x_sb[:, bass.ds(CT * n + j, 1), :].rearrange("p o d -> p (o d)"),
                                                   mv[:, j, 0:1], root[:, j, 0:1], ALU.subtract, ALU.mult)
                        last.then_inc(S["xn2_ready"], 1)
                        for c in range(KC):
                            dve.wait_ge(S["h2_hi"], KC * n + c + 1)
                            cols = bass.ds(CHUNK * n, CHUNK)
                            v.tensor_tensor(h_lo[:, c, cols], t_bank[c][:, :], h_hi[:, c, cols].bitcast(F32), ALU.subtract).then_inc(S["h2_lo"], 1)
                        dve.wait_ge(S["squared"], CT * n + CT)
                        v.tensor_scalar_max(var[:, :, 1], var[:, :, 1], 1e-24).then_inc(S["var2_ready"], 1)
                        dve.wait_ge(S["guess2"], 2 * n + 2)
                        rsqrt_newton(v, step, root[:, :, 1], var[:, :, 1], scratch[:, :, 1])
                        wide = [P, CT, NE]
                        dve.wait_ge(S["logit_T"], n + 1)
                        zl = z_bank[:, :].rearrange("p (t n) -> p t n", n=P)[:, :, 0:NE]
                        step(v.tensor_tensor(lg[:, :, :], zl, root[:, :, 1:2].broadcast_to(wide), ALU.mult))
                        step(v.tensor_reduce(out=m1[:, :], in_=lg[:, :, :], axis=AX.X, op=ALU.max))
                        v.tensor_tensor(ex[:, :, :], lg[:, :, :], m1[:, :].unsqueeze(2).broadcast_to(wide), ALU.subtract).then_inc(S["ex_in"], 1)

                        def pick(src, best, sel):
                            step(v.tensor_tensor(eq[:, :, :], src[:, :, :], best[:, :].unsqueeze(2).broadcast_to(wide), ALU.is_equal))
                            step(v.tensor_tensor(eq[:, :, :], eq[:, :, :], rank[:, :, :], ALU.mult))
                            step(v.tensor_reduce(out=pos[:, :], in_=eq[:, :, :], axis=AX.X, op=ALU.max))
                            step(v.tensor_tensor(sel[:, :, :], eq[:, :, :], pos[:, :].unsqueeze(2).broadcast_to(wide), ALU.is_equal))

                        pick(lg, m1, s1)
                        step(v.scalar_tensor_tensor(out=lg2[:, :, :], in0=s1[:, :, :], scalar=MASKED, in1=lg[:, :, :], op0=ALU.mult, op1=ALU.add))
                        step(v.tensor_reduce(out=m2[:, :], in_=lg2[:, :, :], axis=AX.X, op=ALU.max))
                        pick(lg2, m2, s2)
                        step(v.tensor_tensor(s1[:, :, :], s1[:, :, :], s2[:, :, :], ALU.add))
                        dve.wait_ge(S["ex_ready"], n + 1)
                        step(v.tensor_tensor(s2[:, :, :], s1[:, :, :], ex[:, :, :], ALU.mult))
                        step(v.tensor_reduce(out=den[:, :], in_=s2[:, :, :], axis=AX.X, op=ALU.add))
                        step(v.reciprocal(den[:, :], den[:, :]))
                        v.tensor_tensor(comb[:, t, :], s2[:, :, :], den[:, :].unsqueeze(2).broadcast_to(wide), ALU.mult).then_inc(S["comb_ready"], 1)
                        dve.wait_ge(S["comb_ready"], n + 1)
                        assert made[0] == LINKS, made
                with dve.Fori(0, CHUNKS) as n:
                    for e in range(NE):
                        hi, lo = upT[e % 2]
                        dve.wait_ge(S["up_hi"], NE * n + e + 1)
                        v.tensor_tensor(lo[:, :], [z_bank, fill_bank][e % 2][:, :], hi[:, :].bitcast(F32), ALU.subtract).then_inc(S["up_lo"], 1)
                        for t in range(CT):
                            k = CT * (NE * n + e) + t
                            if t % 2 == 0:
                                dve.wait_ge(S["down_psum"], CT // 2 * (NE * n + e) + t // 2 + 1)
                            y = s_tiles[e % 2][:, t * DM:(t + 1) * DM]
                            weight = comb[:, bass.ds(CT * n + t, 1), e:e + 1].rearrange("p o e -> p (o e)")
                            if e == 0:
                                v.tensor_scalar(res[:, t, :], y, weight, None, ALU.mult).then_inc(S["mixed"], 1)
                            else:
                                dve.wait_ge(S["mixed"], k + 1 - CT)
                                v.scalar_tensor_tensor(out=res[:, t, :], in0=y, scalar=weight, in1=res[:, t, :],
                                                       op0=ALU.mult, op1=ALU.add).then_inc(S["mixed"], 1)
                    b = n // 2
                    dve.wait_ge(S["mixed"], CT * NE * n + CT * NE)
                    t = bass.ds(CT * n, CT)
                    v.tensor_tensor(res[:, :, :], res[:, :, :], mods[:, 3, bass.ds(b, 1), :].broadcast_to([P, CT, DM]), ALU.mult).then_inc(S["pow2"], 1)
                    dve.wait_ge(S["pow2"], n + 1)
                    v.tensor_tensor(x_sb[:, t, :], x_sb[:, t, :], res[:, :, :], ALU.add).then_inc(S["gated"], 1)
                    dve.wait_ge(S["gated"], n + 1)


_OUT = ((BATCH, SEQ, DM), "float32")


def kernel(**inputs):
    import numpy as _np
    import concourse.bacc as _bacc
    from concourse import mybir as _mybir
    from concourse.bass_utils import run_bass_kernel_spmd as _run

    a = {k.replace("L0_", "").replace("attn_", "").replace("ffn_", ""): _np.asarray(v) for k, v in inputs.items()}

    def by_pair(w):
        w = w.reshape(PAIRS, 2, KC, P, DH).transpose(0, 3, 2, 1, 4)
        return w.reshape(PAIRS, P, KC * 2 * DH)

    arrays = {
        "x": a["x"],
        "wqkv": _np.stack([by_pair(a["W_Q"]), by_pair(a["W_K"]), by_pair(a["W_V"])], axis=2),
        "wo": a["W_O"].reshape(PAIRS, 2, DH, DM).transpose(0, 2, 1, 3).reshape(PAIRS, DH, 2 * DM),
        "bias": _np.stack([a["b_Q"].T, a["b_K"].T, a["b_V"].T], axis=1),
        "b_o": a["b_O"].reshape(1, DM),
        "router_w": a["router_w"],
        "wa": a["Wa"].reshape(NE, KC, P, RANK).transpose(2, 1, 0, 3).reshape(P, KC * NE * RANK),
        "wb": a["Wb"].transpose(1, 0, 2).reshape(RANK, NE * DM),
        "cond": a["c"].reshape(BATCH, KC, P).transpose(2, 1, 0),
        "wmod": a["wmod"],
    }
    nc = _bacc.Bacc("TRN2", target_bir_lowering=False, num_devices=1)
    maps, args = {}, []
    for name, v in arrays.items():
        v = _np.ascontiguousarray(v)
        maps[f"in_{name}"] = v
        args.append(nc.dram_tensor(f"in_{name}", v.shape, _mybir.dt.from_np(v.dtype), kind="ExternalInput").ap())
    shape, dtype = _OUT
    args.append(nc.dram_tensor("out_0", shape, _mybir.dt.from_np(_np.dtype(dtype)), kind="ExternalOutput").ap())
    adaln_block(nc, *args)
    r = _run(nc, [maps], core_ids=[0])
    return r.results[0]["out_0"]
```

```python
from contextlib import ExitStack

import concourse.bass as bass
from concourse import mybir

P = 128
BATCH, SEQ, DM, NH, DH = 2, 1024, 256, 16, 128
TOK = BATCH * SEQ
KC = DM // P
TILES = TOK // P
QT = SEQ // P
HALF = SEQ // 2
HT = HALF // P
PAIRS = NH // 2
UNITS = 2 * BATCH
NE, RANK = 8, 128
FIRST = 2
LC = 16
CHUNK = 512
CHUNKS = TOK // CHUNK
CT = CHUNK // P
EPS = 1e-5
SCALE = float(DH) ** -0.5
MASKED = -1e30
RAW_QKV = 3 * KC * 2 * DH
RAW = RAW_QKV + 2 * DM

F32 = mybir.dt.float32
F32R = mybir.dt.float32r
ALU = mybir.AluOpType
ACT = mybir.ActivationFunctionType
AX = mybir.AxisListType

GROUPS = [[(0, min(q + 1, HT))] + ([(HT, q + 1 - HT)] if q >= HT else []) for q in range(QT)]
FIRST_GROUP = [sum(len(g) for g in GROUPS[:q]) for q in range(QT + 1)]
NG = FIRST_GROUP[QT]

PIECES_EVEN = [(0, "wo", 0), (1, "z", 1), (2, "wo", 1), (3, "proj", 0), (4, "proj", 1), (5, "z", 0),
               (6, "proj", 2), (6, "wo", 2), (7, "proj", 3), (7, "wo", 3)]
PIECES_ODD = [(0, "v", 0), (1, "z", 1), (2, "v", 1), (3, "proj", 0), (4, "proj", 1), (5, "z", 0),
              (6, "proj", 2), (6, "v", 2), (7, "proj", 3), (7, "v", 3)]
PIECES = [PIECES_EVEN, PIECES_ODD]
PIECES_START = [(2, "h1", 4), (3, "proj", 0), (3, "h1", 5), (4, "proj", 1), (5, "h1", 6), (5, "z", 0),
                (6, "h1", 7), (6, "proj", 2), (7, "proj", 3)]
PIECES_END = [(1, "z", 1), (2, "h2", 0), (3, "h2", 1), (4, "z", 0), (5, "router", 0),
              (6, "h2", 2), (6, "h2", 3), (7, "wo", 0), (7, "wo", 1)]

NORM1_BANKS = 2 * KC * BATCH
EARLY = KC


def norm1_bank(n):
    b, r = divmod(n, 2 * KC)
    half, c = divmod(r, KC)
    return b, half, c, slice(b * SEQ + half * HALF, b * SEQ + (half + 1) * HALF)


def pieces_of(first, last, u):
    if last and u == UNITS - 1:
        return list(enumerate(PIECES_END, start=1))
    if first and u == 0:
        return list(enumerate(PIECES_START))
    return list(enumerate(PIECES[u % 2]))


def wait(eng, sem, value):
    if isinstance(value, int) and value <= 0:
        return
    eng.wait_ge(sem, value)


def wait_apart(eng, spare, *waits):
    holds, registers = spare
    if not all(isinstance(v, int) for _, v in waits):
        for register, (_, v) in zip(registers, waits):
            eng.reg_mov(register, v)
        waits = [(sem, register) for register, (sem, _) in zip(registers, waits)]
        eng.wait_ge(holds, 1)
    for sem, v in waits:
        wait(eng, sem, v)


def adaln_block(nc, x, wqkv, wo, bias, b_o, router_w, wa, wb, cond, wmod, out):
    ctx = ExitStack()
    with ctx:
        def sb(name, shape, dt=F32, scope=ctx):
            return scope.enter_context(nc.sbuf_tensor(name, shape, dt))

        def under(name, shape):
            with nc.sbuf_tensor(name, shape, F32) as t:
                return t

        def pb(name, shape):
            return ctx.enter_context(nc.psum_tensor(name, shape, F32))

        def sem(name):
            return ctx.enter_context(nc.semaphore(name))

        ident = sb("ident", [P, P])
        mod = sb("mod", [P, 4, KC, BATCH])
        gates = sb("gates", [P, 2, BATCH, DM])
        biases = sb("biases", [P, 3, NH])
        h_hi = sb("h_hi", [P, KC, TOK], F32R)
        h_lo = sb("h_lo", [P, KC, TOK], F32R)
        acc = sb("acc", [P, TILES, DM])
        over_w = under("over_w", [P, 2, 3 * KC * 2 * DH])
        w_qkv = [sb(f"w_qkv_{n}", [P, 3, KC, 2 * DH], F32R) for n in ("hi", "lo")]
        w_a_first = [w[:, 2, :, :].rearrange("p c n -> p (c n)") for w in w_qkv]
        w_o = [sb(f"w_o_{n}", [P, 2, DM], F32R) for n in ("hi", "lo")]
        raw = sb("raw", [P, RAW])
        wa_in = sem("wa_in")
        wb_first_in = sem("wb_first_in")
        full = [over_w[:, n, 0:KC * CHUNK].rearrange("p (c n) -> p c n", c=KC) for n in range(2)]
        stats2 = sb("stats2", [P, CT, 6])
        mv2 = sb("mv2", [P, 2, CT, 2])
        var2 = sb("var2", [P, 2, CT])
        rstd2 = sb("rstd2", [P, 2, CT])
        scratch2 = sb("scratch2", [P, QT])
        power2 = sb("power2", [P, QT])
        raw_r = sb("raw_r", [P, KC, NE])
        over_v = under("over_v", [P, 2, QT, DM])
        values_first = [sb(f"v0_{n}", [P, QT, 2 * DH], F32R) for n in ("hi", "lo")]
        over_v1 = under("over_v1", [P, 2, QT, DM])
        values_second = [sb(f"v1_{n}", [P, QT, 2 * DH], F32R) for n in ("hi", "lo")]
        xn_second = over_v1[:, 0, :, :]
        full1 = [over_v1[:, 1, 2 * n:2 * n + 2, :].rearrange("p t n -> p (t n)") for n in range(2)]
        small = over_v1[:, 1, 4, :]
        stats1 = over_v1[:, 1, 5, 0:6 * QT].rearrange("p (t n) -> p t n", n=6)
        mv1 = small[:, 0:2 * QT].rearrange("p (t n) -> p t n", n=2)
        var1, rstd1, scratch1 = (small[:, QT * n:QT * (n + 1)] for n in (2, 3, 4))
        x_first, xn_first = over_v[:, 0, :, :], over_v[:, 1, :, :]
        ones = x_first[:, 3, DM - 1:DM]
        rank = x_first[:, 3, 0:QT * NE].rearrange("p (t n) -> p t n", n=NE)
        choice = {n: x_first[:, k // 3, QT * NE * (k % 3):QT * NE * (k % 3 + 1)].rearrange("p (t n) -> p t n", n=NE)
                  for k, n in enumerate(("lg", "eq", "s1", "lg2", "s2", "ex"))}
        choice.update({n: x_first[:, 2, QT * k:QT * (k + 1)] for k, n in enumerate(("ss", "norm", "m1", "m2", "pos", "den", "scratch"))})
        choice["rank"] = rank
        square = [w[:, t:t + HT, :].rearrange("p t n -> p (t n)").rearrange("p (c n) -> p c n", c=KC)
                  for w, t in ((x_first, HT), (xn_first, 0))]

        s_tiles = [pb(f"s_tile{i}", [P, SEQ]) for i in range(2)]
        t_bank = [pb(f"t_bank{i}", [P, HALF]) for i in range(2)]
        p_bank = [pb(f"p_bank{i}", [P, HALF]) for i in range(2)]

        prepare(nc, sb, sem, locals())
        attend(nc, sb, sem, locals())
        experts(nc, sb, sem, locals())


def rsqrt_newton(dve, link, y, v, t):
    link(dve.tensor_tensor(t, y, y, ALU.mult))
    link(dve.tensor_tensor(t, t, v, ALU.mult))
    link(dve.tensor_scalar(t, t, -0.5, 1.5, ALU.mult, ALU.add))
    link(dve.tensor_tensor(y, y, t, ALU.mult))


def router(nc, bank, full, square, raw_r, ones, tiles=range(CT)):
    for t in tiles:
        cols = slice(t * P, (t + 1) * P)
        for c in range(KC):
            nc.tensor.matmul(bank[:, t, 0:NE], full[:, c, cols], raw_r[:, c, :], start=(c == 0), stop=(c == KC - 1))
        for c in range(KC):
            last = nc.tensor.matmul(bank[:, t, NE:NE + 1], square[:, c, cols], ones, start=(c == 0), stop=(c == KC - 1))
    return last


def logits_in(bank):
    return bank[:, 0:CT * LC].rearrange("p (t n) -> p t n", n=LC)


def take_logits(v, x, bank, t):
    v.tensor_copy(x["lg2"][:, t, :], bank[:, :, 0:NE])
    return v.tensor_scalar_max(x["ss"][:, t], bank[:, :, NE], 1e-24)


def choose_first(v, link, x):
    wide = [P, QT, NE]
    rsqrt_newton(v, link, x["norm"], x["ss"], x["scratch"])
    link(v.tensor_tensor(x["lg"], x["lg2"], x["norm"].unsqueeze(2).broadcast_to(wide), ALU.mult))
    link(v.tensor_reduce(out=x["m1"], in_=x["lg"], axis=AX.X, op=ALU.max))
    return v.tensor_tensor(x["ex"], x["lg"], x["m1"].unsqueeze(2).broadcast_to(wide), ALU.subtract)


def pick(v, link, x, src, best, sel):
    wide = [P, QT, NE]
    link(v.tensor_tensor(x["eq"], x[src], x[best].unsqueeze(2).broadcast_to(wide), ALU.is_equal))
    link(v.tensor_tensor(x["eq"], x["eq"], x["rank"], ALU.mult))
    link(v.tensor_reduce(out=x["pos"], in_=x["eq"], axis=AX.X, op=ALU.max))
    link(v.tensor_tensor(x[sel], x["eq"], x["pos"].unsqueeze(2).broadcast_to(wide), ALU.is_equal))


def choose_second(v, link, x):
    pick(v, link, x, "lg", "m1", "s1")
    link(v.scalar_tensor_tensor(out=x["lg2"], in0=x["s1"], scalar=MASKED, in1=x["lg"], op0=ALU.mult, op1=ALU.add))
    link(v.tensor_reduce(out=x["m2"], in_=x["lg2"], axis=AX.X, op=ALU.max))


def mark_both(v, link, x):
    pick(v, link, x, "lg2", "m2", "s2")
    link(v.tensor_tensor(x["s1"], x["s1"], x["s2"], ALU.add))


def share_out(v, link, x, comb):
    link(v.tensor_tensor(x["s2"], x["s1"], x["ex"], ALU.mult))
    link(v.tensor_reduce(out=x["den"], in_=x["s2"], axis=AX.X, op=ALU.add))
    link(v.reciprocal(x["den"], x["den"]))
    return v.tensor_tensor(comb, x["s2"], x["den"].unsqueeze(2).broadcast_to([P, QT, NE]), ALU.mult)


def prepare(nc, sb, sem, g):
    ident, mod, gates, biases, h_hi, h_lo, acc, raw, w_qkv = (
        g[n] for n in ("ident", "mod", "gates", "biases", "h_hi", "h_lo", "acc", "raw", "w_qkv"))
    banks = [g["s_tiles"][i][:, HALF * k:HALF * (k + 1)] for i in range(2) for k in range(2)]
    mod_bank, gate_banks = g["p_bank"][0], g["t_bank"]
    with ExitStack() as scope:
        condT = sb("condT", [P, KC, BATCH], scope=scope)
        cexp = sb("cexp", [P, KC, BATCH], scope=scope)
        csilu = sb("csilu", [P, KC, BATCH], scope=scope)
        cwide = sb("cwide", [P, KC, BATCH, P], scope=scope)
        wm = sb("wm", [P, KC, 6 * DM], scope=scope)
        stats = sb("stats", [P, QT, 6], scope=scope)
        mv = sb("mv", [P, QT, 2], scope=scope)
        var = sb("var", [P, QT], scope=scope)
        rstd = sb("rstd", [P, QT], scope=scope)
        scratch = sb("scratch", [P, QT], scope=scope)
        full = g["full1"]
        xn = g["over_v"][:, 1, :, :]
        power = g["power2"]
        cond_in, wm_in, bias_in, wm2_in = (sem(n) for n in ("cond_in", "wm_in", "bias_in", "wm2_in"))
        x_in, x_rest_in = [sem(f"x_in{half}") for half in range(2)], sem("x_rest_in")
        w_in = [sem(f"w_in{kind}") for kind in range(3)]
        id_zero, id_ready, pow_ready = sem("id_zero"), sem("id_ready"), sem("pow_ready")
        c_exp, mod_psum, mod_ready, gates_psum = sem("c_exp"), sem("mod_psum"), sem("mod_ready"), sem("gates_psum")
        var_ready, guess_ready, xn_ready = sem("var_ready"), sem("guess_ready"), sem("xn_ready")
        xT_ready, full_ready, whi_ready = (sem(n) for n in ("xT_ready", "full_ready", "whi_ready"))
        chain = sem("prep_chain")
        SA, CA, GA, SB, CB, GB = range(6)
        def part(kind):
            return slice(kind * KC * 2 * DH, (kind + 1) * KC * 2 * DH)

        with nc.Block() as block:
            @block.sync
            def _(sp):
                xv = g["x"].rearrange("b (t p) d -> p (b t) d", p=P)
                mv_ = g["wmod"].rearrange("(c p) n -> p c n", p=P)
                sp.dma_start(condT[:, :, :], g["cond"]).then_inc(cond_in, 16)
                sp.dma_start(acc[:, 0:HT, :], xv[:, 0:HT, :]).then_inc(x_in[0], 16)
                sp.dma_start(wm[:, :, 0:2 * DM], mv_[:, :, 0:2 * DM]).then_inc(wm_in, 16)
                sp.dma_start(acc[:, HT:QT, :], xv[:, HT:QT, :]).then_inc(x_in[1], 16)
                for kind in range(3):
                    sp.dma_start(raw[:, part(kind)], g["wqkv"][0, :, part(kind)]).then_inc(w_in[kind], 16)
                sp.dma_start(wm[:, :, 2 * DM:], mv_[:, :, 2 * DM:]).then_inc(wm2_in, 16)
                sp.dma_start(acc[:, QT:, :], xv[:, QT:, :]).then_inc(x_rest_in, 16)
                sp.dma_start(biases[:, :, :], g["bias"]).then_inc(bias_in, 16)
                sp.wait_ge(bias_in, 16)

            @block.gpsimd
            def _(pool):
                pool.memset(power[:, :], -0.5).then_inc(pow_ready, 1)
                pool.memset(ident[:, :], 0.0).then_inc(id_zero, 1)
                pool.wait_ge(id_zero, 1)
                pool.affine_select(out=ident[:, :], in_=ident[:, :], compare_op=ALU.not_equal, fill=1.0,
                                   base=0, pattern=[[-1, P]], channel_multiplier=1).then_inc(id_ready, 1)
                pool.wait_ge(pow_ready, 1)
                for half in range(2):
                    t = slice(HT * half, HT * (half + 1))
                    pool.wait_ge(var_ready, half + 1)
                    pool.tensor_tensor(rstd[:, t], var[:, t], power[:, t], ALU.pow).then_inc(guess_ready, 1)
                for kind in range(3):
                    hi, lo = (w[:, kind, :, :].rearrange("p c n -> p (c n)") for w in w_qkv)
                    pool.wait_ge(whi_ready, kind + 1)
                    pool.tensor_tensor(lo, raw[:, part(kind)], hi.bitcast(F32), ALU.subtract)

            @block.scalar
            def _(act):
                act.wait_ge(cond_in, 16)
                nc.scalar.activation(cexp[:, :, :], condT[:, :, :], ACT.Exp, scale=-1.0).then_inc(c_exp, 1)
                for kind in range(3):
                    act.wait_ge(w_in[kind], 16)
                    nc.scalar.activation(w_qkv[0][:, kind, :, :].rearrange("p c n -> p (c n)"), raw[:, part(kind)],
                                         ACT.Copy).then_inc(whi_ready, 1)
                act.wait_ge(mod_ready, 1)
                for n in range(EARLY):
                    b, _, c, cols = norm1_bank(n)
                    act.wait_ge(xT_ready, n + 1)
                    nc.scalar.activation(h_hi[:, c, cols], banks[n], ACT.Identity, scale=mod[:, 0, c, b:b + 1],
                                         bias=mod[:, 1, c, b:b + 1])
                    nc.scalar.activation(full[n], banks[n], ACT.Identity, scale=mod[:, 0, c, b:b + 1],
                                         bias=mod[:, 1, c, b:b + 1]).then_inc(full_ready, 1)
                for k in range(2):
                    act.wait_ge(gates_psum, k + 1)
                    nc.scalar.activation(gates[:, k, :, :].rearrange("p b n -> p (b n)"), gate_banks[k][:, :], ACT.Copy)

            @block.tensor
            def _(pe):
                def mod_columns(kinds, at):
                    for k, kind in enumerate(kinds):
                        for m in range(KC):
                            for c in range(KC):
                                col = kind * DM + m * P
                                last = nc.tensor.matmul(mod_bank[:, (at + k * KC + m) * BATCH:(at + k * KC + m + 1) * BATCH],
                                                        wm[:, c, col:col + P], csilu[:, c, :], start=(c == 0), stop=(c == KC - 1))
                    last.then_inc(mod_psum, 1)

                pe.wait_ge(chain, 3)
                pe.wait_ge(wm_in, 16)
                mod_columns((CA, SA), 0)
                pe.wait_ge(id_ready, 1)
                pe.wait_ge(xn_ready, 1)
                for n in range(EARLY):
                    _, _, c, _ = norm1_bank(n)
                    for t in range(HT):
                        last = nc.tensor.transpose(banks[n][:, t * P:(t + 1) * P], xn[:, t, c * P:(c + 1) * P], ident[:, :])
                    last.then_inc(xT_ready, 1)
                pe.wait_ge(wm2_in, 16)
                pe.wait_ge(mod_ready, 1)
                mod_columns((CB, SB), 2 * KC)
                pe.wait_ge(chain, 4)
                for k, kind in enumerate((GA, GB)):
                    for bb in range(BATCH):
                        for c in range(KC):
                            last = nc.tensor.matmul(gate_banks[k][:, bb * DM:(bb + 1) * DM], cwide[:, c, bb, :],
                                                    wm[:, c, kind * DM:(kind + 1) * DM], start=(c == 0), stop=(c == KC - 1))
                    last.then_inc(gates_psum, 1)

            @block.vector
            def _(dve):
                count = [0]

                def link(ins):
                    count[0] += 1
                    ins.then_inc(chain, 1)
                    dve.wait_ge(chain, count[0])

                def mod_part(half):
                    mp = mod_bank[:, 0:4 * KC * BATCH].rearrange("p (k c b) -> p k c b", k=4, c=KC)
                    dve.wait_ge(mod_psum, half + 1)
                    v.tensor_scalar_add(mod[:, 2 * half, :, :], mp[:, 2 * half, :, :], 1.0)
                    v.tensor_copy(mod[:, 2 * half + 1, :, :], mp[:, 2 * half + 1, :, :]).then_inc(mod_ready, 1)

                v = nc.vector
                wide = [P, KC, BATCH, P]
                dve.wait_ge(c_exp, 1)
                link(v.tensor_scalar_add(cexp[:, :, :], cexp[:, :, :], 1.0))
                link(v.reciprocal(cexp[:, :, :], cexp[:, :, :]))
                link(v.tensor_tensor(csilu[:, :, :], condT[:, :, :], cexp[:, :, :], ALU.mult))
                link(v.tensor_copy(cwide[:, :, :, :], csilu[:, :, :].unsqueeze(3).broadcast_to(wide)))

                def statistics(t0, tiles, stats, mv, var):
                    for t in tiles:
                        last = v.bn_stats(stats[:, t, :], acc[:, t0 + t, :])
                    link(last)
                    for t in tiles:
                        last = v.bn_aggr(mv[:, t, :], stats[:, t, :])
                    link(last)
                    ts = slice(tiles.start, tiles.stop)
                    return v.tensor_scalar_add(var[:, ts], mv[:, ts, 1], EPS)

                def center(half):
                    ts = slice(HT * half, HT * (half + 1))
                    dve.wait_ge(guess_ready, half + 1)
                    rsqrt_newton(v, link, rstd[:, ts], var[:, ts], scratch[:, ts])
                    for t in range(HT * half, HT * (half + 1)):
                        last = v.tensor_scalar(xn[:, t, :], acc[:, t, :], mv[:, t, 0:1], rstd[:, t:t + 1],
                                               ALU.subtract, ALU.mult)
                    last.then_inc(xn_ready, 1)

                dve.wait_ge(x_in[0], 16)
                statistics(0, range(HT), stats, mv, var).then_inc(var_ready, 1)
                center(0)
                mod_part(0)
                dve.wait_ge(x_in[1], 16)
                statistics(0, range(HT, QT), stats, mv, var).then_inc(var_ready, 1)
                center(1)
                for n in range(EARLY):
                    _, _, c, cols = norm1_bank(n)
                    dve.wait_ge(full_ready, n + 1)
                    v.tensor_tensor(h_lo[:, c, cols], full[n], h_hi[:, c, cols].bitcast(F32), ALU.subtract)
                dve.wait_ge(x_rest_in, 16)
                statistics(QT, range(QT), g["stats1"], g["mv1"], g["var1"])
                mod_part(1)


def attend(nc, sb, sem, g):
    ident, biases, h_hi, h_lo, acc, raw, w_qkv, w_o = (
        g[n] for n in ("ident", "biases", "h_hi", "h_lo", "acc", "raw", "w_qkv", "w_o"))
    s_tiles, t_bank, p_bank = (g[n] for n in ("s_tiles", "t_bank", "p_bank"))
    mod, gates, square, full, stats2, mv2, var2, rstd2, scratch2, power2, raw_r, ones, rank, choice = (
        g[n] for n in ("mod", "gates", "square", "full", "stats2", "mv2", "var2", "rstd2", "scratch2", "power2",
                       "raw_r", "ones", "rank", "choice"))
    AHEAD, SLOTS = 2, 4
    with ExitStack() as scope:
        def sbl(name, shape, dt=F32):
            return sb(name, shape, dt, scope)

        def split(name, shape):
            return [sbl(f"{name}_hi", shape, F32R), sbl(f"{name}_lo", shape, F32R)]

        raw_qkv = raw[:, 0:RAW_QKV].rearrange("p (k n) -> p k n", k=3)
        raw_o = raw[:, RAW_QKV:RAW]
        q_half = [split(f"q{i}", [P, HALF]) for i in range(2)]
        k_first = [split(f"k0_{i}", [P, HALF]) for i in range(2)]
        k_second = split("k1", [P, HALF])
        vals = [g["values_first"], g["values_second"]]
        xn_of = [g["over_v"][:, 1, :, :], g["xn_second"]]
        full1, mv1, var1, rstd1, scratch1 = (g[n] for n in ("full1", "mv1", "var1", "rstd1", "scratch1"))
        pT = [split("pT0", [P, HT, HALF]), split("pT1", [P, QT, HALF])]
        z = [split(f"z{i}", [P, SEQ]) for i in range(2)]
        probs = [sbl(f"probs{i}", [P, (HT + 1 + i) * P]) for i in range(SLOTS)]
        mask = sbl("mask", [P, P])
        m_diag, m_rest, neg_max, row_sum, inv_sum = (sbl(n, [P, SLOTS]) for n in ("m_diag", "m_rest", "neg_max", "row_sum", "inv_sum"))

        x_first, xn_first = g["x_first"], g["xn_first"]
        size = sbl("size", [P, DM])

        w_a_first = g["w_a_first"]
        names = ("first_up_hi", "first_up_lo", "guess1", "xn1_ready", "h1_T", "h1_full", "h1_lo", "acc_in", "x_first_in",
                 "router_in", "router_ready", "logits_first", "ss_first", "norm_first", "ex_first", "end_chain",
                 "gates_ready", "weighed", "res_ready", "var2_ready", "guess2", "xn2_ready", "h2_T", "h2_full", "h2_lo", "squared",
                 "raw_qkv_in", "raw_o_in", "mask_zero", "mask_ready", "w_hi", "w_split",
                 "scores", "partial_max", "max_ready", "exp_done", "inv_ready", "normed",
                 "transposed", "pT_hi", "pT_lo", "z_psum", "z_hi", "z_lo",
                 "proj_psum", "proj_hi", "proj_lo", "v_psum", "v_hi", "v_lo", "wo_psum", "wo_added")
        S = {n: sem(n) for n in names}

        logit_bank = logits_in(s_tiles[0])

        def tiles_to(i, u, q):
            return UNITS * QT * i + QT * u + q + 1

        def groups_to(i, u, q):
            return UNITS * NG * i + NG * u + FIRST_GROUP[q + 1]

        def z_to(i, u, c):
            return 2 * UNITS * i + 2 * u + c + 1

        def proj_to(i, u, k):
            return 4 * UNITS * i + 4 * u + k + 1

        def v_to(i, b, k):
            return 4 * BATCH * i + 4 * b + k + 1

        def wo_to(i, b, k):
            return 4 * BATCH * i + 4 * b + k + 1

        def wsplit_to(i, k):
            return 4 * i + k + 1

        def after(i, u, q, n):
            t = QT * u + q + n
            return i + t // (UNITS * QT), t // QT % UNITS, t % QT

        def before_unit(i, u):
            return (i, u - 1) if u else (i - 1, UNITS - 1)

        def next_unit(i, u):
            return (i, u + 1) if u + 1 < UNITS else (i + 1, 0)

        def target(i, u, what, k):
            if what == "z":
                return (i, u) if k == 0 else before_unit(i, u)
            if what == "proj":
                return next_unit(i, u)
            if what == "v":
                return (i, 1) if u == 1 else (i + 1, 0)
            if what in ("h1", "h2", "router"):
                return (0, 0)
            return {0: (i - 1, 1), 2: (i, 0), 3: (i, 1)}[u]

        COUNT = {"z": z_to, "proj": proj_to, "v": v_to, "wo": wo_to, "h2": lambda i, b, k: k + 1,
                 "h1": lambda i, b, n: n - EARLY + 1, "router": lambda i, b, n: n + 1}
        LEFT = {"z": S["z_lo"], "proj": S["proj_lo"], "v": S["v_lo"], "wo": S["wo_added"],
                "h2": S["h2_full"], "h1": S["h1_full"], "router": S["ss_first"]}

        def bank_free(eng, i, u, n, first, last):
            def same(pieces):
                return [(what, k) for m, (_, what, k) in pieces if m % 2 == n % 2]

            here = same([(m, x) for m, x in pieces_of(first, last, u) if m < n])
            if here:
                bi, bu, (what, k) = i, u, here[-1]
            elif first and u == 0:
                wait(eng, LEFT["v"], v_to(0, 0, 2 + n % 2))
                return
            else:
                bi, bu = before_unit(i, u)
                what, k = same(pieces_of(first and bu == u - 1, False, bu))[-1]
            wait(eng, LEFT[what], COUNT[what](*target(bi, bu, what, k), k))

        def schedule(first, last):
            for u in range(UNITS):
                for q in range(QT):
                    pieces = [(n, what, k) for n, (at, what, k) in pieces_of(first, last, u) if at == q]
                    left = QT * (UNITS - u) - q - 1 if last else QT
                    yield u, q, pieces, left >= AHEAD, left >= 1

        def bias_of(kind, i, head):
            return biases[:, kind, bass.ds(2 * i + head, 1)]

        def proj_target(u, k):
            return [(0, 0, q_half[0]), (1, 0, k_first[u % 2]), (1, 1, k_second), (0, 1, q_half[1])][k]

        RESIDUAL_AT = [(2, 3), (2, 4), (2, 7), (3, 1)]
        STATS_AT = [(2, 5), (2, 6), (3, 1), (3, 2)]
        GUESS_AT = [(2, 7), (3, 3)]
        CENTER_AT = [(3, 0), (3, 4)]
        SQUARE_AT = [(3, 4), (3, 7)]
        FIRST_UP_AT = (3, 5)
        ROUTER_AT = (3, 4)

        with nc.Block() as block:
            @block.sync
            def _(sp):
                def load(i, what, when):
                    if when is not None:
                        sp.wait_ge(S["w_split"], when)
                    if what == "qkv":
                        sp.dma_start(raw[:, 0:RAW_QKV], g["wqkv"][bass.ds(i, 1), :, :].rearrange("o p n -> p (o n)")).then_inc(S["raw_qkv_in"], 16)
                    else:
                        sp.dma_start(raw_o, g["wo"][bass.ds(i, 1), :, :].rearrange("o p n -> p (o n)")).then_inc(S["raw_o_in"], 16)

                load(0, "o", None)
                load(1, "qkv", None)
                sp.wait_ge(S["xn1_ready"], 2)
                sp.dma_start(acc[:, :, :].rearrange("p t d -> p (t d)").rearrange("p (t d) -> p t d", d=DM),
                             g["b_o"].unsqueeze(1).broadcast_to([P, TILES, DM])).then_inc(S["acc_in"], 16)
                with sp.Fori(1, PAIRS - 1) as i:
                    load(i, "o", wsplit_to(i - 1, 0))
                    load(i + 1, "qkv", wsplit_to(i - 1, 3))
                load(PAIRS - 1, "o", wsplit_to(PAIRS - 2, 0))
                sp.dma_start(raw_r[:, :, :], g["router_w"].rearrange("(c p) n -> p c n", p=P)).then_inc(S["router_in"], 16)
                sp.wait_ge(S["w_split"], wsplit_to(PAIRS - 1, 0))
                sp.dma_start(raw[:, :], g["wa"]).then_inc(g["wa_in"], 16)
                sp.wait_ge(S["z_psum"], z_to(PAIRS - 1, 1, 1))
                sp.dma_start(x_first, g["x"].rearrange("b (t p) d -> p (b t) d", p=P)[:, 0:QT, :]).then_inc(S["x_first_in"], 16)
                sp.wait_ge(S["first_up_lo"], 1)
                sp.dma_start(raw[:, 0:FIRST * DM], g["wb"][:, 0:FIRST * DM]).then_inc(g["wb_first_in"], 16)

            @block.gpsimd
            def _(pool):
                pool_spare = (S["mask_ready"], [pool.alloc_register(f"pool_until_{n}") for n in range(2)])
                def normalise(i, u, q):
                    s = q % SLOTS
                    w = (q + 1) * P
                    wait(pool, S["inv_ready"], tiles_to(i, u, q))
                    pool.tensor_tensor(probs[s][:, 0:w], probs[s][:, 0:w], inv_sum[:, s:s + 1].broadcast_to([P, w]),
                                       ALU.mult).then_inc(S["normed"], 1)

                def split_weights(raw, pair, n):
                    hi, lo = pair
                    pool.tensor_copy(hi, raw).then_inc(S["w_hi"], 1)
                    wait(pool, S["w_hi"], n)
                    pool.tensor_tensor(lo, raw, hi.bitcast(F32), ALU.subtract).then_inc(S["w_split"], 1)

                def w_of(kind):
                    return [w[:, kind, :, :].rearrange("p c n -> p (c n)") for w in w_qkv]

                def w_o_all():
                    return [w[:, :, :].rearrange("p h n -> p (h n)") for w in w_o]

                def pair(i, first, last):
                    for u, q, _, _, more in schedule(first, last):
                        if (u, q) == (1, 0):
                            wait_apart(pool, pool_spare, (S["raw_o_in"], 16 * (i + 1)), (S["wo_psum"], wo_to(i - 1, 1, 3)))
                            split_weights(raw_o, w_o_all(), wsplit_to(i, 0))
                        if (u, q) == (2, 0) and not last:
                            wait_apart(pool, pool_spare, (S["raw_qkv_in"], 16 * (i + 1)), (S["v_psum"], v_to(i, 1, 3)))
                            split_weights(raw_qkv[:, 2, :], w_of(2), wsplit_to(i, 1))
                        if (u, q) == (3, 0) and not last:
                            for kind in range(2):
                                wait_apart(pool, pool_spare, (S["proj_psum"], proj_to(i, 3, 3)))
                                split_weights(raw_qkv[:, kind, :], w_of(kind), wsplit_to(i, 2 + kind))
                        if more:
                            normalise(*after(i, u, q, 1))
                        if last:
                            towards_experts(u, q)

                def router_constants():
                    pool.wait_ge(S["res_ready"], 4)
                    pool.memset(ones, 1.0)
                    for e in range(NE):
                        last = pool.memset(rank[:, :, e:e + 1], float(NE - e))
                    last.then_inc(S["router_ready"], 1)

                def residual(k):
                    t = slice(2 * k, 2 * k + 2)
                    pool.wait_ge(S["gates_ready"], 1)
                    pool.wait_ge(S["wo_added"], wo_to(PAIRS - 1, 0, k))
                    pool.tensor_tensor(acc[:, t, :], acc[:, t, :], gates[:, 0, 0, :].unsqueeze(1).broadcast_to([P, 2, DM]),
                                       ALU.mult).then_inc(S["weighed"], 1)
                    pool.wait_ge(S["weighed"], k + 1)
                    pool.wait_ge(S["x_first_in"], 16)
                    pool.tensor_tensor(acc[:, t, :], acc[:, t, :], x_first[:, t, :], ALU.add).then_inc(S["res_ready"], 1)

                def guess(n):
                    pool.wait_ge(S["var2_ready"], n + 1)
                    pool.tensor_tensor(rstd2[:, n, :], var2[:, n, :], power2[:, 0:CT], ALU.pow).then_inc(S["guess2"], 1)

                def towards_experts(u, q):
                    if (u, q) in GUESS_AT:
                        guess(GUESS_AT.index((u, q)))
                    if (u, q) in RESIDUAL_AT:
                        residual(RESIDUAL_AT.index((u, q)))
                    if (u, q) == ROUTER_AT:
                        router_constants()

                pool.tensor_tensor(rstd1, var1, power2[:, :], ALU.pow).then_inc(S["guess1"], 1)
                pool.memset(mask[:, :], 0.0).then_inc(S["mask_zero"], 1)
                pool.wait_ge(S["mask_zero"], 1)
                pool.affine_select(out=mask[:, :], in_=mask[:, :], compare_op=ALU.is_ge, fill=MASKED,
                                   base=0, pattern=[[-1, P]], channel_multiplier=1).then_inc(S["mask_ready"], 1)
                normalise(0, 0, 0)
                pair(0, True, False)
                with pool.Fori(1, PAIRS - 1) as i:
                    pair(i, False, False)
                pair(PAIRS - 1, False, True)
                pool.wait_ge(S["ss_first"], 2)
                pool.tensor_tensor(choice["norm"], choice["ss"], power2[:, :], ALU.pow).then_inc(S["norm_first"], 1)

            @block.tensor
            def _(pe):
                mm = nc.tensor.matmul

                def product(dst, a, b, start, stop):
                    mm(dst, a[0], b[0], start=start, stop=False)
                    mm(dst, a[0], b[1], start=False, stop=False)
                    return mm(dst, a[1], b[0], start=False, stop=stop)

                def cut(pair, *idx):
                    return [x[idx] for x in pair]

                def score(i, u, q):
                    wait(pe, S["exp_done"], tiles_to(i, u, q) - 2)
                    if q == 0:
                        wait(pe, S["proj_lo"], proj_to(i, u, 1))
                    if q == HT:
                        wait(pe, S["proj_lo"], proj_to(i, u, 3))
                    dst = s_tiles[q % 2]
                    c = slice(q % HT * P, (q % HT + 1) * P)
                    rows = cut(q_half[q // HT], slice(None), c)
                    w = min((q + 1) * P, HALF)
                    last = product(dst[:, 0:w], rows, cut(k_first[u % 2], slice(None), slice(0, w)), True, True)
                    if q >= HT:
                        w = (q + 1 - HT) * P
                        last = product(dst[:, HALF:HALF + w], rows, cut(k_second, slice(None), slice(0, w)), True, True)
                    last.then_inc(S["scores"], 1)

                def project(bank, i, u, k):
                    kind, half, _ = proj_target(u, k)
                    b, head = divmod(u, 2)
                    if (u, k) == (0, 0):
                        wait(pe, S["w_split"], wsplit_to(i - 1, 3))
                    cols = slice(b * SEQ + half * HALF, b * SEQ + (half + 1) * HALF)
                    for c in range(KC):
                        last = product(bank[:, :], cut(w_qkv, slice(None), kind, c, slice(head * DH, (head + 1) * DH)),
                                       [h_hi[:, c, cols], h_lo[:, c, cols]], c == 0, c == KC - 1)
                    last.then_inc(S["proj_psum"], 1)

                def values(bank, i, b, k):
                    if (b, k) == (0, 0):
                        wait(pe, S["w_split"], wsplit_to(i - 1, 1))
                    for n in range(2):
                        t = b * QT + 2 * k + n
                        for c in range(KC):
                            last = product(bank[:, n * DM:(n + 1) * DM],
                                           [h_hi[:, c, t * P:(t + 1) * P], h_lo[:, c, t * P:(t + 1) * P]],
                                           cut(w_qkv, slice(None), 2, c, slice(None)), c == 0, c == KC - 1)
                    last.then_inc(S["v_psum"], 1)

                def out_project(bank, i, b, k):
                    if (b, k) == (0, 0):
                        wait(pe, S["w_split"], wsplit_to(i, 0))
                    if k % 2 == 0:
                        wait(pe, S["z_lo"], z_to(i, 2 * b + 1, k // 2))
                    for n in range(2):
                        t = slice((2 * k + n) * P, (2 * k + n + 1) * P)
                        for h in range(2):
                            last = product(bank[:, n * DM:(n + 1) * DM], cut(z[h], slice(None), t),
                                           cut(w_o, slice(None), h, slice(None)), h == 0, h == 1)
                    last.then_inc(S["wo_psum"], 1)

                def transpose(i, u, q):
                    wait(pe, S["normed"], tiles_to(i, u, q))
                    for n, (k0, count) in enumerate(GROUPS[q]):
                        m = FIRST_GROUP[q] + n
                        bank = t_bank[m % 2]
                        wait(pe, S["pT_lo"], UNITS * NG * i + NG * u + m - 1)
                        for j in range(count):
                            last = nc.tensor.transpose(bank[:, j * P:(j + 1) * P], probs[q % SLOTS][:, (k0 + j) * P:(k0 + j + 1) * P], ident[:, :])
                        last.then_inc(S["transposed"], 1)

                def attend_values(bank, i, u, c):
                    b, head = divmod(u, 2)
                    wait(pe, S["pT_lo"], groups_to(i, u, HT * c + HT - 1))
                    if (head, c) == (0, 0):
                        wait(pe, S["v_lo"], v_to(i, b, 3))
                    blocks = HT * (c + 1)
                    for k in range(blocks):
                        q0 = max(0, k - HT * c) * P
                        last = product(bank[:, q0:HALF], cut(vals[b], slice(None), k, slice(head * DH, (head + 1) * DH)),
                                       cut(pT[c], slice(None), k, slice(q0, HALF)), k == 0, k == blocks - 1)
                    last.then_inc(S["z_psum"], 1)

                def transpose_h1(bank, i, u, n):
                    b, half, c, _ = norm1_bank(n)
                    if b:
                        pe.wait_ge(S["xn1_ready"], half + 1)
                    for t in range(HT):
                        last = nc.tensor.transpose(bank[:, t * P:(t + 1) * P], xn_of[b][:, HT * half + t, c * P:(c + 1) * P], ident[:, :])
                    last.then_inc(S["h1_T"], 1)

                def transpose_h2(bank, i, b, k):
                    n, c = divmod(k, KC)
                    pe.wait_ge(S["xn2_ready"], n + 1)
                    for t in range(CT):
                        last = nc.tensor.transpose(bank[:, t * P:(t + 1) * P], xn_first[:, CT * n + t, c * P:(c + 1) * P], ident[:, :])
                    last.then_inc(S["h2_T"], 1)

                def route(bank, i, u, n):
                    pe.wait_ge(S["router_in"], 16)
                    pe.wait_ge(S["router_ready"], 1)
                    pe.wait_ge(S["squared"], n + 1)
                    router(nc, logits_in(bank), full[n], square[n], raw_r, ones).then_inc(S["logits_first"], 1)

                MAKE = {"proj": project, "v": values, "wo": out_project, "z": attend_values, "h1": transpose_h1,
                        "h2": transpose_h2, "router": route}

                def pair(i, first, last):
                    for u, q, pieces, ahead, _ in schedule(first, last):
                        if ahead:
                            score(*after(i, u, q, AHEAD))
                        if first and (u, q) == (1, 0):
                            pe.wait_ge(S["h1_lo"], NORM1_BANKS - EARLY)
                        for n, what, k in pieces:
                            bank_free(pe, i, u, n, first, last)
                            MAKE[what](p_bank[n % 2], *target(i, u, what, k), k)
                        if last and (u, q) == (UNITS - 1, QT - 1):
                            pe.wait_ge(S["squared"], 2)
                            pe.wait_ge(S["exp_done"], tiles_to(i, u, q) - 1)
                            router(nc, logit_bank, full[1], square[1], raw_r, ones, range(CT // 2))
                        transpose(i, u, q)
                        if last and (u, q) == (UNITS - 1, QT - 1):
                            router(nc, logit_bank, full[1], square[1], raw_r, ones, range(CT // 2, CT)).then_inc(S["logits_first"], 1)

                def first_projection(k):
                    kind, half, _ = proj_target(0, k)
                    for c in range(KC):
                        cols = slice(half * HALF, (half + 1) * HALF)
                        last = product(p_bank[k % 2][:, :], cut(w_qkv, slice(None), kind, c, slice(0, DH)),
                                       [h_hi[:, c, cols], h_lo[:, c, cols]], c == 0, c == KC - 1)
                    last.then_inc(S["proj_psum"], 1)

                for k in range(2):
                    first_projection(k)
                    transpose_h1(t_bank[k], 0, 0, EARLY + k)
                for k in range(2):
                    pe.wait_ge(S["proj_lo"], k + 1)
                    values(p_bank[k % 2], 0, 0, k)
                for q in range(AHEAD):
                    score(0, 0, q)
                pe.wait_ge(S["h1_lo"], 2 * KC - EARLY)
                for k in range(2, 4):
                    pe.wait_ge(S["v_lo"], k - 1)
                    first_projection(k)
                for k in range(2, 4):
                    pe.wait_ge(S["proj_lo"], k + 1)
                    values(p_bank[k % 2], 0, 0, k)
                pair(0, True, False)
                with pe.Fori(1, PAIRS - 1) as i:
                    pair(i, False, False)
                pair(PAIRS - 1, False, True)
                pe.wait_ge(S["wo_added"], wo_to(PAIRS - 1, 1, 0))
                attend_values(p_bank[0], PAIRS - 1, UNITS - 1, 1)
                pe.wait_ge(S["wo_added"], wo_to(PAIRS - 1, 1, 1))
                for k in range(2, 4):
                    out_project(p_bank[(k + 1) % 2], PAIRS - 1, 1, k)
                pe.wait_ge(S["h2_lo"], 2 * KC)

            @block.scalar
            def _(act):
                act_spare = (S["mask_ready"], [act.alloc_register(f"act_until_{n}") for n in range(2)])
                def exponential(i, u, q):
                    s = q % SLOTS
                    w = (q + 1) * P
                    wait(act, S["max_ready"], tiles_to(i, u, q))
                    bi, bu, bq = after(i, u, q, -SLOTS)
                    wait(act, S["transposed"], groups_to(bi, bu, bq))
                    nc.scalar.activation(probs[s][:, 0:w], s_tiles[q % 2][:, 0:w], ACT.Exp, bias=neg_max[:, s:s + 1],
                                         scale=SCALE, accum_out=row_sum[:, s:s + 1]).then_inc(S["exp_done"], 1)

                def hi_projection(bank, i, u, k):
                    kind, _, dst = proj_target(u, k)
                    wait_apart(act, act_spare, (S["proj_psum"], proj_to(i, u, k)),
                               (S["scores"], [tiles_to(i, u - 1, HT - 1), tiles_to(i, u - 2, QT - 1),
                                              tiles_to(i, u - 1, QT - 1), tiles_to(i, u - 1, QT - 1)][k]))
                    nc.scalar.activation(dst[0][:, :], bank[:, :], ACT.Identity,
                                         bias=bias_of(kind, i, u % 2)).then_inc(S["proj_hi"], 1)

                def hi_values(bank, i, b, k):
                    wait(act, S["v_psum"], v_to(i, b, k))
                    wait(act, S["z_psum"], z_to(i - 1, 2 * b + 1, 1))
                    nc.scalar.activation(vals[b][0][:, 2 * k:2 * k + 2, :].rearrange("p t n -> p (t n)"), bank[:, :],
                                         ACT.Copy).then_inc(S["v_hi"], 1)

                def hi_transposed(i, u, q):
                    c, ql = divmod(q, HT)
                    if ql == 0:
                        bi, bu = (i, u - 1) if u else (i - 1, UNITS - 1)
                        wait(act, S["z_psum"], z_to(bi, bu, c))
                    for n, (k0, count) in enumerate(GROUPS[q]):
                        m = FIRST_GROUP[q] + n
                        wait(act, S["transposed"], UNITS * NG * i + NG * u + m + 1)
                        nc.scalar.activation(pT[c][0][:, k0:k0 + count, ql * P:(ql + 1) * P],
                                             t_bank[m % 2][:, 0:count * P].rearrange("p (k n) -> p k n", n=P), ACT.Copy).then_inc(S["pT_hi"], 1)

                def hi_z(bank, i, u, c):
                    b, head = divmod(u, 2)
                    wait_apart(act, act_spare, (S["z_psum"], z_to(i, u, c)), (S["wo_psum"], wo_to(i, b - 1, 2 * c + 1)))
                    nc.scalar.activation(z[head][0][:, c * HALF:(c + 1) * HALF], bank[:, :], ACT.Identity,
                                         bias=bias_of(2, i, head)).then_inc(S["z_hi"], 1)

                def hi_h1(bank, i, u, n):
                    b, _, c, cols = norm1_bank(n)
                    act.wait_ge(S["h1_T"], n - EARLY + 1)
                    nc.scalar.activation(h_hi[:, c, cols], bank[:, :], ACT.Identity, scale=mod[:, 0, c, b:b + 1], bias=mod[:, 1, c, b:b + 1])
                    if n >= EARLY + 2:
                        act.wait_ge(S["h1_lo"], n - EARLY - 1)
                    nc.scalar.activation(full1[n % 2], bank[:, :], ACT.Identity, scale=mod[:, 0, c, b:b + 1],
                                         bias=mod[:, 1, c, b:b + 1]).then_inc(S["h1_full"], 1)

                def hi_h2(bank, i, b, k):
                    n, c = divmod(k, KC)
                    act.wait_ge(S["h2_T"], k + 1)
                    nc.scalar.activation(h_hi[:, c, CHUNK * n:CHUNK * (n + 1)], bank[:, :], ACT.Identity,
                                         scale=mod[:, 2, c, 0:1], bias=mod[:, 3, c, 0:1])
                    nc.scalar.activation(full[n][:, c, :], bank[:, :], ACT.Identity,
                                         scale=mod[:, 2, c, 0:1], bias=mod[:, 3, c, 0:1]).then_inc(S["h2_full"], 1)

                TAKE = {"proj": hi_projection, "v": hi_values, "z": hi_z, "h1": hi_h1, "h2": hi_h2}

                def pair(i, first, last):
                    for u, q, pieces, _, more in schedule(first, last):
                        if more:
                            exponential(*after(i, u, q, 1))
                        if first and (u, q) == (1, 0):
                            act.wait_ge(S["h1_lo"], NORM1_BANKS - EARLY)
                        if last and (u, q) == FIRST_UP_AT:
                            act.wait_ge(g["wa_in"], 16)
                            nc.scalar.activation(w_a_first[0], raw[:, 0:FIRST * KC * RANK], ACT.Copy).then_inc(S["first_up_hi"], 1)
                        if last and (u, q) in SQUARE_AT:
                            n = SQUARE_AT.index((u, q))
                            act.wait_ge(S["h2_full"], KC * (n + 1))
                            act.wait_ge(S["res_ready"], 4)
                            nc.scalar.activation(square[n], full[n], ACT.Square).then_inc(S["squared"], 1)
                        for n, what, k in pieces:
                            if what in TAKE:
                                TAKE[what](p_bank[n % 2], *target(i, u, what, k), k)
                        hi_transposed(i, u, q)

                for k in range(2):
                    hi_projection(p_bank[k % 2], 0, 0, k)
                    hi_h1(t_bank[k], 0, 0, EARLY + k)
                for k in range(2):
                    hi_values(p_bank[k % 2], 0, 0, k)
                exponential(0, 0, 0)
                for k in range(2, 4):
                    hi_projection(p_bank[k % 2], 0, 0, k)
                for k in range(2, 4):
                    hi_values(p_bank[k % 2], 0, 0, k)
                pair(0, True, False)
                with act.Fori(1, PAIRS - 1) as i:
                    pair(i, False, False)
                pair(PAIRS - 1, False, True)
                act.wait_ge(S["ex_first"], 1)
                nc.scalar.activation(choice["ex"], choice["ex"], ACT.Exp)
                hi_z(p_bank[0], PAIRS - 1, UNITS - 1, 1)

            @block.vector
            def _(dve):
                dve_spare = (S["mask_ready"], [dve.alloc_register(f"dve_until_{n}") for n in range(2)])
                v = nc.vector

                def maximum(i, u, q):
                    s = q % SLOTS
                    t = s_tiles[q % 2]
                    n = tiles_to(i, u, q)
                    wait_apart(dve, dve_spare, (S["scores"], n))
                    diag = t[:, q * P:(q + 1) * P]
                    v.tensor_tensor_reduce(out=diag, in0=diag, in1=mask[:, :], scale=1.0, scalar=-3e38, op0=ALU.add,
                                           op1=ALU.max, accum_out=m_diag[:, s:s + 1]).then_inc(S["partial_max"], 1)
                    if q:
                        v.tensor_reduce(out=m_rest[:, s:s + 1], in_=t[:, 0:q * P], axis=AX.X,
                                        op=ALU.max).then_inc(S["partial_max"], 1)
                    wait(dve, S["partial_max"], (2 * QT - 1) * UNITS * i + (2 * QT - 1) * u + 2 * q + 1)
                    other = m_rest if q else m_diag
                    v.tensor_scalar(neg_max[:, s:s + 1], m_diag[:, s:s + 1], other[:, s:s + 1], -SCALE,
                                    ALU.max, ALU.mult).then_inc(S["max_ready"], 1)

                def invert(i, u, q):
                    s = q % SLOTS
                    wait(dve, S["exp_done"], tiles_to(i, u, q))
                    v.reciprocal(inv_sum[:, s:s + 1], row_sum[:, s:s + 1]).then_inc(S["inv_ready"], 1)

                def lo_projection(bank, i, u, k):
                    kind, _, dst = proj_target(u, k)
                    wait(dve, S["proj_hi"], proj_to(i, u, k))
                    v.scalar_tensor_tensor(out=dst[1][:, :], in0=bank[:, :], scalar=bias_of(kind, i, u % 2),
                                           in1=dst[0][:, :].bitcast(F32), op0=ALU.add, op1=ALU.subtract).then_inc(S["proj_lo"], 1)

                def lo_values(bank, i, b, k):
                    hi, lo = [x[:, 2 * k:2 * k + 2, :].rearrange("p t n -> p (t n)") for x in vals[b]]
                    wait(dve, S["v_hi"], v_to(i, b, k))
                    v.tensor_tensor(lo, bank[:, :], hi.bitcast(F32), ALU.subtract).then_inc(S["v_lo"], 1)

                def add_projected(bank, i, b, k):
                    t = b * QT + 2 * k
                    dst = acc[:, t:t + 2, :].rearrange("p t n -> p (t n)")
                    wait(dve, S["wo_psum"], wo_to(i, b, k))
                    v.tensor_tensor(dst, bank[:, :], dst, ALU.add).then_inc(S["wo_added"], 1)

                def lo_transposed(i, u, q):
                    c, ql = divmod(q, HT)
                    for n, (k0, count) in enumerate(GROUPS[q]):
                        m = FIRST_GROUP[q] + n
                        hi, lo = [x[:, k0:k0 + count, ql * P:(ql + 1) * P] for x in pT[c]]
                        wait(dve, S["pT_hi"], UNITS * NG * i + NG * u + m + 1)
                        v.tensor_tensor(lo, t_bank[m % 2][:, 0:count * P].rearrange("p (k n) -> p k n", n=P), hi.bitcast(F32),
                                        ALU.subtract).then_inc(S["pT_lo"], 1)

                def lo_z(bank, i, u, c):
                    head = u % 2
                    hi, lo = [x[:, c * HALF:(c + 1) * HALF] for x in z[head]]
                    wait(dve, S["z_hi"], z_to(i, u, c))
                    v.scalar_tensor_tensor(out=lo, in0=bank[:, :], scalar=bias_of(2, i, head), in1=hi.bitcast(F32),
                                           op0=ALU.add, op1=ALU.subtract).then_inc(S["z_lo"], 1)

                count = [0]

                def link(ins):
                    count[0] += 1
                    ins.then_inc(S["end_chain"], 1)
                    dve.wait_ge(S["end_chain"], count[0])

                def gate(kind, b):
                    gt = gates[:, kind, b, :]
                    link(v.tensor_scalar(size[:, :], gt, -1.0, None, ALU.mult))
                    link(v.tensor_tensor(size[:, :], size[:, :], gt, ALU.max))
                    link(v.tensor_scalar(size[:, :], size[:, :], 0.25, None, ALU.max))
                    link(v.tensor_scalar(gt, gt, 0.0, 2.0, ALU.is_ge, ALU.mult))
                    v.scalar_tensor_tensor(out=gt, in0=gt, scalar=1.0, in1=size[:, :], op0=ALU.subtract,
                                           op1=ALU.mult).then_inc(S["gates_ready"], 1)
                    dve.wait_ge(S["gates_ready"], 2 * kind + b + 1)

                def stats_of(k):
                    n = k // 2
                    dve.wait_ge(S["res_ready"], k + 1)
                    for j in range(2):
                        t = 2 * k + j
                        last = v.bn_stats(stats2[:, t % CT, :], acc[:, t, :])
                    link(last)
                    for j in range(2):
                        t = 2 * k + j
                        last = v.bn_aggr(mv2[:, n, t % CT, :], stats2[:, t % CT, :])
                    link(last)
                    if k % 2:
                        v.tensor_scalar_add(var2[:, n, :], mv2[:, n, :, 1], EPS).then_inc(S["var2_ready"], 1)

                def center(n):
                    dve.wait_ge(S["guess2"], n + 1)
                    rsqrt_newton(v, link, rstd2[:, n, :], var2[:, n, :], scratch2[:, 0:CT])
                    for j in range(CT):
                        last = v.tensor_scalar(xn_first[:, CT * n + j, :], acc[:, CT * n + j, :], mv2[:, n, j, 0:1],
                                               rstd2[:, n, j:j + 1], ALU.subtract, ALU.mult)
                    last.then_inc(S["xn2_ready"], 1)

                def towards_experts(u, q):
                    if u < 2 and q in (2, 5):
                        gate(u, q // 3)
                    if (u, q) in STATS_AT:
                        stats_of(STATS_AT.index((u, q)))
                    if (u, q) == FIRST_UP_AT:
                        dve.wait_ge(S["first_up_hi"], 1)
                        v.tensor_tensor(w_a_first[1], raw[:, 0:FIRST * KC * RANK], w_a_first[0].bitcast(F32), ALU.subtract).then_inc(S["first_up_lo"], 1)
                    if (u, q) in CENTER_AT:
                        center(CENTER_AT.index((u, q)))

                def lo_h1(bank, i, u, n):
                    _, _, c, cols = norm1_bank(n)
                    dve.wait_ge(S["h1_full"], n - EARLY + 1)
                    v.tensor_tensor(h_lo[:, c, cols], full1[n % 2], h_hi[:, c, cols].bitcast(F32), ALU.subtract).then_inc(S["h1_lo"], 1)

                def center1(half):
                    ts = slice(HT * half, HT * (half + 1))
                    dve.wait_ge(S["guess1"], 1)
                    rsqrt_newton(v, link, rstd1[:, ts], var1[:, ts], scratch1[:, ts])
                    for t in range(HT * half, HT * (half + 1)):
                        last = v.tensor_scalar(xn_of[1][:, t, :], acc[:, QT + t, :], mv1[:, t, 0:1], rstd1[:, t:t + 1],
                                               ALU.subtract, ALU.mult)
                    last.then_inc(S["xn1_ready"], 1)

                def lo_h2(bank, i, b, k):
                    n, c = divmod(k, KC)
                    cols = slice(CHUNK * n, CHUNK * (n + 1))
                    dve.wait_ge(S["h2_full"], k + 1)
                    v.tensor_tensor(h_lo[:, c, cols], full[n][:, c, :], h_hi[:, c, cols].bitcast(F32), ALU.subtract).then_inc(S["h2_lo"], 1)

                def take_routed(bank, n):
                    dve.wait_ge(S["logits_first"], n + 1)
                    take_logits(v, choice, bank, slice(CT * n, CT * (n + 1))).then_inc(S["ss_first"], 1)
                    dve.wait_ge(S["ss_first"], n + 1)

                TAKE = {"router": lambda bank, i, b, n: take_routed(logits_in(bank), n), "proj": lo_projection,
                        "v": lo_values, "wo": add_projected, "z": lo_z, "h1": lo_h1, "h2": lo_h2}

                def pair(i, first, last):
                    for u, q, pieces, ahead, more in schedule(first, last):
                        if ahead:
                            maximum(*after(i, u, q, AHEAD))
                        if more:
                            invert(*after(i, u, q, 1))
                        if first and (u, q) == (1, 0):
                            dve.wait_ge(S["h1_lo"], NORM1_BANKS - EARLY)
                        if first and (u, q) == (2, 0):
                            dve.wait_ge(S["acc_in"], 16)
                        for n, what, k in pieces:
                            TAKE[what](p_bank[n % 2], *target(i, u, what, k), k)
                        lo_transposed(i, u, q)
                        if first and u == 0:
                            if q < 2:
                                center1(q)
                        if last:
                            towards_experts(u, q)

                for k in range(2):
                    lo_projection(p_bank[k % 2], 0, 0, k)
                    lo_h1(None, 0, 0, EARLY + k)
                for k in range(2):
                    lo_values(p_bank[k % 2], 0, 0, k)
                dve.wait_ge(S["mask_ready"], 1)
                for q in range(AHEAD):
                    maximum(0, 0, q)
                invert(0, 0, 0)
                for k in range(2, 4):
                    lo_projection(p_bank[k % 2], 0, 0, k)
                for k in range(2, 4):
                    lo_values(p_bank[k % 2], 0, 0, k)
                pair(0, True, False)
                with dve.Fori(1, PAIRS - 1) as i:
                    pair(i, False, False)
                pair(PAIRS - 1, False, True)
                take_routed(logit_bank, 1)
                dve.wait_ge(S["router_ready"], 1)
                dve.wait_ge(S["norm_first"], 1)
                choose_first(v, link, choice).then_inc(S["ex_first"], 1)
                choose_second(v, link, choice)
                lo_z(p_bank[0], PAIRS - 1, UNITS - 1, 1)
                mark_both(v, link, choice)
                for k in range(2, 4):
                    add_projected(p_bank[(k + 1) % 2], PAIRS - 1, 1, k)


def experts(nc, sb, sem, g):
    ident, acc, h_hi, h_lo, mod, gates, raw = (g[n] for n in ("ident", "acc", "h_hi", "h_lo", "mod", "gates", "raw"))
    s_tiles, t_bank, p_bank, w_a_first = (g[n] for n in ("s_tiles", "t_bank", "p_bank", "w_a_first"))
    square, full, stats, mv, var, rstd, scratch, power, raw_r, ones, choice = (
        g[n] for n in ("square", "full", "stats2", "mv2", "var2", "rstd2", "scratch2", "power2", "raw_r", "ones", "choice"))
    HC = CHUNKS // BATCH
    logit_bank = logits_in(t_bank[1])
    with ExitStack() as scope:
        def sbl(name, shape, dt=F32):
            return sb(name, shape, dt, scope)

        def split(name, shape):
            return [sbl(f"{name}_hi", shape, F32R), sbl(f"{name}_lo", shape, F32R)]

        x_second = sbl("x_second", [P, QT, DM])
        raw_b = sbl("raw_b", [P, NE * DM])
        w_a = split("w_a", [P, (NE - FIRST) * KC * RANK])
        w_b = split("w_b", [P, NE * DM])
        xn = sbl("xn2", [P, 2, CT, DM])
        comb = sbl("comb", [P, TILES, NE])
        upT = [split(f"up{i}", [P, CHUNK]) for i in range(2)]
        res = sbl("res", [P, 2, CT, DM])
        part = sbl("part", [P, 2, DM])

        wb_in = [g["wb_first_in"]] + [sem(f"wb_in{k}") for k in (1, 2)]
        x_second_in = [sem(f"x_second_in{k}") for k in range(HC)]
        names = ("chain2", "a_hi", "b_hi", "a_lo", "b_lo", "a_end", "b_end", "weighed2", "res_ready2", "var3_ready", "guess3",
                 "xn3_ready", "h3_T", "h3_full", "h3_lo", "squared3", "logit_psum", "ss_ready", "norm_guess",
                 "ex_in", "ex_ready", "up_psum", "up_hi", "up_lo", "down_psum", "mixed",
                 "scaled", "out_ready", "out_end", "stored", "weighed_up", "summed", "chosen")
        S = {n: sem(n) for n in names}

        STEPS = {(0, 2): [("stats", 2, 0)], (0, 3): [("stats", 2, 1)], (0, 4): [("center", 2, 0)],
                 (0, 5): [("center", 2, 1), ("stats", 3, 0)], (0, 6): [("h", 2, 0), ("stats", 3, 1)],
                 (0, 7): [("h", 2, 1)], (1, 0): [("logits", 2, 0), ("center", 3, 0)], (1, 1): [("logits", 2, 1), ("center", 3, 1)],
                 (1, 2): [("h", 3, 0)], (1, 3): [("h", 3, 1)], (1, 4): [("logits", 3, 0)], (1, 5): [("logits", 3, 1)],
                 (1, 6): [("choose", 1, 0)], (1, 7): [("choose", 1, 1)]}
        POOL_STEPS = {(0, 2): [("guess", 2, 0), ("residual", 3, 0)], (0, 3): [("residual", 3, 1)],
                      (0, 5): [("lo", 2, 0)], (0, 6): [("guess", 3, 0), ("lo", 2, 1)],
                      (1, 1): [("lo", 3, 0)], (1, 2): [("lo", 3, 1)], (1, 4): [("norm", 1, 0)]}
        OWN = CT - 1
        PARTS = [(0, 2), (2, 4), (4, NE)]

        def part_a(k):
            return [slice((e - first) * KC * RANK, (end - first) * KC * RANK) for first in (0, FIRST) for e, end in (PARTS[k],)]

        def part_b(k):
            return slice(PARTS[k][0] * DM, PARTS[k][1] * DM)

        with nc.Block() as block:
            @block.sync
            def _(sp):
                xv = g["x"].rearrange("b (t p) d -> p (b t) d", p=P)
                ov = g["out"].rearrange("b (t p) d -> p (b t) d", p=P)
                for k in range(len(PARTS)):
                    if k:
                        sp.dma_start(raw_b[:, part_b(k)], g["wb"][:, part_b(k)]).then_inc(wb_in[k], 16)
                    if k < HC:
                        t = slice(HT * k, HT * (k + 1))
                        sp.dma_start(x_second[:, t, :], xv[:, QT + HT * k:QT + HT * (k + 1), :]).then_inc(x_second_in[k], 16)
                with sp.Fori(0, CHUNKS - 1) as n:
                    sp.wait_ge(S["out_ready"], n + 1)
                    sp.dma_start(ov[:, bass.ds(CT * n, CT), :], acc[:, bass.ds(CT * n, CT), :]).then_inc(S["stored"], 16)
                for ready, t in ((S["out_end"], slice(TILES - CT, TILES - 1)), (S["out_ready"], slice(TILES - 1, TILES))):
                    sp.wait_ge(ready, 1 if t.stop < TILES else CHUNKS)
                    sp.dma_start(ov[:, t, :], acc[:, t, :]).then_inc(S["stored"], 16)
                sp.wait_ge(S["stored"], 16 * (CHUNKS + 1))

            @block.gpsimd
            def _(pool):
                def residual(m, k):
                    j = 2 * (m - HC) + k
                    t = slice(QT + 2 * j, QT + 2 * j + 2)
                    pool.tensor_tensor(acc[:, t, :], acc[:, t, :], gates[:, 0, 1, :].unsqueeze(1).broadcast_to([P, 2, DM]),
                                       ALU.mult).then_inc(S["weighed2"], 1)
                    pool.wait_ge(S["weighed2"], j + 1)
                    pool.wait_ge(x_second_in[m - HC], 16)
                    pool.tensor_tensor(acc[:, t, :], acc[:, t, :], x_second[:, 2 * j:2 * j + 2, :], ALU.add).then_inc(S["res_ready2"], 1)

                def guess(m, _):
                    j = m - HC
                    pool.wait_ge(S["var3_ready"], j + 1)
                    pool.tensor_tensor(rstd[:, j, :], var[:, j, :], power[:, 0:CT], ALU.pow).then_inc(S["guess3"], 1)

                def norm_guess(b, _):
                    pool.wait_ge(S["ss_ready"], CHUNKS // BATCH)
                    pool.tensor_tensor(choice["norm"], choice["ss"], power[:, :], ALU.pow).then_inc(S["norm_guess"], 1)

                def lo(m, c):
                    cols = slice(CHUNK * m, CHUNK * (m + 1))
                    pool.wait_ge(S["h3_full"], KC * (m - HC) + c + 1)
                    pool.tensor_tensor(h_lo[:, c, cols], full[m % 2][:, c, :], h_hi[:, c, cols].bitcast(F32), ALU.subtract).then_inc(S["h3_lo"], 1)

                def mix_last(n, e):
                    pool.wait_ge(S["weighed_up"], NE * n + e + 1)
                    wait(pool, S["summed"], (NE - 1) * n + e - 1)
                    pool.tensor_tensor(res[:, n % 2, OWN, :], res[:, n % 2, OWN, :], part[:, e % 2, :], ALU.add).then_inc(S["summed"], 1)

                def finish(n, t0):
                    t = slice(CT * n + t0, CT * (n + 1))
                    total = res[:, n % 2, t0:CT, :]
                    pool.wait_ge(S["summed"], (NE - 1) * (n + 1))
                    if t0 < OWN:
                        pool.wait_ge(S["mixed"], OWN * NE * (n + 1))
                    pool.tensor_tensor(total, total, gates[:, 1, n // HC, :].unsqueeze(1).broadcast_to([P, CT - t0, DM]),
                                       ALU.mult).then_inc(S["scaled"], 1)
                    pool.wait_ge(S["scaled"], n + 1)
                    pool.tensor_tensor(acc[:, t, :], acc[:, t, :], total, ALU.add).then_inc(S["out_ready"], 1)

                def split_last(raw_w, pair, src, dst):
                    hi, lo = (w[:, dst] for w in pair)
                    return pool.tensor_tensor(lo, raw_w[:, src], hi.bitcast(F32), ALU.subtract)

                DO = {"residual": residual, "guess": guess, "lo": lo, "norm": norm_guess}
                residual(2, 0)
                pool.wait_ge(S["a_hi"], 2)
                split_last(raw, w_a, *part_a(2)).then_inc(S["a_end"], 1)
                pool.wait_ge(S["b_hi"], 3)
                split_last(raw_b, w_b, part_b(2), part_b(2)).then_inc(S["b_end"], 1)
                residual(2, 1)
                for n in range(CHUNKS):
                    for e in range(NE):
                        if e:
                            mix_last(n, e)
                        for what, m, k in POOL_STEPS.get((n, e), []):
                            DO[what](m, k)
                        if e == HC and n:
                            finish(n - 1, 0)
                finish(CHUNKS - 1, OWN)

            @block.scalar
            def _(act):
                act_spare = (wb_in[0], [act.alloc_register(f"act_then_{n}") for n in range(2)])

                def norm_out(m, c):
                    j = m - HC
                    cols = slice(CHUNK * m, CHUNK * (m + 1))
                    scale, bias = mod[:, 2, c, 1:2], mod[:, 3, c, 1:2]
                    act.wait_ge(S["h3_T"], KC * j + c + 1)
                    nc.scalar.activation(h_hi[:, c, cols], t_bank[c][:, :], ACT.Identity, scale=scale, bias=bias)
                    nc.scalar.activation(full[j][:, c, :], t_bank[c][:, :], ACT.Identity, scale=scale, bias=bias).then_inc(S["h3_full"], 1)
                    act.wait_ge(S["h3_full"], KC * j + c + 1)
                    nc.scalar.activation(square[j][:, c, :], full[j][:, c, :], ACT.Square).then_inc(S["squared3"], 1)

                def hi_a(k):
                    src, dst = part_a(k)
                    nc.scalar.activation(w_a[0][:, dst], raw[:, src], ACT.Copy).then_inc(S["a_hi"], 1)

                def hi_b(k):
                    act.wait_ge(wb_in[k], 16)
                    nc.scalar.activation(w_b[0][:, part_b(k)], (raw_b if k else raw)[:, part_b(k)], ACT.Copy).then_inc(S["b_hi"], 1)

                def up_hi(n, e):
                    wait_apart(act, act_spare, (S["up_psum"], NE * n + e + 1), (S["down_psum"], 2 * (NE * n + e - 1)))
                    nc.scalar.activation(upT[e % 2][0][:, :], p_bank[e % 2][:, :], ACT.Copy).then_inc(S["up_hi"], 1)

                def weigh(n, e):
                    share = comb[:, bass.ds(CT * n + OWN, 1), e:e + 1].rearrange("p o e -> p (o e)")
                    free = (S["summed"], (NE - 1) * n + max(e - 2, 0)) if e else (S["out_ready"], n - 1)
                    wait_apart(act, act_spare, (S["mixed"], OWN * (NE * n + e + 1)), free)
                    slot = n % 2 if isinstance(n, int) else n - HC
                    dst = part[:, e % 2, :] if e else res[:, bass.ds(slot, 1), OWN, :].rearrange("p o d -> p (o d)")
                    nc.scalar.activation(dst, s_tiles[e % 2][:, OWN * DM:CT * DM], ACT.Copy,
                                         scale=share).then_inc(S["weighed_up"], 1)

                hi_b(0)
                up_hi(0, 0)
                hi_a(1)
                for n in range(HC):
                    if n:
                        up_hi(n, 0)
                    for e in range(NE):
                        if e + 1 < NE:
                            up_hi(n, e + 1)
                        if (n, e) == (0, 0):
                            hi_a(2)
                            hi_b(1)
                            hi_b(2)
                        if e:
                            weigh(n, e - 1)
                        for what, m, k in STEPS.get((n, e), []):
                            if what == "h":
                                norm_out(m, k)
                            elif (what, k) == ("choose", 0):
                                act.wait_ge(S["ex_in"], 1)
                                nc.scalar.activation(choice["ex"], choice["ex"], ACT.Exp).then_inc(S["ex_ready"], 1)
                    weigh(n, NE - 1)
                with act.Fori(HC, CHUNKS) as n:
                    up_hi(n, 0)
                    for e in range(NE):
                        if e + 1 < NE:
                            up_hi(n, e + 1)
                        if e:
                            weigh(n, e - 1)
                    weigh(n, NE - 1)

            @block.tensor
            def _(pe):
                mm = nc.tensor.matmul

                def product(dst, a, b, start, stop):
                    mm(dst, a[0], b[0], start=start, stop=False)
                    mm(dst, a[0], b[1], start=False, stop=False)
                    return mm(dst, a[1], b[0], start=False, stop=stop)

                def transposed(m, c):
                    j = m - HC
                    if c == 0:
                        pe.wait_ge(S["xn3_ready"], j + 1)
                        if j:
                            pe.wait_ge(S["h3_full"], KC)
                    elif j:
                        pe.wait_ge(S["ss_ready"], j)
                    for t in range(CT):
                        last = nc.tensor.transpose(t_bank[c][:, t * P:(t + 1) * P], xn[:, j, t, c * P:(c + 1) * P], ident[:, :])
                    last.then_inc(S["h3_T"], 1)

                def logits(m, k):
                    j = m - HC
                    if k == 0:
                        pe.wait_ge(S["squared3"], KC * (j + 1))
                    last = router(nc, logit_bank, full[j], square[j], raw_r, ones, (2 * k, 2 * k + 1))
                    if k:
                        last.then_inc(S["logit_psum"], 1)

                def up(n, e):
                    cols = bass.ds(CHUNK * n, CHUNK)
                    wait(pe, S["up_lo"], NE * n + e - 1)
                    for c in range(KC):
                        k = (e if e < FIRST else e - FIRST) * KC + c
                        w = [x[:, k * RANK:(k + 1) * RANK] for x in (w_a_first if e < FIRST else w_a)]
                        last = product(p_bank[e % 2][:, :], w, [h_hi[:, c, cols], h_lo[:, c, cols]], c == 0, c == KC - 1)
                    last.then_inc(S["up_psum"], 1)

                def down(n, e):
                    wait(pe, S["mixed"], OWN * (NE * n + e - 1))
                    wait(pe, S["weighed_up"], NE * n + e - 1)
                    wait(pe, S["up_lo"], NE * n + e + 1)
                    for t in range(CT):
                        last = product(s_tiles[e % 2][:, t * DM:(t + 1) * DM], [x[:, t * P:(t + 1) * P] for x in upT[e % 2]],
                                       [x[:, e * DM:(e + 1) * DM] for x in w_b], True, True)
                        if t % 2:
                            last.then_inc(S["down_psum"], 1)

                up(0, 0)
                for n in range(HC):
                    if n:
                        up(n, 0)
                    for e in range(NE):
                        if (n, e + 1) == (0, PARTS[1][0]):
                            pe.wait_ge(S["a_lo"], 1)
                        if (n, e + 1) == (0, PARTS[2][0]):
                            pe.wait_ge(S["a_end"], 1)
                        if e + 1 < NE:
                            up(n, e + 1)
                        if (n, e) in ((0, PARTS[0][0]), (0, PARTS[1][0])):
                            pe.wait_ge(S["b_lo"], 2 if e else 1)
                        if (n, e) == (0, PARTS[2][0]):
                            pe.wait_ge(S["b_end"], 1)
                        down(n, e)
                        for what, m, k in STEPS.get((n, e), []):
                            if what == "h":
                                transposed(m, k)
                            elif what == "logits":
                                logits(m, k)
                pe.wait_ge(S["h3_lo"], KC * HC)
                with pe.Fori(HC, CHUNKS) as n:
                    up(n, 0)
                    for e in range(NE):
                        if e + 1 < NE:
                            up(n, e + 1)
                        down(n, e)

            @block.vector
            def _(dve):
                v = nc.vector
                count = [0]
                wide = [P, QT, NE]

                def link(ins):
                    count[0] += 1
                    ins.then_inc(S["chain2"], 1)
                    dve.wait_ge(S["chain2"], count[0])

                def stats_of(m, k):
                    j = m - HC
                    dve.wait_ge(S["res_ready2"], 2 * j + k + 1)
                    for t in (2 * k, 2 * k + 1):
                        last = v.bn_stats(stats[:, t, :], acc[:, CT * m + t, :])
                    link(last)
                    for t in (2 * k, 2 * k + 1):
                        last = v.bn_aggr(mv[:, j, t, :], stats[:, t, :])
                    link(last)
                    if k:
                        v.tensor_scalar_add(var[:, j, :], mv[:, j, :, 1], EPS).then_inc(S["var3_ready"], 1)

                def center(m, k):
                    j = m - HC
                    if k == 0:
                        dve.wait_ge(S["guess3"], j + 1)
                        rsqrt_newton(v, link, rstd[:, j, :], var[:, j, :], scratch[:, 0:CT])
                    for t in (2 * k, 2 * k + 1):
                        last = v.tensor_scalar(xn[:, j, t, :], acc[:, CT * m + t, :], mv[:, j, t, 0:1], rstd[:, j, t:t + 1],
                                               ALU.subtract, ALU.mult)
                    if k:
                        last.then_inc(S["xn3_ready"], 1)

                def lo_a(k):
                    src, dst = part_a(k)
                    dve.wait_ge(S["a_hi"], k)
                    v.tensor_tensor(w_a[1][:, dst], raw[:, src], w_a[0][:, dst].bitcast(F32), ALU.subtract).then_inc(S["a_lo"], 1)

                def lo_b(k):
                    dve.wait_ge(S["b_hi"], k + 1)
                    v.tensor_tensor(w_b[1][:, part_b(k)], (raw_b if k else raw)[:, part_b(k)], w_b[0][:, part_b(k)].bitcast(F32), ALU.subtract).then_inc(S["b_lo"], 1)

                def shares(b):
                    share_out(v, link, choice, comb[:, b * QT:(b + 1) * QT, :]).then_inc(S["chosen"], 1)
                    dve.wait_ge(S["chosen"], b + 1)

                def choose(k):
                    if k == 0:
                        dve.wait_ge(S["norm_guess"], 1)
                        choose_first(v, link, choice).then_inc(S["ex_in"], 1)
                    elif k == 1:
                        choose_second(v, link, choice)
                    elif k == 2:
                        mark_both(v, link, choice)
                    else:
                        dve.wait_ge(S["ex_ready"], 1)
                        shares(1)

                def up_lo(n, e):
                    hi, lo = upT[e % 2]
                    dve.wait_ge(S["up_hi"], NE * n + e + 1)
                    v.tensor_tensor(lo[:, :], p_bank[e % 2][:, :], hi[:, :].bitcast(F32), ALU.subtract).then_inc(S["up_lo"], 1)

                def mix(n, e):
                    if e == 0 and n >= 2:
                        dve.wait_ge(S["out_ready"], n - 1)
                    for t in range(OWN):
                        k = OWN * (NE * n + e) + t
                        if t % 2 == 0:
                            dve.wait_ge(S["down_psum"], CT // 2 * (NE * n + e) + t // 2 + 1)
                        y = s_tiles[e % 2][:, t * DM:(t + 1) * DM]
                        share = comb[:, CT * n + t, e:e + 1]
                        if e == 0:
                            v.tensor_scalar(res[:, n % 2, t, :], y, share, None, ALU.mult).then_inc(S["mixed"], 1)
                        else:
                            dve.wait_ge(S["mixed"], k + 1 - OWN)
                            v.scalar_tensor_tensor(out=res[:, n % 2, t, :], in0=y, scalar=share, in1=res[:, n % 2, t, :],
                                                   op0=ALU.mult, op1=ALU.add).then_inc(S["mixed"], 1)

                shares(0)
                lo_b(0)
                up_lo(0, 0)
                lo_a(1)
                for n in range(CHUNKS):
                    if n:
                        up_lo(n, 0)
                    for e in range(NE):
                        if e + 1 < NE:
                            up_lo(n, e + 1)
                        if (n, e) == (HC, 0):
                            choose(2)
                            choose(3)
                        mix(n, e)
                        if (n, e) == (0, 0):
                            lo_b(1)
                        for what, m, k in STEPS.get((n, e), []):
                            if what == "stats":
                                stats_of(m, k)
                            elif what == "center":
                                center(m, k)
                            elif (what, k) == ("logits", 1):
                                j = m - HC
                                dve.wait_ge(S["logit_psum"], j + 1)
                                take_logits(v, choice, logit_bank, slice(CT * j, CT * (j + 1))).then_inc(S["ss_ready"], 1)
                                dve.wait_ge(S["ss_ready"], j + 1)
                            elif what == "choose":
                                choose(k)
                n = CHUNKS - 1
                total = res[:, n % 2, 0:OWN, :]
                t = slice(CT * n, CT * n + OWN)
                dve.wait_ge(S["mixed"], OWN * NE * CHUNKS)
                link(v.tensor_tensor(total, total, gates[:, 1, 1, :].unsqueeze(1).broadcast_to([P, OWN, DM]), ALU.mult))
                v.tensor_tensor(acc[:, t, :], acc[:, t, :], total, ALU.add).then_inc(S["out_end"], 1)


_OUT = ((BATCH, SEQ, DM), "float32")


def kernel(**inputs):
    import numpy as _np
    import concourse.bacc as _bacc
    from concourse import mybir as _mybir
    from concourse.bass_utils import run_bass_kernel_spmd as _run

    a = {k.replace("L0_", "").replace("attn_", "").replace("ffn_", ""): _np.asarray(v) for k, v in inputs.items()}

    def by_pair(w):
        w = w.reshape(PAIRS, 2, KC, P, DH).transpose(0, 3, 2, 1, 4)
        return w.reshape(PAIRS, P, KC * 2 * DH)

    arrays = {
        "x": a["x"],
        "wqkv": _np.concatenate([by_pair(a["W_Q"]), by_pair(a["W_K"]), by_pair(a["W_V"])], axis=2),
        "wo": a["W_O"].reshape(PAIRS, 2, DH, DM).transpose(0, 2, 1, 3).reshape(PAIRS, DH, 2 * DM),
        "bias": _np.stack([a["b_Q"].T, a["b_K"].T, a["b_V"].T], axis=1),
        "b_o": a["b_O"].reshape(1, DM),
        "router_w": a["router_w"],
        "wa": a["Wa"].reshape(NE, KC, P, RANK).transpose(2, 0, 1, 3).reshape(P, KC * NE * RANK),
        "wb": a["Wb"].transpose(1, 0, 2).reshape(RANK, NE * DM),
        "cond": a["c"].reshape(BATCH, KC, P).transpose(2, 1, 0),
        "wmod": a["wmod"],
    }
    nc = _bacc.Bacc("TRN2", target_bir_lowering=False, num_devices=1)
    maps, args = {}, []
    for name, v in arrays.items():
        v = _np.ascontiguousarray(v)
        maps[f"in_{name}"] = v
        args.append(nc.dram_tensor(f"in_{name}", v.shape, _mybir.dt.from_np(v.dtype), kind="ExternalInput").ap())
    shape, dtype = _OUT
    args.append(nc.dram_tensor("out_0", shape, _mybir.dt.from_np(_np.dtype(dtype)), kind="ExternalOutput").ap())
    adaln_block(nc, *args)
    r = _run(nc, [maps], core_ids=[0])
    return r.results[0]["out_0"]
```
